# Optimizing a Trainium2 kernel written in Bass

```python
import numpy as np
import jax
import jax.numpy as jnp

def _softmax(x, axis=-1):
    return jax.nn.softmax(x, axis=axis)

def _gelu(x):
    return jax.nn.gelu(x, approximate=True)

def _silu(x):
    return jax.nn.silu(x)

def _sigmoid(x):
    return jax.nn.sigmoid(x)

def _layernorm(x, axis=-1, eps=1e-05):
    m = jnp.mean(x, axis=axis, keepdims=True)
    v = jnp.var(x, axis=axis, keepdims=True)
    return (x - m) / jnp.sqrt(v + eps)

def _scatter_add(tgt, idx, src, axis=0):
    return tgt.at[idx].add(src)

def _segment_sum(src, seg, n):
    return jax.ops.segment_sum(src, seg, n)
kernel_name = 'mk_gps_d1_gnn_r32_d725ef'

def setup_inputs(seed: int=0):
    np.random.seed(seed)
    _w = jnp.asarray

    def _rec_inputs():
        import jax
        import jax.numpy as jnp
        _gk = jax.random.key(seed)
        x = 0.0001755 + 0.9998 * jax.random.normal(jax.random.fold_in(_gk, 1), (3125, 256), jnp.float32)
        src = jax.random.randint(jax.random.fold_in(_gk, 2), (50000,), 0, 3125, jnp.int32)
        dst = jnp.minimum((3125 * jax.random.uniform(jax.random.fold_in(_gk, 3), (50000,)) ** 2.0).astype(jnp.int32), 99999)
        _o = jnp.argsort(dst, stable=True)
        src = src[_o]
        dst = dst[_o]
        edge_attr_64 = jax.random.uniform(jax.random.fold_in(_gk, 11), (50000, 64), jnp.float32, 0.0, 1)
        return (x, src, dst, edge_attr_64)
    x, src, dst, edge_attr_64 = _rec_inputs()

    def _L0_gnn_setup():
        import jax, jax.numpy as jnp
        import numpy as np
        N, E, HID, NRBF = (10000, 10000, 256, 64)
        key = jax.random.key(seed)
        ks = jax.random.split(key, 12)

        def lin(k, fin, fout):
            bound = 1.0 / np.sqrt(fin)
            kw, kb = jax.random.split(k)
            W = jax.random.uniform(kw, (fin, fout), jnp.float32, -bound, bound)
            b = jax.random.uniform(kb, (fout,), jnp.float32, -bound, bound)
            return (W, b)
        W1, b1 = lin(ks[0], NRBF, HID)
        W2, b2 = lin(ks[1], HID, HID)
        U1, c1 = lin(ks[2], 2 * HID, HID)
        U2, c2 = lin(ks[3], HID, HID)
        h = jax.random.normal(ks[4], (N, HID), jnp.float32)
        edge_index = jax.random.randint(ks[5], (2, E), 0, N, jnp.int64)
        rbf = jax.random.uniform(ks[6], (E, NRBF), jnp.float32)
        return {'h': h, 'edge_index': edge_index, 'rbf': rbf, 'W1': W1, 'b1': b1, 'W2': W2, 'b2': b2, 'U1': U1, 'c1': c1, 'U2': U2, 'c2': c2}
    _L0_gnn_all = _L0_gnn_setup()
    _L0_gnn_in = {k: v for k, v in _L0_gnn_all.items() if k in ('W1', 'b1', 'W2', 'b2', 'U1', 'c1', 'U2', 'c2')}
    del _L0_gnn_all

    def _L0_mix_setup():
        import jax, jax.numpy as jnp
        import numpy as np
        import math
        EMBED = 256
        HEADS = 4
        HEAD_DIM = EMBED // HEADS
        OUT_DIM = 256
        LN_EPS = 1e-05

        def _qkv_init(key):
            spread = math.sqrt(3.0 / EMBED)
            gain, delta = (0.01, 0.01)
            w = jax.random.uniform(key, (EMBED, EMBED), minval=-spread, maxval=spread) * gain
            return w + delta * jnp.eye(EMBED, dtype=w.dtype)

        def _layer_norm(x, g, b):
            mu = jnp.mean(x, axis=-1, keepdims=True)
            var = jnp.mean(jnp.square(x - mu), axis=-1, keepdims=True)
            return (x - mu) * jax.lax.rsqrt(var + LN_EPS) * g + b

        def _split_heads(x, B, S):
            return x.reshape(B, S, HEADS, HEAD_DIM).transpose(0, 2, 1, 3)
        key = jax.random.key(seed)
        ks = jax.random.split(key, 6)
        seq = jax.random.normal(ks[0], (4, 256, EMBED), dtype=jnp.float32)
        wq = _qkv_init(ks[1])
        wk = _qkv_init(ks[2])
        wv = _qkv_init(ks[3])
        bound = 1.0 / math.sqrt(EMBED)
        wo = jax.random.uniform(ks[4], (OUT_DIM, EMBED), minval=-bound, maxval=bound)
        bo = jax.random.uniform(ks[5], (OUT_DIM,), minval=-bound, maxval=bound)
        ln_k_g = jnp.ones((HEAD_DIM,), jnp.float32)
        ln_k_b = jnp.zeros((HEAD_DIM,), jnp.float32)
        ln_v_g = jnp.ones((HEAD_DIM,), jnp.float32)
        ln_v_b = jnp.zeros((HEAD_DIM,), jnp.float32)
        return {'seq': seq, 'wq': wq, 'wk': wk, 'wv': wv, 'wo': wo, 'bo': bo, 'ln_k_g': ln_k_g, 'ln_k_b': ln_k_b, 'ln_v_g': ln_v_g, 'ln_v_b': ln_v_b}
    _L0_mix_all = _L0_mix_setup()
    _L0_mix_in = {k: v for k, v in _L0_mix_all.items() if k in ('wq', 'wk', 'wv', 'wo', 'bo', 'ln_k_g', 'ln_k_b', 'ln_v_g', 'ln_v_b')}
    del _L0_mix_all

    def _L0_ffn_setup():
        import jax, jax.numpy as jnp
        import numpy as np
        D_MODEL = 256
        N_EXPERTS = 16
        HIDDEN = 512
        SCALE = 0.02
        key = jax.random.key(seed)
        ks = jax.random.split(key, 5)
        x = jax.random.normal(ks[0], (4, 256, D_MODEL), dtype=jnp.float32)
        gate_w = jax.random.normal(ks[1], (D_MODEL, N_EXPERTS), dtype=jnp.float32) * SCALE
        gate_b = jnp.zeros((N_EXPERTS,), dtype=jnp.float32)
        w1 = jax.random.normal(ks[2], (N_EXPERTS, D_MODEL, HIDDEN), dtype=jnp.float32) * SCALE
        w2 = jax.random.normal(ks[3], (N_EXPERTS, D_MODEL, HIDDEN), dtype=jnp.float32) * SCALE
        w3 = jax.random.normal(ks[4], (N_EXPERTS, HIDDEN, D_MODEL), dtype=jnp.float32) * SCALE
        return {'x': x, 'gate_w': gate_w, 'gate_b': gate_b, 'w1': w1, 'w2': w2, 'w3': w3}
    _L0_ffn_all = _L0_ffn_setup()
    _L0_ffn_in = {k: v for k, v in _L0_ffn_all.items() if k in ('gate_w', 'gate_b', 'w1', 'w2', 'w3')}
    del _L0_ffn_all
    return {'x': x, 'src': src, 'dst': dst, 'edge_attr_64': edge_attr_64, 'L0_gnn_W1': _L0_gnn_in['W1'], 'L0_gnn_b1': _L0_gnn_in['b1'], 'L0_gnn_W2': _L0_gnn_in['W2'], 'L0_gnn_b2': _L0_gnn_in['b2'], 'L0_gnn_U1': _L0_gnn_in['U1'], 'L0_gnn_c1': _L0_gnn_in['c1'], 'L0_gnn_U2': _L0_gnn_in['U2'], 'L0_gnn_c2': _L0_gnn_in['c2'], 'L0_mix_wq': _L0_mix_in['wq'], 'L0_mix_wk': _L0_mix_in['wk'], 'L0_mix_wv': _L0_mix_in['wv'], 'L0_mix_wo': _L0_mix_in['wo'], 'L0_mix_bo': _L0_mix_in['bo'], 'L0_mix_ln_k_g': _L0_mix_in['ln_k_g'], 'L0_mix_ln_k_b': _L0_mix_in['ln_k_b'], 'L0_mix_ln_v_g': _L0_mix_in['ln_v_g'], 'L0_mix_ln_v_b': _L0_mix_in['ln_v_b'], 'L0_ffn_gate_w': _L0_ffn_in['gate_w'], 'L0_ffn_gate_b': _L0_ffn_in['gate_b'], 'L0_ffn_w1': _L0_ffn_in['w1'], 'L0_ffn_w2': _L0_ffn_in['w2'], 'L0_ffn_w3': _L0_ffn_in['w3']}

def reference(x, src, dst, edge_attr_64, L0_gnn_W1, L0_gnn_b1, L0_gnn_W2, L0_gnn_b2, L0_gnn_U1, L0_gnn_c1, L0_gnn_U2, L0_gnn_c2, L0_mix_wq, L0_mix_wk, L0_mix_wv, L0_mix_wo, L0_mix_bo, L0_mix_ln_k_g, L0_mix_ln_k_b, L0_mix_ln_v_g, L0_mix_ln_v_b, L0_ffn_gate_w, L0_ffn_gate_b, L0_ffn_w1, L0_ffn_w2, L0_ffn_w3):
    import jax
    import jax.numpy as jnp

    def _L0_gnn_ref(h, edge_index, rbf, W1, b1, W2, b2, U1, c1, U2, c2):
        import jax, jax.numpy as jnp
        import numpy as np
        N, E, HID, NRBF = (10000, 10000, 256, 64)
        src, dst = (edge_index[0], edge_index[1])
        gate = jax.nn.sigmoid(jax.nn.silu(rbf @ W1 + b1) @ W2 + b2)
        msg = gate * h[src]
        aggr = jax.ops.segment_sum(msg, dst, num_segments=h.shape[0])
        upd = jax.nn.silu(jnp.concatenate([h, aggr], axis=-1) @ U1 + c1) @ U2 + c2
        return h + upd

    def _L0_mix_ref(seq, wq, wk, wv, wo, bo, ln_k_g, ln_k_b, ln_v_g, ln_v_b):
        import jax, jax.numpy as jnp
        import numpy as np
        import math
        EMBED = 256
        HEADS = 4
        HEAD_DIM = EMBED // HEADS
        OUT_DIM = 256
        LN_EPS = 1e-05

        def _qkv_init(key):
            spread = math.sqrt(3.0 / EMBED)
            gain, delta = (0.01, 0.01)
            w = jax.random.uniform(key, (EMBED, EMBED), minval=-spread, maxval=spread) * gain
            return w + delta * jnp.eye(EMBED, dtype=w.dtype)

        def _layer_norm(x, g, b):
            mu = jnp.mean(x, axis=-1, keepdims=True)
            var = jnp.mean(jnp.square(x - mu), axis=-1, keepdims=True)
            return (x - mu) * jax.lax.rsqrt(var + LN_EPS) * g + b

        def _split_heads(x, B, S):
            return x.reshape(B, S, HEADS, HEAD_DIM).transpose(0, 2, 1, 3)
        B, S, _ = seq.shape
        q = _split_heads(seq @ wq.T, B, S)
        k = _split_heads(seq @ wk.T, B, S)
        v = _split_heads(seq @ wv.T, B, S)
        k = _layer_norm(k, ln_k_g, ln_k_b)
        v = _layer_norm(v, ln_v_g, ln_v_b)
        kv = jnp.einsum('bhsd,bhse->bhde', k, v) / S
        ga = jnp.einsum('bhsd,bhde->bhse', q, kv)
        ga = ga.transpose(0, 2, 1, 3).reshape(B, S, EMBED)
        return ga @ wo.T + bo

    def _L0_ffn_ref(x, gate_w, gate_b, w1, w2, w3):
        import jax, jax.numpy as jnp
        import numpy as np
        D_MODEL = 256
        N_EXPERTS = 16
        HIDDEN = 512
        SCALE = 0.02
        n_experts = w1.shape[0]
        logits = jnp.einsum('bsd,de->bse', x, gate_w) + gate_b
        probs = jax.nn.softmax(logits, axis=-1)
        top_probs, top_idx = jax.lax.top_k(probs, 2)
        top_probs = top_probs / jnp.sum(top_probs, axis=-1, keepdims=True)
        dispatch = jnp.sum(jax.nn.one_hot(top_idx, n_experts, dtype=x.dtype) * top_probs[..., None], axis=-2)
        h1 = jnp.einsum('bsd,edh->bseh', x, w1)
        h2 = jnp.einsum('bsd,edh->bseh', x, w2)
        hidden = jax.nn.silu(h1) * h2
        expert_out = jnp.einsum('bseh,eho->bseo', hidden, w3)
        return jnp.einsum('bseo,bse->bso', expert_out, dispatch)
    edge_index = jnp.stack([src, dst])
    xn = _layernorm(x, axis=-1)
    x = x + _L0_gnn_ref(xn, edge_index, edge_attr_64, L0_gnn_W1, L0_gnn_b1, L0_gnn_W2, L0_gnn_b2, L0_gnn_U1, L0_gnn_c1, L0_gnn_U2, L0_gnn_c2) + _L0_mix_ref(xn[None], L0_mix_wq, L0_mix_wk, L0_mix_wv, L0_mix_wo, L0_mix_bo, L0_mix_ln_k_g, L0_mix_ln_k_b, L0_mix_ln_v_g, L0_mix_ln_v_b)[0]
    x = x + _L0_ffn_ref(_layernorm(x, axis=-1)[None], L0_ffn_gate_w, L0_ffn_gate_b, L0_ffn_w1, L0_ffn_w2, L0_ffn_w3)[0]
    return x

_drawn_inputs = setup_inputs


def setup_inputs(seed=0):
    import zlib

    import numpy as np

    out = dict(_drawn_inputs(seed))
    spreads = {'L0_mix_ln_k_g': (1.0, 0.6),
     'L0_mix_ln_k_b': (0.0, 0.8),
     'L0_mix_ln_v_g': (1.0, 0.6),
     'L0_mix_ln_v_b': (0.0, 0.8),
     'L0_ffn_gate_b': (0.0, 0.8)}
    factors = {'edge_attr_64': 8.0,
     'L0_gnn_W1': 7.81,
     'L0_gnn_b1': 8.0,
     'L0_gnn_W2': 7.594,
     'L0_gnn_b2': 27.245,
     'L0_gnn_c1': 8.0,
     'L0_gnn_c2': 3.126,
     'L0_mix_wq': 8.0,
     'L0_mix_wk': 8.0,
     'L0_mix_wv': 8.0,
     'L0_mix_wo': 8.0,
     'L0_mix_bo': 3.091,
     'L0_ffn_gate_w': 7.388,
     'L0_ffn_w1': 6.792,
     'L0_ffn_w2': 6.72,
     'L0_ffn_w3': 6.709}
    for name, (base, spread) in spreads.items():
        noise = np.random.default_rng([zlib.crc32(name.encode()), seed]).standard_normal(out[name].shape)
        drawn = base * np.exp(spread * noise) if base else spread * noise
        out[name] = jnp.asarray(drawn.astype(out[name].dtype))
    for name, factor in factors.items():
        out[name] = (out[name] * factor).astype(out[name].dtype)
    return out
```

```python
import concourse.bass as bass
import concourse.mybir as mybir
from contextlib import ExitStack

f32 = mybir.dt.float32
i32 = mybir.dt.int32
ALU = mybir.AluOpType
ACT = mybir.ActivationFunctionType
X = mybir.AxisListType.X

P = 128
N, D, E, RB = 3125, 256, 50000, 64
DC = D // P
NT = -(-N // P)
NP = NT * P
LAST = N - (NT - 1) * P
EG = 512
ET = EG // P
NG = -(-E // EG)
EP = NG * EG
W = 96
FW = 2 * W
NW = -(-NP // FW)
AW = NW * FW
FAR = 1 << 20
HEADS, HD = 4, 64
NX, HF = 16, 512
HC = HF // P
SB = 256
CAPB = (2 * N - NX) // SB + NX
CAPB += CAPB % 2
NS = CAPB * SB // P
EPS = 1e-5
MAGIC = 1597463007.0


def ds(start, size):
    return bass.ds(start, size)


def in_pairs(eng, n, body, peeled=False):
    if peeled:
        body(0, 0, 0)
        body(1, 0, 1)
    with eng.Fori(int(peeled), n // 2) as j:
        body(j * 2, j, 0)
        body(j * 2 + 1, j, 1)
    if n % 2:
        body(n - 1, n // 2, 0)


def gps_layer(nc, x_d, src_d, dst_d, first_d, rbf_d, W1_d, b1_d, W2_d, b2_d, U1_d, c1_d, U2_d, c2_d,
              wq_d, wkvT_d, woT_d, bo_d, kg_d, kb_d, vg_d, vb_d, gw_d, gb_d, w1_d, w2_d, w3_d, out_d):
    xn_d = nc.dram_tensor("xn_rows", (NP, D), f32).ap()
    xn2_d = nc.dram_tensor("xn2_rows", (NP, D), f32).ap()
    y_d = nc.dram_tensor("expert_rows", (CAPB * SB, D), f32).ap()

    ctx = ExitStack()
    with ctx:
        def sb(name, shape, dt=f32):
            return ctx.enter_context(nc.sbuf_tensor(name, shape, dt))

        def sem(name):
            return ctx.enter_context(nc.semaphore(name))

        ident = sb("ident", [P, P])
        ones = sb("ones", [P, P])
        before = sb("before", [P, P])
        iota = sb("iota", [P, FW])
        valid = sb("valid", [P, 1])
        tok = sb("tok", [P, 2, NT])
        W1 = sb("W1", [RB, D])
        b1 = sb("b1", [P, DC])
        W2 = sb("W2", [P, DC, D])
        b2bc = sb("b2bc", [P, 2, D])
        U1 = sb("U1", [P, 2 * DC, D])
        c1 = sb("c1", [P, DC])
        U2 = sb("U2", [P, DC, D])
        cb = sb("cb", [P, 2, D])
        wq = sb("wq", [P, DC, D])
        wkv = sb("wkv", [P, DC, 2 * D])
        woT = sb("woT", [P, DC, D])
        kgb = sb("kgb", [P, 2, P])
        vgb = sb("vgb", [P, 2])
        gw = sb("gw", [P, DC, NX])
        gb = sb("gb", [P, NX])
        x = sb("x_nodes", [P, NT, D])
        xnT = sb("xnT", [P, DC, NP])
        agg = sb("aggrT", [P, DC, AW])
        xn = [sb(f"xn{i}", [P, D]) for i in range(2)]
        xt = [sb(f"xt{i}", [P, DC, P]) for i in range(2)]
        st6 = sb("st6", [P, NT, 6])
        mean = sb("mean", [P, NT])
        rstd = sb("rstd", [P, NT])
        v_a = sb("v_a", [P, NT * 8])
        v_b = sb("v_b", [P, NT * 8])
        v_c = sb("v_c", [P, NT * 8])
        ssq = sb("ssq", [P, NT * 8])
        kvr = sb("kvr", [P, NT * 8])
        M = wkv[:, :, 0:D]
        arena = sb("arena", [P, NT * 2 * D])
        kvc = arena[:, :].rearrange("p (t c) -> p t c", t=NT)
        srcs = sb("srcs", [P, NG * ET], i32)
        dstf = sb("dstf", [P, NG * ET])
        rel = sb("rel", [P, NG * ET])
        dsti = rel[:, :].bitcast(i32)
        basef = sb("basef", [P, NG])
        basei = sb("basei", [P, NG], i32)
        flag = sb("flag", [P, 1], i32)
        cover = arena[:, 0:NG * ET]
        rbf = [sb(f"rbf{i}", [RB, EG]) for i in range(2)]
        h1T = [sb(f"h1T{i}", [P, DC, EG]) for i in range(2)]
        th = [sb(f"th{i}", [P, ET, D]) for i in range(2)]
        hg = [sb(f"hg{i}", [P, ET, D]) for i in range(2)]
        msg = [sb(f"msg{i}", [P, ET, D]) for i in range(2)]
        oh = [sb(f"oh{i}", [P, ET, FW]) for i in range(2)]
        idx = [sb(f"idx{i}", [P, ET], i32) for i in range(2)]

        sq = [th[i][:, 0:2, :].rearrange("p a d -> p (a d)") for i in range(2)]
        khs = [msg[i][:, :, :].rearrange("p a d -> p (a d)")[:, 0:2 * (P + 2)]
               .rearrange("p (j c) -> p j c", j=2) for i in range(2)]
        vhs = [hg[i][:, 0, :] for i in range(2)]
        kvt = h1T[0][:, 0, 0:DC * P].rearrange("p (c d) -> p c d", c=DC)
        kv_t = h1T[0][:, 1, 0:P]
        kv_r = h1T[0][:, 1, P:2 * P]
        kv_s = h1T[0][:, 1, 2 * P:2 * P + 1]
        A1 = h1T[1][:, :, 0:D]
        sst = [h1T[i][:, :, 0:P] for i in range(2)]
        def part(at, *shape):
            size = 1
            for s in shape:
                size *= s
            ap = arena[:, at:at + size]
            return ap if len(shape) == 1 else ap.rearrange("p (a b) -> p a b", a=shape[0])
        TX = NT * NX
        lg = part(0, NT, NX)
        ohx = [part(TX * (1 + k), NT, NX) for k in range(2)]
        m12 = part(TX * 3, NT, NX)
        t_a = part(TX * 4, NT, NX)
        t_b = part(TX * 5, NT, NX)
        t_et = part(TX * 6, NX, NT)
        t_in = part(TX * 7, NX, NT)
        t_ex = part(TX * 8, NX, NT)
        top = part(TX * 9, 2, NT)
        n_e = part(TX * 9 + 64, NX)
        c_e = part(TX * 9 + 80, NX)
        cend = part(TX * 9 + 96, NX)
        off = part(TX * 9 + 112, NX)
        c_i = sb("c_i", [P, NX], i32)
        texp_f = part(TX * 9 + 128, CAPB)
        tcmp = part(TX * 10, CAPB, NX)
        onerow = part(TX * 10 + CAPB * NX, TX)
        texp = sb("texp", [P, CAPB], i32)
        posf = part(TX * 6 + 0, 2, NT)
        posi = sb("posi", [P, 2, NT], i32)
        bits = part(TX * 6 + 64, 2, NT).bitcast(i32)
        lof = part(TX * 6 + 128, 2, NT)
        hif = part(TX * 6 + 192, 2, NT)
        wts = sb("wts", [P, 2, NT])
        exw = sb("exw", [P, NT])
        tA = [oh[i][:, 0, 0:P] for i in range(2)]
        tB = [oh[i][:, 1, 0:NS] for i in range(2)]
        tab = sb("tab", [P, NS], i32)
        flat = agg[:, :, :].rearrange("p c n -> p (c n)")
        WB = 2 * DC * HF
        w12 = [flat[:, i * WB:(i + 1) * WB].rearrange("p (m c h) -> p m c h", m=2, c=DC) for i in range(2)]
        w3 = [part(HC * D * i, HC, D) for i in range(2)]
        A0 = NT * 2 * D - 8192
        xs = [part(A0 + 512 * i, 2, D) for i in range(2)]
        xsT = [part(A0 + 1024 + 512 * i, DC, SB) for i in range(2)]
        gate = [part(A0 + 2048 + 512 * i, 512) for i in range(2)]
        hid = [part(A0 + 3072 + HC * SB * i, HC, SB) for i in range(2)]
        ys = [part(A0 + 5120 + 512 * i, 2, D) for i in range(2)]
        yg = [part(A0 + 6144 + 512 * i, 2, D) for i in range(2)]
        oo = [part(A0 + 7168 + 512 * i, 2, D) for i in range(2)]

        ps = ctx.enter_context(nc.psum_tensor("ps", [P, 8, 512], f32))

        s_par = sem("params_in")
        s_x = [sem(f"x_in{i}") for i in range(3)]
        s_edge = sem("edge_tables_in")
        s_const = sem("constants_made")
        s_pc = sem("pool_steps")
        s_xpad = sem("x_padding_zeroed")
        s_dve = sem("vector_steps")
        s_xn = sem("xn_made")
        s_xnst = [sem(f"xn_stored{i}") for i in range(2)]
        s_tp = sem("xn_transposed")
        s_xt = sem("xt_copied")
        s_xnT = sem("xnT_kept")
        s_kv = sem("kv_projected")
        s_kvd = sem("kv_drained")
        s_sq = sem("squares_summed")
        s_kh = sem("kv_scaled")
        s_khp = sem("kv_summed")
        s_mx = sem("mix_products")
        s_mv = sem("mix_vector")
        s_rbf = [sem(f"rbf_in{i}") for i in range(2)]
        s_w1 = sem("edge_w1_done")
        s_silu = sem("edge_silu_done")
        s_w2 = sem("edge_w2_done")
        s_zb = sem("edge_bias_added")
        s_th = sem("edge_tanh_done")
        s_idx = sem("src_indices_staged")
        s_hg = [sem(f"src_rows_in{i}") for i in range(2)]
        s_msg = sem("messages_made")
        s_sc = sem("messages_scattered")
        s_agg = sem("window_added")
        s_cov = sem("uncovered_counted")
        s_flag = sem("flag_ready")
        s_gnn = sem("aggregate_done")
        s_xcb = sem("x_plus_biases")
        s_xnc = sem("xn_tile_staged")
        s_u1 = sem("u1_done")
        s_us = sem("u1_silu_done")
        s_uo = sem("u2_done")
        s_x1 = sem("x1_made")
        s_xn2 = sem("xn2_made")
        s_xn2st = [sem(f"xn2_stored{i}") for i in range(2)]
        s_tp2 = sem("xn2_transposed")
        s_xt2 = sem("xt2_copied")
        s_lg = sem("logits_done")
        s_lgc = sem("logits_copied")
        s_m12 = sem("choices_made")
        s_cnt = sem("choices_counted")
        s_dif = sem("logit_gap_made")
        s_ex = sem("gap_exp_done")
        s_hot = sem("slot_onehots_made")
        s_tab = sem("slot_table_done")
        s_tabi = sem("slot_table_kept")
        s_texp = sem("block_experts_ready")
        s_w12 = [sem(f"w12_in{i}") for i in range(2)]
        s_w3 = [sem(f"w3_in{i}") for i in range(2)]
        s_sidx = sem("slot_indices_staged")
        s_xs = [sem(f"slot_rows_in{i}") for i in range(2)]
        s_xsp = sem("slots_transposed")
        s_xsT = sem("slots_copied")
        s_h = sem("expert_up_done")
        s_g = sem("expert_silu_done")
        s_hid = sem("expert_hidden_made")
        s_o = sem("expert_down_done")
        s_y = sem("expert_out_copied")
        s_yst = [sem(f"expert_rows_stored{i}") for i in range(2)]
        s_pidx = sem("pair_indices_staged")
        s_yg = [sem(f"pair_rows_in{i}") for i in range(2)]
        s_fin = sem("out_made")
        s_out = [sem(f"out_stored{i}") for i in range(2)]

        block = ctx.enter_context(nc.Block())
        NPAR = 22

        @block.sync
        def _(sp):
            sp.dma_start(x[:, 0:12, :], x_d[0:12 * P, :].rearrange("(t p) d -> p t d", p=P)).then_inc(s_x[0], 16)
            sp.dma_start(x[:, 12:24, :], x_d[12 * P:24 * P, :].rearrange("(t p) d -> p t d", p=P)).then_inc(s_x[1], 16)
            sp.wait_ge(s_xpad, 1)
            sp.dma_start(x[0:LAST, NT - 1, :], x_d[(NT - 1) * P:N, :]).then_inc(s_x[2], 16)
            sp.dma_start(dsti, dst_d).then_inc(s_edge, 16)
            sp.dma_start(srcs[:, :], src_d).then_inc(s_edge, 16)
            sp.dma_start(basei[:, :], first_d.to_broadcast([P, NG])).then_inc(s_edge, 16)

            def store_xn(t, j, p):
                sp.wait_ge(s_xn, t + 1)
                sp.dma_start(xn_d[ds(t * P, P), :], xn[p][:, :]).then_inc(s_xnst[p], 16)
            in_pairs(sp, NT, store_xn)

            def edges(n0, h0):
                def load(i, j, p):
                    sp.wait_ge(s_w1, (n0 + i) * 2 + 2)
                    sp.dma_start(rbf[p][:, :], rbf_d[ds(i, 1), :, :].rearrange("a r e -> (a r) e"))\
                        .then_inc(s_rbf[p], 16)
                in_pairs(sp, NG, load)
            edges(0, 0)
            sp.wait_ge(s_flag, 1)
            left = sp.value_load(flag[0:1, 0:1], min_val=0, max_val=E)
            with sp.If(left > 0):
                with sp.Fori(0, NW) as w:
                    edges((w + 1) * NG, (w + 1) * (NG // 2))

            def store_xn2(t, j, p):
                sp.wait_ge(s_xn2, t + 1)
                sp.dma_start(xn2_d[ds(t * P, P), :], xn[p][:, :]).then_inc(s_xn2st[p], 16)
            in_pairs(sp, NT, store_xn2)

            sp.wait_ge(s_texp, 1)
            def store_y(i, j, p):
                sp.wait_ge(s_y, 2 + i + 1)
                sp.dma_start(y_d[ds(i * SB, SB), :].rearrange("(s p) d -> p s d", p=P), ys[p])\
                    .then_inc(s_yst[p], 16)

            def load_w(i, p):
                e = sp.value_load(texp[0:1, ds(i, 1)], min_val=0, max_val=NX - 1)
                sp.wait_ge(s_h, 4 * i + 4)
                for m, w_d in enumerate((w1_d, w2_d)):
                    sp.dma_start(w12[p][:, m, :, :],
                                 w_d[ds(e, 1), :, :].rearrange("e (c p) h -> p (e c) h", p=P))\
                        .then_inc(s_w12[p], 16)
                sp.wait_ge(s_o, i + 1)
                sp.dma_start(w3[p], w3_d[ds(e, 1), :, :].rearrange("e (c p) h -> p (e c) h", p=P))\
                    .then_inc(s_w3[p], 16)
            load_w(0, 0)
            load_w(1, 1)
            store_y(0, 0, 0)
            with sp.Fori(1, CAPB // 2) as j:
                load_w(j * 2, 0)
                store_y(j * 2 - 1, j - 1, 1)
                load_w(j * 2 + 1, 1)
                store_y(j * 2, j, 0)
            store_y(CAPB - 1, CAPB // 2 - 1, 1)

            def store_out(t, j, p, rows=P):
                sp.wait_ge(s_fin, t + 3)
                sp.dma_start(out_d[ds(t * P, rows), :], oo[p][0:rows, 1, :]).then_inc(s_out[p], 16)
            with sp.Fori(0, NT // 2) as j:
                store_out(j * 2, j, 0)
                store_out(j * 2 + 1, j, 1)
            store_out(NT - 1, NT // 2, 0, LAST)
            for p in range(2):
                sp.wait_ge(s_out[p], 16 * ((NT + 1 - p) // 2))

        @block.gpsimd
        def _(pool):
            steps = [0]

            def link(ins):
                steps[0] += 1
                ins.then_inc(s_pc, 1)
                pool.wait_ge(s_pc, steps[0])

            pool.memset(x[:, NT - 1, :], 0.0).then_inc(s_xpad, 1)
            link(pool.memset(ident[:, :], 0.0))
            link(pool.affine_select(out=ident[:, :], in_=ident[:, :], compare_op=ALU.not_equal, fill=1.0,
                                    base=0, pattern=[[-1, P]], channel_multiplier=1))
            link(pool.memset(ones[:, :], 1.0))
            link(pool.affine_select(out=before[:, :], in_=ones[:, :], compare_op=ALU.is_gt, fill=0.0,
                                    base=0, pattern=[[1, P]], channel_multiplier=-1))
            link(pool.iota(iota[:, :], [[1, FW]], base=0, channel_multiplier=0,
                           allow_small_or_imprecise_dtypes=True))
            link(pool.iota(tok[:, :, :], [[0, 2], [P, NT]], base=0, channel_multiplier=1,
                           allow_small_or_imprecise_dtypes=True))
            link(pool.affine_select(out=tok[:, :, :], in_=tok[:, :, :], compare_op=ALU.is_gt, fill=0.0,
                                    base=N, pattern=[[0, 2], [-P, NT]], channel_multiplier=-1))
            link(pool.affine_select(out=valid[:, :], in_=ones[:, 0:1], compare_op=ALU.is_gt, fill=0.0,
                                    base=LAST, pattern=[[0, 1]], channel_multiplier=-1))
            for p in range(2):
                link(pool.memset(khs[p][:, :, P:P + 2], 1.0))
            link(pool.memset(kvt, 0.0))
            pool.memset(agg[:, :, :], 0.0).then_inc(s_const, 1)

            pool.sem_inc(s_xnT, 2)
            def keep(t, j, p):
                pool.wait_ge(s_xt, t + 1)
                pool.tensor_copy(xnT[:, :, ds(t * P, P)], xt[p][:, :, :]).then_inc(s_xnT, 1)
            in_pairs(pool, NT, keep)

            pool.wait_ge(s_par, 16 * NPAR)
            pool.wait_ge(s_xn, NT)
            link(pool.tensor_tensor(cb[:, 0, :], cb[:, 0, :], cb[:, 1, :], ALU.add))
            def biased(t, j, p):
                pool.tensor_tensor(x[:, ds(t, 1), :], x[:, ds(t, 1), :], cb[:, 0:1, :], ALU.add).then_inc(s_xcb, 1)
            in_pairs(pool, NT, biased)

            for p in range(2):
                pool.wait_ge(s_xnst[p], 16 * ((NT + 1 - p) // 2))
            pool.wait_ge(s_edge, 48)

            def edges(n0, h0):
                def gather(i, j, p):
                    pool.wait_ge(s_msg, n0 + i + 1)
                    pool.tensor_copy(idx[p][:, :], srcs[:, ds(i * ET, ET)]).then_inc(s_idx, 1)
                    pool.wait_ge(s_edge, 64)
                    pool.wait_ge(s_idx, n0 + i + 1)
                    for s in range(ET):
                        pool.indirect_dma_start(hg[p][:, s, :], None, xn_d[:, :],
                                                bass.IndirectOffsetOnAxis(idx[p][:, s:s + 1], 0))\
                            .then_inc(s_hg[p], 16)
                in_pairs(pool, NG, gather)
            pool.wait_ge(s_mv, 5)
            edges(0, 0)
            pool.wait_ge(s_flag, 1)
            left = pool.value_load(flag[0:1, 0:1], min_val=0, max_val=E)
            with pool.If(left > 0):
                with pool.Fori(0, NW) as w:
                    edges((w + 1) * NG, (w + 1) * (NG // 2))

            def stage(t, j, p):
                pool.wait_ge(s_uo, t + 1)
                pool.tensor_copy(xt[p][:, :, :], xnT[:, :, ds(t * P, P)]).then_inc(s_xnc, 1)
            in_pairs(pool, NT, stage)

            for p in range(2):
                pool.wait_ge(s_xn2st[p], 16 * ((NT + 1 - p) // 2))
            pool.wait_ge(s_tabi, 1)
            def gather_slots(i, j, p):
                pool.wait_ge(s_xsp, i + 1)
                pool.tensor_copy(idx[p][:, 0:2], tab[:, ds(i * 2, 2)]).then_inc(s_sidx, 1)
                pool.wait_ge(s_tabi, 1)
                pool.wait_ge(s_sidx, i + 1)
                for s in range(2):
                    pool.indirect_dma_start(xs[p][:, s, :], None, xn2_d[:, :],
                                            bass.IndirectOffsetOnAxis(idx[p][:, s:s + 1], 0))\
                        .then_inc(s_xs[p], 16)
            in_pairs(pool, CAPB, gather_slots)

            for p in range(2):
                pool.wait_ge(s_yst[p], 16 * (CAPB // 2))
                pool.wait_ge(s_xs[p], 32 * (CAPB // 2))
            def gather_pairs(t, j, p):
                pool.wait_ge(s_fin, t + 1)
                pool.tensor_copy(idx[p][:, 0:2], posi[:, :, ds(t, 1)].rearrange("p k t -> p (k t)"))\
                    .then_inc(s_pidx, 1)
                pool.wait_ge(s_tabi, 1)
                pool.wait_ge(s_pidx, t + 1)
                for k in range(2):
                    pool.indirect_dma_start(yg[p][:, k, :], None, y_d[:, :],
                                            bass.IndirectOffsetOnAxis(idx[p][:, k:k + 1], 0))\
                        .then_inc(s_yg[p], 16)
            in_pairs(pool, NT, gather_pairs)

        @block.scalar
        def _(act):
            def row(ap, n, parts=P):
                return ap.rearrange("(a n) -> a n", a=1).to_broadcast([parts, n])

            for dst, src in (
                (wkv[:, :, :], wkvT_d.rearrange("(c p) n -> p c n", p=P)),
                (W1[:, :], W1_d), (W2[:, :, :], W2_d.rearrange("(c p) n -> p c n", p=P)),
                (b1[:, :], b1_d),
                (c1[:, :], c1_d),
                (b2bc[:, 0, :], row(b2_d, D)), (b2bc[:, 1, :], row(b2_d, D)),
                (U1[:, :, :], U1_d.rearrange("(c p) n -> p c n", p=P)),
                (U2[:, :, :], U2_d.rearrange("(c p) n -> p c n", p=P)),
                (wq[:, :, :], wq_d.rearrange("(c p) n -> p c n", p=P)),
                (woT[:, :, :], woT_d.rearrange("(c p) n -> p c n", p=P)),
                (cb[:, 0, :], row(c2_d, D)), (cb[:, 1, :], row(bo_d, D)),
                (kgb[:, 0, 0:HD], row(kg_d, HD)), (kgb[:, 0, HD:P], row(kg_d, HD)),
                (kgb[:, 1, 0:HD], row(kb_d, HD)), (kgb[:, 1, HD:P], row(kb_d, HD)),
                (vgb[0:HD, 0:1], vg_d.rearrange("(n a) -> n a", a=1)),
                (vgb[HD:P, 0:1], vg_d.rearrange("(n a) -> n a", a=1)),
                (vgb[0:HD, 1:2], vb_d.rearrange("(n a) -> n a", a=1)),
                (vgb[HD:P, 1:2], vb_d.rearrange("(n a) -> n a", a=1)),
                (gw[:, :, :], gw_d.rearrange("(c p) n -> p c n", p=P)),
            ):
                act.dma_start(dst, src).then_inc(s_par, 16)
            act.dma_start(gb[:, :], row(gb_d, NX)).then_inc(s_edge, 16)
            act.wait_ge(s_par, 16 * NPAR)

            act.sem_inc(s_kvd, 2)
            def copy_xt(t, p):
                act.wait_ge(s_tp, t + 3)
                act.wait_ge(s_xnT, t + 1)
                act.wait_ge(s_kv, t + 1)
                act.copy(xt[p][:, :, :], ps[:, p, 0:D].rearrange("p (c q) -> p c q", c=DC)).then_inc(s_xt, 1)

            def drain_kv(t, j, p):
                act.wait_ge(s_kv, t + 3)
                act.copy(kvc[:, ds(t, 1), :].rearrange("p a c -> p (a c)"), ps[:, 2 + p, :])
                act.wait_ge(s_sq, t + 1)
                act.activation(sq[p], ps[:, 2 + p, :], ACT.Square).then_inc(s_kvd, 1)
            copy_xt(0, 0)
            with act.Fori(0, NT // 2) as j:
                copy_xt(j * 2 + 1, 1)
                drain_kv(j * 2, j, 0)
                copy_xt(j * 2 + 2, 0)
                drain_kv(j * 2 + 1, j, 1)
            drain_kv(NT - 1, NT // 2, 0)

            act.sem_inc(s_silu, 2)
            act.wait_ge(s_mv, 5)
            def edges(n0, h0):
                def silu(i, p):
                    for m in range(DC):
                        act.wait_ge(s_w1, (n0 + i) * 2 + 5 + m)
                        act.wait_ge(s_w2, (n0 + i) * 2 + 2)
                        act.activation(h1T[p][:, m, :], ps[:, m, :], ACT.Silu, bias=b1[:, m:m + 1]).then_inc(s_silu, 1)

                def tanh(i, p):
                    act.wait_ge(s_zb, (n0 + i) * 2 + 4)
                    act.activation(th[p][:, :, :], th[p][:, :, :], ACT.Tanh, scale=0.5).then_inc(s_th, 1)
                silu(0, 0)
                with act.Fori(0, NG // 2 - 1) as j:
                    silu(j * 2 + 1, 1)
                    tanh(j * 2, 0)
                    silu(j * 2 + 2, 0)
                    tanh(j * 2 + 1, 1)
                silu(NG - 1, 1)
                tanh(NG - 2, 0)
                tanh(NG - 1, 1)
            edges(0, 0)
            act.wait_ge(s_flag, 1)
            left = act.value_load(flag[0:1, 0:1], min_val=0, max_val=E)
            with act.If(left > 0):
                with act.Fori(0, NW) as w:
                    edges((w + 1) * NG, (w + 1) * (NG // 2))

            act.sem_inc(s_us, 2)
            def u1_silu(t, j, p):
                act.wait_ge(s_u1, t + 1)
                act.wait_ge(s_uo, t + 1)
                for m in range(DC):
                    last = act.activation(sst[p][:, m, :], ps[:, p, m * P:(m + 1) * P], ACT.Silu, bias=c1[:, m:m + 1])
                last.then_inc(s_us, 1)
            in_pairs(act, NT, u1_silu)

            def copy_xt2(t, j, p):
                act.wait_ge(s_tp2, t + 3)
                act.wait_ge(s_lg, t + 1)
                act.copy(xt[p][:, :, :], ps[:, 4 + p, 0:D].rearrange("p (c q) -> p c q", c=DC)).then_inc(s_xt2, 1)
            in_pairs(act, NT, copy_xt2)

            act.wait_ge(s_dif, 1)
            act.activation(exw[:, :], exw[:, :], ACT.Exp).then_inc(s_ex, 1)

            act.sem_inc(s_xsT, 1)
            act.sem_inc(s_y, 2)
            def copy_xsT(i, p):
                act.wait_ge(s_xsp, i + 3)
                act.wait_ge(s_h, i * 4 + 4)
                act.copy(xsT[p], ps[:, 7, :].rearrange("p (c q) -> p c q", c=DC)).then_inc(s_xsT, 1)

            def silu_g(i, q):
                act.wait_ge(s_h, i * 4 + 8 + 2 * q + 1)
                act.wait_ge(s_hid, i * 2 + q + 1)
                act.activation(gate[q], ps[:, q, :], ACT.Silu).then_inc(s_g, 1)

            def copy_y(i, j, p):
                act.wait_ge(s_o, i + 3)
                if i is not p:
                    act.wait_ge(s_yst[p], j * 16)
                act.copy(ys[p], ps[:, 4 + p, :].rearrange("p (s d) -> p s d", s=2)).then_inc(s_y, 1)
            def two_blocks(i, j):
                silu_g(i + 1, 0)
                copy_xsT(i + 2, 0)
                copy_y(i, j, 0)
                silu_g(i + 1, 1)
                silu_g(i + 2, 0)
                copy_xsT(i + 3, 1)
                copy_y(i + 1, j, 1)
                silu_g(i + 2, 1)
            copy_xsT(0, 0)
            silu_g(0, 0)
            copy_xsT(1, 1)
            silu_g(0, 1)
            two_blocks(0, 0)
            with act.Fori(1, CAPB // 2 - 1) as j:
                two_blocks(j * 2, j)
            silu_g(CAPB - 1, 0)
            copy_y(CAPB - 2, CAPB // 2 - 1, 0)
            silu_g(CAPB - 1, 1)
            copy_y(CAPB - 1, CAPB // 2 - 1, 1)

        @block.vector
        def _(dve):
            steps = [0]

            def link(ins):
                steps[0] = steps[0] + 1
                ins.then_inc(s_dve, 1)
                dve.wait_ge(s_dve, steps[0])

            def rsqrt(y, v, a, b):
                link(dve.tensor_scalar(a.bitcast(i32), v.bitcast(i32), 1, None, ALU.arith_shift_right))
                link(dve.tensor_scalar(y.bitcast(i32), a.bitcast(i32), -1.0, MAGIC, ALU.mult, ALU.add))
                for _ in range(4):
                    link(dve.tensor_tensor(a, y, y, ALU.mult))
                    link(dve.tensor_tensor(b, a, v, ALU.mult))
                    link(dve.tensor_scalar(a, b, -0.5, 1.5, ALU.mult, ALU.add))
                    link(dve.tensor_tensor(y, y, a, ALU.mult))

            def layer_stats():
                a, b, v = v_a[:, 0:NT], v_b[:, 0:NT], v_c[:, 0:NT]
                link(dve.tensor_tensor(a, st6[:, :, 1], st6[:, :, 4], ALU.add))
                link(dve.tensor_scalar(mean[:, :], a, 0.5, None, ALU.mult))
                link(dve.tensor_tensor(a, st6[:, :, 1], st6[:, :, 4], ALU.subtract))
                link(dve.tensor_tensor(b, a, a, ALU.mult))
                link(dve.tensor_tensor(a, st6[:, :, 2], st6[:, :, 5], ALU.add))
                link(dve.tensor_scalar(b, b, 0.25, EPS, ALU.mult, ALU.add))
                link(dve.scalar_tensor_tensor(v, a, 1.0 / D, b, ALU.mult, ALU.add))
                rsqrt(rstd[:, :], v, a, b)

            def stats(t, j=None, p=None):
                return dve.bn_stats(st6[:, ds(t, 1), :].rearrange("p a s -> p (a s)"),
                                    x[:, ds(t, 1), :].rearrange("p a d -> p (a d)"))
            dve.wait_ge(s_x[0], 16)
            with dve.Fori(0, 12) as t:
                stats(t)
            dve.wait_ge(s_x[1], 16)
            with dve.Fori(12, 24) as t:
                stats(t)
            dve.wait_ge(s_x[2], 16)
            link(stats(NT - 1))
            layer_stats()

            dve.wait_ge(s_par, 16 * NPAR)
            for c in range(DC):
                heads = wkv[:, c, :].rearrange("p (h d) -> p h d", d=HD)
                link(dve.tensor_reduce(v_a[:, 0:8], heads, X, ALU.add))
                link(dve.tensor_scalar(v_a[:, 0:8], v_a[:, 0:8], 1.0 / HD, None, ALU.mult))
                link(dve.tensor_tensor(heads, heads, v_a[:, 0:8].unsqueeze(2).to_broadcast([P, 8, HD]), ALU.subtract))
            dve.sem_inc(s_mv, 1)

            dve.sem_inc(s_sq, 2)
            def make_xn(t, j, p, ready, stored, used):
                if t is not p:
                    dve.wait_ge(stored[p], j * 16)
                dve.wait_ge(used, t + 1)
                dve.tensor_scalar(xn[p][:, :], x[:, ds(t, 1), :].rearrange("p a d -> p (a d)"),
                                  mean[:, ds(t, 1)], rstd[:, ds(t, 1)], ALU.subtract, ALU.mult).then_inc(ready, 1)

            def xn1(t, j, p):
                make_xn(t, j, p, s_xn, s_xnst, s_tp)

            def sum_sq(t, j, p):
                dve.wait_ge(s_kvd, t + 3)
                dve.tensor_reduce(ssq[:, ds(t * 8, 8)], sq[p].rearrange("p (h d) -> p h d", d=HD), X, ALU.add)\
                    .then_inc(s_sq, 1)
            xn1(0, 0, 0)
            xn1(1, 0, 1)
            with dve.Fori(0, NT // 2 - 1) as j:
                xn1(j * 2 + 2, j + 1, 0)
                sum_sq(j * 2, j, 0)
                xn1(j * 2 + 3, j + 1, 1)
                sum_sq(j * 2 + 1, j, 1)
            xn1(NT - 1, NT // 2, 0)
            for t in range(NT - 3, NT):
                sum_sq(t, t // 2, t % 2)
            dve.wait_ge(s_sq, NT + 2)
            link(dve.tensor_scalar(v_c[:, :], ssq[:, :], 1.0 / HD, EPS, ALU.mult, ALU.add))
            rsqrt(kvr[:, :], v_c[:, :], v_a[:, :], v_b[:, :])

            def scale_kv(t, j, p):
                dve.wait_ge(s_khp, t + 1)
                r = kvr[:, ds(t * 8, 8)].unsqueeze(2).to_broadcast([P, 8, HD])
                kv = kvc[:, ds(t, 1), :].rearrange("p a (h d) -> p (a h) d", d=HD)
                for jj in range(2):
                    dve.tensor_tensor(khs[p][:, jj, 0:P].rearrange("p (h d) -> p h d", d=HD),
                                      kv[:, 2 * jj:2 * jj + 2, :], r[:, 2 * jj:2 * jj + 2, :], ALU.mult)
                dve.tensor_tensor(vhs[p].rearrange("p (h d) -> p h d", d=HD), kv[:, 4:8, :], r[:, 4:8, :], ALU.mult)\
                    .then_inc(s_kh, 1)
            dve.wait_ge(s_const, 1)
            in_pairs(dve, NT, scale_kv)

            dve.wait_ge(s_mx, 1)
            for c in range(DC):
                link(dve.tensor_copy(kv_s, ps[:, 4 + c, P:P + 1]))
                link(dve.tensor_tensor(kv_t, ps[:, 4 + c, 0:P], kgb[:, 0, :], ALU.mult))
                link(dve.scalar_tensor_tensor(kv_t, kgb[:, 1, :], kv_s, kv_t, ALU.mult, ALU.add))
                link(dve.tensor_tensor(kv_r, ps[:, 6, c * P:(c + 1) * P], kgb[:, 0, :], ALU.mult))
                link(dve.scalar_tensor_tensor(kv_r, kgb[:, 1, :], float(N), kv_r, ALU.mult, ALU.add))
                link(dve.tensor_scalar(kv_t, kv_t, vgb[:, 0:1], None, ALU.mult))
                for h in range(2):
                    q = slice(h * HD, (h + 1) * HD)
                    link(dve.scalar_tensor_tensor(kvt[q, c, q], kv_r[q, :][:, q], vgb[q, 1:2], kv_t[q, :][:, q],
                                                  ALU.mult, ALU.add))
            dve.sem_inc(s_mv, 1)
            dve.wait_ge(s_mx, 2)
            link(dve.tensor_copy(A1, ps[:, 0, :].rearrange("p (c n) -> p c n", c=DC)))
            dve.sem_inc(s_mv, 1)
            dve.wait_ge(s_mx, 3)
            link(dve.tensor_scalar(M, ps[:, 1, :].rearrange("p (c n) -> p c n", c=DC), 1.0 / N, None, ALU.mult))
            for c in range(DC):
                q = slice(c * P, (c + 1) * P)
                link(dve.tensor_tensor(M[:, c, q], M[:, c, q], ident[:, :], ALU.add))
            dve.sem_inc(s_mv, 2)

            dve.wait_ge(s_edge, 64)
            link(dve.tensor_copy(dstf[:, :], dsti))
            link(dve.tensor_copy(basef[:, :], basei[:, :]))
            link(dve.tensor_scalar(basef[:, :], basef[:, :], 0.0, float(AW - W), ALU.max, ALU.min))
            link(dve.tensor_copy(basei[:, :], basef[:, :]))
            link(dve.tensor_tensor(rel[:, :].rearrange("p (g s) -> p g s", s=ET),
                                   dstf[:, :].rearrange("p (g s) -> p g s", s=ET),
                                   basef[:, :].unsqueeze(2).to_broadcast([P, NG, ET]), ALU.subtract))
            link(dve.tensor_scalar(cover, rel[:, :], 0.0, None, ALU.is_ge))
            link(dve.scalar_tensor_tensor(cover, rel[:, :], float(W), cover, ALU.is_lt, ALU.mult))
            link(dve.scalar_tensor_tensor(cover, dstf[:, :], 1.0, cover, ALU.add, ALU.mult))
            link(dve.tensor_tensor(dstf[:, :], dstf[:, :], cover, ALU.subtract))
            link(dve.tensor_scalar(cover, dstf[:, :], 0.0, None, ALU.is_ge))
            link(dve.scalar_tensor_tensor(cover, dstf[:, :], float(N), cover, ALU.is_lt, ALU.mult))
            link(dve.tensor_reduce(v_a[:, 0:1], cover, X, ALU.add))
            dve.sem_inc(s_cov, 1)
            dve.wait_ge(s_cov, 2)
            dve.tensor_copy(flag[:, :], ps[:, 7, 0:1]).then_inc(s_flag, 1)

            dve.sem_inc(s_zb, 2)
            dve.sem_inc(s_msg, 2)
            dve.sem_inc(s_agg, 2)

            def edges(n0, h0, w_n, base, rel_t):
                def onehot_bias(i, j, p):
                    for b in range(2):
                        dve.wait_ge(s_w2, (n0 + i) * 2 + 5 + b)
                        dve.tensor_tensor(th[p][:, 2 * b:2 * b + 2, :],
                                          ps[:, 2 + b, :].rearrange("p (s d) -> p s d", s=2),
                                          b2bc[:, :, :], ALU.add).then_inc(s_zb, 1)
                    dve.wait_ge(s_sc, n0 + i + 1)
                    dve.tensor_tensor(oh[p][:, :, 0:w_n], iota[:, 0:w_n].unsqueeze(1).to_broadcast([P, ET, w_n]),
                                      rel_t[:, ds(i * ET, ET)].unsqueeze(2).to_broadcast([P, ET, w_n]), ALU.is_equal)

                def message(i, j, p):
                    dve.wait_ge(s_th, n0 + i + 1)
                    dve.wait_ge(s_hg[p], (h0 + j + 1) * (16 * ET))
                    dve.scalar_tensor_tensor(msg[p][:, :, :], th[p][:, :, :], 1.0, hg[p][:, :, :], ALU.add, ALU.mult)\
                        .then_inc(s_msg, 1)

                def add_window(i, p):
                    at = base(i)
                    dve.wait_ge(s_sc, n0 + i + 3)
                    dve.wait_ge(s_agg, n0 + i + 2)
                    a = agg[:, :, ds(at, w_n)]
                    dve.scalar_tensor_tensor(a, ps[:, 4 + p, 0:DC * w_n].rearrange("p (c w) -> p c w", c=DC), 0.5,
                                             a, ALU.mult, ALU.add).then_inc(s_agg, 1)
                onehot_bias(0, 0, 0)
                message(0, 0, 0)
                onehot_bias(1, 0, 1)
                message(1, 0, 1)
                with dve.Fori(1, NG // 2) as j:
                    for p in range(2):
                        onehot_bias(j * 2 + p, j, p)
                        add_window(j * 2 + p - 2, p)
                        message(j * 2 + p, j, p)
                add_window(NG - 2, 0)
                add_window(NG - 1, 1)
            edges(0, 0, W, lambda i: dve.value_load(basei[0:1, ds(i, 1)], min_val=0, max_val=AW - W), rel)
            left = dve.value_load(flag[0:1, 0:1], min_val=0, max_val=E)
            with dve.If(left > 0):
                with dve.Fori(0, NW) as w:
                    edges((w + 1) * NG, (w + 1) * (NG // 2), FW, lambda i: w * FW, dstf)
                    dve.tensor_scalar(dstf[:, :], dstf[:, :], float(FW), None, ALU.subtract).then_inc(s_cov, 1)
                    dve.wait_ge(s_cov, w + 3)
            link(dve.tensor_copy(v_a[:, 0:1], agg[:, 0, 0:1]))
            dve.sem_inc(s_gnn, 1)

            dve.wait_ge(s_xcb, NT)
            dve.sem_inc(s_x1, 2)
            def x1(t, j, p):
                dve.wait_ge(s_uo, t + 3)
                xr = x[:, ds(t, 1), :].rearrange("p a d -> p (a d)")
                dve.tensor_tensor(xr, ps[:, 2 + p, 0:D], xr, ALU.add).then_inc(s_x1, 1)
            x1(0, 0, 0)
            with dve.Fori(0, NT // 2) as j:
                for p in range(2):
                    x1(j * 2 + p + 1, j, 1 - p)
                    dve.wait_ge(s_x1, j * 2 + p + 3)
                    stats(j * 2 + p)
            dve.wait_ge(s_x1, NT + 2)
            link(stats(NT - 1))
            layer_stats()

            def xn2(t, j, p):
                make_xn(t, j, p, s_xn2, s_xn2st, s_tp2)

            def logits(t, j, p):
                dve.wait_ge(s_lg, t + 3)
                dve.tensor_tensor(lg[:, ds(t, 1), :].rearrange("p a n -> p (a n)"), ps[:, 6 + p, 0:NX], gb[:, :], ALU.add)\
                    .then_inc(s_lgc, 1)
            dve.sem_inc(s_lgc, 2)
            xn2(0, 0, 0)
            xn2(1, 0, 1)
            with dve.Fori(0, NT // 2 - 1) as j:
                xn2(j * 2 + 2, j + 1, 0)
                logits(j * 2, j, 0)
                xn2(j * 2 + 3, j + 1, 1)
                logits(j * 2 + 1, j, 1)
            xn2(NT - 1, NT // 2, 0)
            for t in range(NT - 3, NT):
                logits(t, t // 2, t % 2)
            dve.wait_ge(s_lgc, NT + 2)

            io = iota[:, 0:NX].unsqueeze(1).to_broadcast([P, NT, NX])
            for k in range(2):
                m = top[:, k, :]
                link(dve.tensor_reduce(m, lg, X, ALU.max))
                link(dve.tensor_tensor(t_a, lg, m.unsqueeze(2).to_broadcast([P, NT, NX]), ALU.is_equal))
                link(dve.tensor_scalar(t_a, t_a, -float(NX), float(NX), ALU.mult, ALU.add))
                link(dve.tensor_tensor(t_a, t_a, io, ALU.add))
                link(dve.tensor_reduce(v_a[:, 0:NT], t_a, X, ALU.min))
                link(dve.tensor_tensor(ohx[k], io, v_a[:, 0:NT].unsqueeze(2).to_broadcast([P, NT, NX]), ALU.is_equal))
                if k == 0:
                    link(dve.scalar_tensor_tensor(lg, ohx[0], -3e38, lg, ALU.mult, ALU.add))
            link(dve.tensor_tensor(exw[:, :], top[:, 1, :], top[:, 0, :], ALU.subtract))
            dve.sem_inc(s_dif, 1)
            for k in range(2):
                link(dve.tensor_scalar(ohx[k][:, NT - 1, :], ohx[k][:, NT - 1, :], valid[:, 0:1], None, ALU.mult))
            link(dve.tensor_tensor(m12, ohx[0], ohx[1], ALU.add))
            dve.sem_inc(s_m12, 1)
            dve.wait_ge(s_ex, 1)
            link(dve.tensor_scalar(v_a[:, 0:NT], exw[:, :], 1.0, None, ALU.add))
            link(dve.reciprocal(wts[:, 0, :], v_a[:, 0:NT]))
            link(dve.tensor_tensor(wts[:, 1, :], wts[:, 0, :], exw[:, :], ALU.mult))

            dve.wait_ge(s_cnt, 1)
            link(dve.memset(onerow, 1.0))
            link(dve.tensor_copy(t_et, ps[:, 1, 0:TX].rearrange("p (t e) -> p e t", e=NX)))
            ff = lambda ap: ap.rearrange("p a b -> p (a b)")
            link(dve.tensor_tensor_scan(ff(t_in), onerow, ff(t_et), 0.0, ALU.mult, ALU.add))
            link(dve.tensor_tensor(t_ex, t_in, t_et, ALU.subtract))
            link(dve.tensor_tensor(n_e, t_in[:, :, NT - 1], t_ex[:, :, 0], ALU.subtract))
            link(dve.tensor_scalar(c_i[:, :], n_e, float(SB - 1), None, ALU.add))
            link(dve.tensor_scalar(c_i[:, :], c_i[:, :], SB.bit_length() - 1, None, ALU.arith_shift_right))
            link(dve.tensor_copy(c_e, c_i[:, :]))
            link(dve.tensor_tensor_scan(cend, onerow[:, 0:NX], c_e, 0.0, ALU.mult, ALU.add))
            link(dve.tensor_tensor(off, cend, c_e, ALU.subtract))
            link(dve.scalar_tensor_tensor(off, off, float(SB), t_ex[:, :, 0], ALU.mult, ALU.subtract))
            link(dve.tensor_tensor(t_a, t_ex.rearrange("p e t -> p t e"),
                                   off.unsqueeze(1).to_broadcast([P, NT, NX]), ALU.add))
            link(dve.tensor_tensor(t_a, ps[:, 0, 0:TX].rearrange("p (t e) -> p t e", e=NX), t_a, ALU.add))
            for k in range(2):
                link(dve.tensor_tensor(t_b, ohx[k], t_a, ALU.mult))
                link(dve.tensor_reduce(posf[:, k, :], t_b, X, ALU.add))
            link(dve.tensor_copy(posi[:, :, :], posf))
            link(dve.tensor_scalar(bits, posi[:, :, :], P - 1, None, ALU.bitwise_and))
            link(dve.tensor_copy(lof, bits))
            link(dve.tensor_scalar(bits, posi[:, :, :], 7, None, ALU.arith_shift_right))
            link(dve.tensor_copy(hif, bits))
            link(dve.tensor_tensor(tcmp, cend.unsqueeze(1).to_broadcast([P, CAPB, NX]),
                                   iota[:, 0:CAPB].unsqueeze(2).to_broadcast([P, CAPB, NX]), ALU.is_le))
            link(dve.tensor_reduce(texp_f, tcmp, X, ALU.add))
            dve.tensor_scalar(texp[:, :], texp_f, float(NX - 1), None, ALU.min).then_inc(s_texp, 1)

            def onehots(c, p, waits=True):
                k_t = lambda ap: ap.rearrange("p k t -> p (k t)")[:, ds(c, 1)]
                if waits:
                    dve.wait_ge(s_tab, c - 1)
                dve.tensor_scalar(tA[p], iota[:, 0:P], k_t(lof), None, ALU.is_equal)
                dve.tensor_scalar(tB[p], iota[:, 0:NS], k_t(hif), k_t(tok[:, :, :]), ALU.is_equal, ALU.mult)\
                    .then_inc(s_hot, 1)
            onehots(0, 0, False)
            onehots(1, 1, False)
            with dve.Fori(1, NT) as j:
                onehots(j * 2, 0)
                onehots(j * 2 + 1, 1)
            dve.wait_ge(s_tab, 2 * NT)
            dve.tensor_copy(tab[:, :], ps[:, 2, 0:NS]).then_inc(s_tabi, 1)

            dve.sem_inc(s_hid, 2)
            def hidden(i, p, q):
                dve.wait_ge(s_h, i * 4 + 8 + 2 * q + 2)
                dve.wait_ge(s_g, i * 2 + q + 1)
                dve.wait_ge(s_o, i + 1)
                dve.tensor_tensor(hid[p][:, 2 * q:2 * q + 2, :], gate[q].rearrange("p (k s) -> p k s", k=2),
                                  ps[:, 2 + q, :].rearrange("p (k s) -> p k s", k=2), ALU.mult).then_inc(s_hid, 1)
            with dve.Fori(0, CAPB // 2) as j:
                for p in range(2):
                    for q in range(2):
                        hidden(j * 2 + p, p, q)

            dve.sem_inc(s_fin, 2)
            def combine(t, j, p):
                dve.wait_ge(s_yg[p], (j + 1) * 32)
                if t is not p:
                    dve.wait_ge(s_out[p], j * 16)
                dve.scalar_tensor_tensor(oo[p][:, 0, :], yg[p][:, 0, :], wts[:, 0, ds(t, 1)],
                                         x[:, ds(t, 1), :].rearrange("p a d -> p (a d)"), ALU.mult, ALU.add)\
                    .then_inc(s_x1, 1)
                dve.wait_ge(s_x1, t + NT + 3)
                dve.scalar_tensor_tensor(oo[p][:, 1, :], yg[p][:, 1, :], wts[:, 1, ds(t, 1)],
                                         oo[p][:, 0, :], ALU.mult, ALU.add).then_inc(s_fin, 1)
            in_pairs(dve, NT, combine, peeled=True)

        @block.tensor
        def _(pe):
            mm = pe.matmul
            pe.wait_ge(s_const, 1)
            pe.sem_inc(s_tp, 2)
            pe.sem_inc(s_kv, 2)
            pe.wait_ge(s_mv, 1)

            def transpose_xn(t, p, bank, ready, made, copied=None):
                pe.wait_ge(made, t + 1)
                if copied is not None:
                    pe.wait_ge(*copied)
                for c in range(DC):
                    last = pe.transpose(ps[:, bank + p, c * P:(c + 1) * P], xn[p][:, c * P:(c + 1) * P], ident[:, :])
                last.then_inc(ready, 1)

            def project(t, p):
                pe.wait_ge(s_xt, t + 1)
                pe.wait_ge(s_kvd, t + 1)
                for c in range(DC):
                    last = mm(ps[:, 2 + p, :], xt[p][:, c, :], wkv[:, c, :], start=c == 0, stop=c == DC - 1)
                last.then_inc(s_kv, 1)
            transpose_xn(0, 0, 0, s_tp, s_xn)
            transpose_xn(1, 1, 0, s_tp, s_xn)
            project(0, 0)
            with pe.Fori(1, NT // 2) as j:
                transpose_xn(j * 2, 0, 0, s_tp, s_xn, (s_xt, j * 2 - 1))
                project(j * 2 - 1, 1)
                transpose_xn(j * 2 + 1, 1, 0, s_tp, s_xn, (s_xt, j * 2))
                project(j * 2, 0)
            transpose_xn(NT - 1, 0, 0, s_tp, s_xn, (s_xt, NT - 2))
            project(NT - 2, 1)
            project(NT - 1, 0)

            pe.sem_inc(s_khp, 2)
            def sum_kv(t, p, start=False, stop=False):
                pe.wait_ge(s_kh, t + 1)
                for c in range(DC):
                    mm(ps[:, 4 + c, 0:P + 1], vhs[p][:, c * P:(c + 1) * P], khs[p][:, c, 0:P + 1], start=start, stop=stop)
                mm(ps[:, 6, 0:D].rearrange("p (c d) -> p c d", c=DC), ones[:, :], khs[p][:, :, 0:P],
                   start=start, stop=stop).then_inc(s_khp, 1)
            sum_kv(0, 0, start=True)
            sum_kv(1, 1)
            with pe.Fori(1, NT // 2) as j:
                sum_kv(j * 2, 0)
                sum_kv(j * 2 + 1, 1)
            sum_kv(NT - 1, 0, stop=True)
            pe.wait_ge(s_khp, NT + 2)
            pe.sem_inc(s_mx, 1)
            pe.wait_ge(s_mv, 2)
            for c in range(DC):
                last = mm(ps[:, 0, c * D:(c + 1) * D], kvt[:, c, :], woT[:, c, :], start=True, stop=True)
            last.then_inc(s_mx, 1)
            pe.wait_ge(s_mv, 3)
            for m in range(DC):
                for c in range(DC):
                    last = mm(ps[:, 1, m * D:(m + 1) * D], wq[:, c, m * P:(m + 1) * P], A1[:, c, :],
                              start=c == 0, stop=c == DC - 1)
            last.then_inc(s_mx, 1)
            pe.wait_ge(s_cov, 1)
            mm(ps[:, 7, 0:1], ones[:, :], v_a[:, 0:1], start=True, stop=True).then_inc(s_cov, 1)

            pe.sem_inc(s_w1, 4)
            pe.sem_inc(s_w2, 4)
            pe.sem_inc(s_sc, 2)
            pe.wait_ge(s_mv, 5)

            def edges(n0, h0, w_n):
                def up(i, j, p):
                    pe.wait_ge(s_rbf[p], (h0 + j + 1) * 16)
                    for m in range(DC):
                        pe.wait_ge(s_silu, (n0 + i) * 2 + m + 1)
                        mm(ps[:, m, :], W1[:, m * P:(m + 1) * P], rbf[p][:, :], start=True, stop=True).then_inc(s_w1, 1)

                def gates(i, p):
                    pe.wait_ge(s_silu, (n0 + i) * 2 + 4)
                    for s in range(ET):
                        if s % 2 == 0:
                            pe.wait_ge(s_zb, (n0 + i) * 2 + s // 2 + 1)
                        for c in range(DC):
                            last = mm(ps[:, 2 + s // 2, (s % 2) * D:(s % 2 + 1) * D], h1T[p][:, c, s * P:(s + 1) * P],
                                      W2[:, c, :], start=c == 0, stop=c == DC - 1)
                        if s % 2:
                            last.then_inc(s_w2, 1)

                def scatter(i, p):
                    pe.wait_ge(s_msg, n0 + i + 3)
                    pe.wait_ge(s_agg, n0 + i + 1)
                    for c in range(DC):
                        for s in range(ET):
                            last = mm(ps[:, 4 + p, c * w_n:(c + 1) * w_n], msg[p][:, s, c * P:(c + 1) * P],
                                      oh[p][:, s, 0:w_n], start=s == 0, stop=s == ET - 1)
                    last.then_inc(s_sc, 1)
                up(0, 0, 0)
                up(1, 0, 1)
                gates(0, 0)
                with pe.Fori(1, NG // 2) as j:
                    up(j * 2, j, 0)
                    gates(j * 2 - 1, 1)
                    scatter(j * 2 - 2, 0)
                    up(j * 2 + 1, j, 1)
                    gates(j * 2, 0)
                    scatter(j * 2 - 1, 1)
                gates(NG - 1, 1)
                scatter(NG - 2, 0)
                scatter(NG - 1, 1)
            edges(0, 0, W)
            pe.wait_ge(s_flag, 1)
            left = pe.value_load(flag[0:1, 0:1], min_val=0, max_val=E)
            with pe.If(left > 0):
                with pe.Fori(0, NW) as w:
                    edges((w + 1) * NG, (w + 1) * (NG // 2), FW)

            pe.sem_inc(s_uo, 2)
            pe.wait_ge(s_gnn, 1)
            pe.wait_ge(s_xnT, NT + 2)
            def node_up(t, p):
                pe.wait_ge(s_us, t + 1)
                for m in range(DC):
                    for k in range(2 * DC):
                        src = (xnT if k < DC else agg)[:, k % DC, ds(t * P, P)]
                        last = mm(ps[:, p, m * P:(m + 1) * P], U1[:, k, m * P:(m + 1) * P], src,
                                  start=k == 0, stop=k == 2 * DC - 1)
                last.then_inc(s_u1, 1)

            def node_down(t, p):
                pe.wait_ge(s_us, t + 3)
                pe.wait_ge(s_xnc, t + 1)
                for k in range(2 * DC):
                    lhs, rhs = (sst[p][:, k, :], U2[:, k, :]) if k < DC else (xt[p][:, k - DC, :], M[:, k - DC, :])
                    last = mm(ps[:, 2 + p, 0:D], lhs, rhs, start=k == 0, stop=k == 2 * DC - 1)
                last.then_inc(s_uo, 1)
            node_up(0, 0)
            node_up(1, 1)
            node_down(0, 0)
            with pe.Fori(1, NT // 2) as j:
                node_up(j * 2, 0)
                pe.wait_ge(s_x1, j * 2)
                node_down(j * 2 - 1, 1)
                node_up(j * 2 + 1, 1)
                pe.wait_ge(s_x1, j * 2 + 1)
                node_down(j * 2, 0)
            node_up(NT - 1, 0)
            pe.wait_ge(s_x1, NT - 1)
            node_down(NT - 2, 1)
            pe.wait_ge(s_x1, NT)
            node_down(NT - 1, 0)

            pe.sem_inc(s_tp2, 2)
            pe.sem_inc(s_lg, 2)
            def gate_logits(t, p):
                pe.wait_ge(s_xt2, t + 1)
                pe.wait_ge(s_lgc, t + 1)
                for c in range(DC):
                    last = mm(ps[:, 6 + p, 0:NX], xt[p][:, c, :], gw[:, c, :], start=c == 0, stop=c == DC - 1)
                last.then_inc(s_lg, 1)
            transpose_xn(0, 0, 4, s_tp2, s_xn2)
            transpose_xn(1, 1, 4, s_tp2, s_xn2)
            gate_logits(0, 0)
            with pe.Fori(1, NT // 2) as j:
                transpose_xn(j * 2, 0, 4, s_tp2, s_xn2, (s_xt2, j * 2 - 1))
                gate_logits(j * 2 - 1, 1)
                transpose_xn(j * 2 + 1, 1, 4, s_tp2, s_xn2, (s_xt2, j * 2))
                gate_logits(j * 2, 0)
            transpose_xn(NT - 1, 0, 4, s_tp2, s_xn2, (s_xt2, NT - 2))
            gate_logits(NT - 2, 1)
            gate_logits(NT - 1, 0)

            pe.wait_ge(s_m12, 1)
            mf = m12.rearrange("p t e -> p (t e)")
            mm(ps[:, 0, 0:TX], before[:, :], mf, start=True, stop=True)
            mm(ps[:, 1, 0:TX], ones[:, :], mf, start=True, stop=True).then_inc(s_cnt, 1)

            def place(c, p, start=False, stop=False):
                pe.wait_ge(s_hot, c + 1)
                mm(ps[:, 2, 0:NS], tA[p], tB[p], start=start, stop=stop).then_inc(s_tab, 1)
            place(0, 0, start=True)
            place(1, 1)
            with pe.Fori(1, NT - 1) as j:
                place(j * 2, 0)
                place(j * 2 + 1, 1)
            place(2 * NT - 2, 0)
            place(2 * NT - 1, 1, stop=True)

            pe.sem_inc(s_xsp, 2)
            pe.sem_inc(s_h, 8)
            pe.sem_inc(s_o, 2)
            pe.wait_ge(s_tabi, 1)
            def turn(i, j, p):
                pe.wait_ge(s_xs[p], (j + 1) * 32)
                pe.wait_ge(s_xsT, i + 1)
                for s in range(2):
                    for c in range(DC):
                        last = pe.transpose(ps[:, 7, c * SB + s * P:c * SB + (s + 1) * P],
                                            xs[p][:, s, c * P:(c + 1) * P], ident[:, :])
                last.then_inc(s_xsp, 1)

            def expert_up(i, j, p, q):
                if q == 0:
                    pe.wait_ge(s_w12[p], (j + 1) * 32)
                    pe.wait_ge(s_xsT, i + 2)
                pe.wait_ge(s_hid, i * 2 + q + 1)
                for m in range(2):
                    for k in range(2):
                        h = (2 * q + k) * P
                        for c in range(DC):
                            last = mm(ps[:, 2 * m + q, k * SB:(k + 1) * SB], w12[p][:, m, c, h:h + P],
                                      xsT[p][:, c, :], start=c == 0, stop=c == DC - 1)
                    last.then_inc(s_h, 1)

            def expert_down(i, j, p):
                pe.wait_ge(s_w3[p], (j + 1) * 16)
                pe.wait_ge(s_hid, i * 2 + 4)
                pe.wait_ge(s_y, i + 1)
                for s in range(2):
                    for k in range(HC):
                        last = mm(ps[:, 4 + p, s * D:(s + 1) * D], hid[p][:, k, s * P:(s + 1) * P], w3[p][:, k, :],
                                  start=k == 0, stop=k == HC - 1)
                last.then_inc(s_o, 1)
            turn(0, 0, 0)
            expert_up(0, 0, 0, 0)
            turn(1, 0, 1)
            expert_up(0, 0, 0, 1)
            with pe.Fori(0, CAPB // 2 - 1) as j:
                expert_up(j * 2 + 1, j, 1, 0)
                turn(j * 2 + 2, j + 1, 0)
                expert_down(j * 2, j, 0)
                expert_up(j * 2 + 1, j, 1, 1)
                expert_up(j * 2 + 2, j + 1, 0, 0)
                turn(j * 2 + 3, j + 1, 1)
                expert_down(j * 2 + 1, j, 1)
                expert_up(j * 2 + 2, j + 1, 0, 1)
            expert_up(CAPB - 1, CAPB // 2 - 1, 1, 0)
            expert_down(CAPB - 2, CAPB // 2 - 1, 0)
            expert_up(CAPB - 1, CAPB // 2 - 1, 1, 1)
            expert_down(CAPB - 1, CAPB // 2 - 1, 1)


def kernel(x, src, dst, edge_attr_64, L0_gnn_W1, L0_gnn_b1, L0_gnn_W2, L0_gnn_b2, L0_gnn_U1, L0_gnn_c1,
           L0_gnn_U2, L0_gnn_c2, L0_mix_wq, L0_mix_wk, L0_mix_wv, L0_mix_wo, L0_mix_bo, L0_mix_ln_k_g,
           L0_mix_ln_k_b, L0_mix_ln_v_g, L0_mix_ln_v_b, L0_ffn_gate_w, L0_ffn_gate_b, L0_ffn_w1,
           L0_ffn_w2, L0_ffn_w3):
    import numpy as np
    import concourse.bacc as bacc
    from concourse.bass_utils import run_bass_kernel_spmd

    def edge_columns(a, fill):
        a = np.pad(np.asarray(a), (0, EP - E), constant_values=fill)
        return np.ascontiguousarray(a.reshape(NG * ET, P).T)

    rbf = np.pad(np.asarray(edge_attr_64), ((0, EP - E), (0, 0)))
    arrays = {
        "x": x,
        "src": edge_columns(src, 0),
        "dst": edge_columns(dst, FAR),
        "first": np.asarray(dst)[::EG].reshape(1, NG),
        "rbf": rbf.reshape(NG, EG, RB).transpose(0, 2, 1),
        "W1": L0_gnn_W1, "b1": np.asarray(L0_gnn_b1).reshape(DC, P).T, "W2": L0_gnn_W2, "b2": L0_gnn_b2,
        "U1": L0_gnn_U1, "c1": np.asarray(L0_gnn_c1).reshape(DC, P).T, "U2": L0_gnn_U2, "c2": L0_gnn_c2,
        "wq": L0_mix_wq,
        "wkvT": np.concatenate([np.asarray(L0_mix_wk).T, np.asarray(L0_mix_wv).T], axis=1),
        "woT": np.asarray(L0_mix_wo).T, "bo": L0_mix_bo,
        "kg": L0_mix_ln_k_g, "kb": L0_mix_ln_k_b, "vg": L0_mix_ln_v_g, "vb": L0_mix_ln_v_b,
        "gw": L0_ffn_gate_w, "gb": L0_ffn_gate_b, "w1": L0_ffn_w1, "w2": L0_ffn_w2, "w3": L0_ffn_w3,
    }
    arrays = {"in_" + k: np.ascontiguousarray(v) for k, v in arrays.items()}
    nc = bacc.Bacc("TRN2", target_bir_lowering=False, num_devices=1)
    args = [nc.dram_tensor(k, v.shape, mybir.dt.from_np(v.dtype), kind="ExternalInput").ap()
            for k, v in arrays.items()]
    out = nc.dram_tensor("out", (N, D), f32, kind="ExternalOutput").ap()
    gps_layer(nc, *args, out)
    r = run_bass_kernel_spmd(nc, [arrays], core_ids=[0])
    return r.results[0]["out"]
```

```python
import concourse.bass as bass
import concourse.mybir as mybir
from contextlib import ExitStack

f32 = mybir.dt.float32
f32r = mybir.dt.float32r
i32 = mybir.dt.int32
ALU = mybir.AluOpType
ACT = mybir.ActivationFunctionType
X = mybir.AxisListType.X

P = 128
N, D, E, RB = 3125, 256, 50000, 64
DC = D // P
NT = -(-N // P)
NP = NT * P
LAST = N - (NT - 1) * P
EG = 512
ET = EG // P
NG = -(-E // EG)
EP = NG * EG
W = 96
FW = 2 * W
NW = -(-NP // FW)
AW = NW * FW
FAR = 1 << 20
HEADS, HD = 4, 64
NX, HF = 16, 512
HC = HF // P
SB = 256
CAPB = (2 * N - NX) // SB + NX
CAPB += CAPB % 2
LOWP = (2 * N - 1) // (2 * SB)
NS = CAPB * SB // P
PK = 4096
PARTS = ((0, 0), (0, 1), (1, 0))
EPS = 1e-5
MAGIC = 1597463007.0


def ds(start, size):
    return bass.ds(start, size)


def in_pairs(eng, n, body, peeled=False):
    if peeled:
        body(0, 0, 0)
        body(1, 0, 1)
    with eng.Fori(int(peeled), n // 2) as j:
        body(j * 2, j, 0)
        body(j * 2 + 1, j, 1)
    if n % 2:
        body(n - 1, n // 2, 0)


def last_pair(eng, lastp):
    return eng.value_load(lastp[0:1, 0:1], min_val=LOWP - 1, max_val=CAPB // 2 - 2) + 1


def gps_layer(nc, x_d, src_d, dst_d, first_d, rbf_d, W1_d, b1_d, W2_d, b2_d, U1_d, c1_d, U2_d, c2_d,
              wq_d, wkvT_d, woT_d, bo_d, kg_d, kb_d, vg_d, vb_d, gw_d, gb_d, w1_d, w2_d, w3_d, out_d):
    xn_d = nc.dram_tensor("xn_rows", (NP, D), f32).ap()
    xn2_d = nc.dram_tensor("xn2_rows", (NP, D), f32).ap()
    y_d = nc.dram_tensor("expert_rows", (2 * NP + CAPB * SB, D), f32).ap()

    ctx = ExitStack()
    with ctx:
        def sb(name, shape, dt=f32):
            return ctx.enter_context(nc.sbuf_tensor(name, shape, dt))

        def sem(name):
            return ctx.enter_context(nc.semaphore(name))

        ident = sb("ident", [P, P])
        ones = sb("ones", [P, P])
        before = sb("before", [P, P])
        iota = sb("iota", [P, FW])
        slot = sb("slot", [P, NS])
        valid = sb("valid", [P, 1])
        tok = sb("tok", [P, 2, NT])
        W1 = sb("W1", [P, D])
        b1 = sb("b1", [P, DC])
        W2 = sb("W2", [P, DC, D])
        b2bc = sb("b2bc", [P, 2, D])
        U1 = sb("U1", [P, 2 * DC, D])
        c1 = sb("c1", [P, DC])
        U2 = sb("U2", [P, DC, D])
        cb = sb("cb", [P, 2, D])
        wq = sb("wq", [P, DC, D])
        wkv = sb("wkv", [P, DC, 2 * D])
        woT = sb("woT", [P, DC, D])
        kgb = sb("kgb", [P, 2, P])
        vgb = sb("vgb", [P, 2])
        gw = sb("gw", [P, DC, NX])
        gb = sb("gb", [P, NX])
        x = sb("x_nodes", [P, NT, D])
        xnT = sb("xnT", [P, DC, NP])
        xn = [sb(f"xn{i}", [P, D]) for i in range(2)]
        xt = [sb(f"xt{i}", [P, DC, P]) for i in range(2)]
        st6 = sb("st6", [P, NT, 6])
        mean = sb("mean", [P, NT])
        rstd = sb("rstd", [P, NT])
        v_a = sb("v_a", [P, NT * 8])
        v_b = sb("v_b", [P, NT * 8])
        v_c = sb("v_c", [P, NT * 8])
        ssq = sb("ssq", [P, NT * 8])
        kvr = sb("kvr", [P, NT * 8])
        M = wkv[:, :, 0:D]
        big = sb("big", [P, NT * 2 * D])

        def part(mem, at, *shape):
            size = 1
            for n in shape:
                size *= n
            ap = mem[:, at:at + size]
            if len(shape) == 3:
                return ap.rearrange("p (a b c) -> p a b c", a=shape[0], b=shape[1])
            return ap if len(shape) == 1 else ap.rearrange("p (a b) -> p a b", a=shape[0])
        kvc = part(big, 0, NT, 2 * D)
        agg = part(big, 0, DC, AW)
        EV = DC * AW
        th = [part(big, EV + ET * D * i, ET, D) for i in range(2)]
        hg = [part(big, EV + ET * D * (2 + i), ET, D) for i in range(2)]
        msg = [part(big, EV + ET * D * (4 + i), ET, D) for i in range(2)]
        fr = sb("fr", [P, 12 * 1024], f32r)
        h1s = [[part(fr, EG * DC * (2 * i + k), DC, EG) for k in range(2)] for i in range(2)]
        rbs = [part(fr, 4096 + EG * i, EG) for i in range(2)]
        W1s = [part(fr, 5120 + D * k, D) for k in range(2)]
        W2s = [part(fr, 5632 + DC * D * k, DC, D) for k in range(2)]
        ws = [[part(fr, 1024 * (2 * r + k), 4, D) for k in range(2)] for r in range(3)]
        xTs = [[part(fr, 6144 + 512 * (2 * i + k), DC, SB) for k in range(2)] for i in range(2)]
        hids = [[part(fr, 8192 + HC * SB * (2 * i + k), HC, SB) for k in range(2)] for i in range(2)]
        srcs = sb("srcs", [P, NG * ET], i32)
        dstf = sb("dstf", [P, NG * ET])
        rel = sb("rel", [P, NG * ET])
        dsti = rel[:, :].bitcast(i32)
        basef = sb("basef", [P, NG])
        basei = sb("basei", [P, NG], i32)
        flag = sb("flag", [P, 1], i32)
        cover = part(big, EV, NG * ET)
        rbf = [sb(f"rbf{i}", [P, EG]) for i in range(2)]
        h1f = sb("h1f", [P, DC, EG])
        oh = [sb(f"oh{i}", [P, ET, FW]) for i in range(2)]
        idx = [sb(f"idx{i}", [P, ET], i32) for i in range(2)]

        sq = [h1f[:, i, :] for i in range(2)]
        oflat = [oh[i][:, :, :].rearrange("p s w -> p (s w)") for i in range(2)]
        khs = [oflat[i][:, 0:2 * (P + 2)].rearrange("p (j c) -> p j c", j=2) for i in range(2)]
        vhs = [oflat[i][:, 2 * (P + 2):2 * (P + 2) + D] for i in range(2)]
        hflat = h1f[:, :, :].rearrange("p c e -> p (c e)")
        kvt = part(hflat, 0, DC, P)
        kv_t = part(hflat, 256, P)
        kv_r = part(hflat, 384, P)
        A1 = part(hflat, 512, DC, D)
        kv_s = v_b[:, 0:1]
        sst = [part(hflat, 256 * i, DC, P) for i in range(2)]
        TX = NT * NX
        lg = part(big, EV, NT, NX)
        ohx = [part(big, EV + TX * (1 + k), NT, NX) for k in range(2)]
        m12 = part(big, EV + TX * 3, NT, NX)
        t_a = part(big, EV + TX * 4, NT, NX)
        t_b = part(big, EV + TX * 5, NT, NX)
        t_et = part(big, EV + TX * 6, NX, NT)
        t_in = part(big, EV + TX * 7, NX, NT)
        t_ex = part(big, EV + TX * 8, NX, NT)
        top = part(big, EV + TX * 9, 2, NT)
        n_e = part(big, EV + TX * 9 + 64, NX)
        c_e = part(big, EV + TX * 9 + 80, NX)
        cend = part(big, EV + TX * 9 + 96, NX)
        off = part(big, EV + TX * 9 + 112, NX)
        c_i = sb("c_i", [P, NX], i32)
        texp_f = part(big, EV + TX * 9 + 128, CAPB)
        tcmp = part(big, EV + TX * 10, CAPB, NX)
        onerow = part(big, EV + TX * 10 + CAPB * NX, TX)
        texp = sb("texp", [P, CAPB], i32)
        lastp = sb("lastp", [P, 1], i32)
        posf = part(big, EV + TX * 6 + 0, 2, NT)
        posi = sb("posi", [P, 2, NT], i32)
        bits = part(big, EV + TX * 6 + 64, 2, NT).bitcast(i32)
        lof = part(big, EV + TX * 6 + 128, 2, NT)
        hif = part(big, EV + TX * 6 + 192, 2, NT)
        wts = sb("wts", [P, 2, NT])
        exw = sb("exw", [P, NT])
        tA = [oh[i][:, 0, 0:P] for i in range(2)]
        tB = [oh[i][:, 1, 0:NS] for i in range(2)]
        tab = sb("tab", [P, NS], i32)
        dest = sb("dest", [P, NS], i32)
        tf = [part(big, EV + TX * 3 + 128 * i, NS) for i in range(3)]
        wst = [[part(big, 1024 * (2 * r + i), 4, D) for i in range(2)] for r in range(3)]
        xfl = xnT[:, :, :].rearrange("p c n -> p (c n)")
        xs = [part(xfl, 512 * i, 2, D) for i in range(2)]
        gate = [part(xfl, 1024 + 512 * i, 512) for i in range(2)]
        hidf = [part(xfl, 2048 + 512 * i, 2, SB) for i in range(2)]
        ys = [part(xfl, 3072 + 512 * i, 2, D) for i in range(2)]
        yg = [part(xfl, 4096 + 512 * i, 2, D) for i in range(2)]
        oo = [part(xfl, 5120 + 512 * i, 2, D) for i in range(2)]

        ps = ctx.enter_context(nc.psum_tensor("ps", [P, 8, 512], f32))

        s_par = sem("params_in")
        s_x = [sem(f"x_in{i}") for i in range(3)]
        s_edge = sem("edge_tables_in")
        s_const = sem("constants_made")
        s_pc = sem("pool_steps")
        s_xpad = sem("x_padding_zeroed")
        s_dve = sem("vector_steps")
        s_xn = sem("xn_made")
        s_xnst = [sem(f"xn_stored{i}") for i in range(2)]
        s_tp = sem("xn_transposed")
        s_xt = sem("xt_copied")
        s_xnT = sem("xnT_kept")
        s_kv = sem("kv_projected")
        s_kvd = sem("kv_drained")
        s_sq = sem("squares_summed")
        s_kh = sem("kv_scaled")
        s_khp = sem("kv_summed")
        s_mx = sem("mix_products")
        s_mv = sem("mix_vector")
        s_rbf = [sem(f"rbf_in{i}") for i in range(2)]
        s_whi = sem("edge_weights_high")
        s_wlow = sem("edge_weights_low")
        s_rhi = sem("rbf_high")
        s_rlo = sem("rbf_low")
        s_hhi = sem("edge_hidden_high")
        s_hlo = sem("edge_hidden_low")
        s_w1 = sem("edge_w1_done")
        s_silu = sem("edge_silu_done")
        s_w2 = sem("edge_w2_done")
        s_zb = sem("edge_bias_added")
        s_th = sem("edge_tanh_done")
        s_idx = sem("src_indices_staged")
        s_hg = [sem(f"src_rows_in{i}") for i in range(2)]
        s_msg = sem("messages_made")
        s_sc = sem("messages_scattered")
        s_agg = sem("window_added")
        s_cov = sem("uncovered_counted")
        s_flag = sem("flag_ready")
        s_gnn = sem("aggregate_done")
        s_xcb = sem("x_plus_biases")
        s_xnc = sem("xn_tile_staged")
        s_u1 = sem("u1_done")
        s_us = sem("u1_silu_done")
        s_uo = sem("u2_done")
        s_x1 = sem("x1_made")
        s_xn2 = sem("xn2_made")
        s_xn2st = [sem(f"xn2_stored{i}") for i in range(2)]
        s_tp2 = sem("xn2_transposed")
        s_xt2 = sem("xt2_copied")
        s_lg = sem("logits_done")
        s_lgc = sem("logits_copied")
        s_m12 = sem("choices_made")
        s_cnt = sem("choices_counted")
        s_dif = sem("logit_gap_made")
        s_ex = sem("gap_exp_done")
        s_hot = sem("slot_onehots_made")
        s_tab = sem("slot_table_done")
        s_tabi = sem("slot_table_kept")
        s_texp = sem("block_experts_ready")
        s_win = [[sem(f"w_in{r}{i}") for i in range(2)] for r in range(3)]
        s_wh = [sem(f"w_high{r}") for r in range(3)]
        s_wlo = [sem(f"w_low{r}") for r in range(3)]
        s_sidx = sem("slot_indices_staged")
        s_xs = [sem(f"slot_rows_in{i}") for i in range(2)]
        s_xsp = sem("slots_transposed")
        s_xhi = sem("slots_high")
        s_xlo = sem("slots_low")
        s_hdh = sem("expert_hidden_high")
        s_hdl = sem("expert_hidden_low")
        s_didx = sem("slot_rows_staged")
        s_h = sem("expert_up_done")
        s_g = sem("expert_silu_done")
        s_hid = sem("expert_hidden_made")
        s_o = sem("expert_down_done")
        s_y = sem("expert_out_copied")
        s_yst = [sem(f"expert_rows_stored{i}") for i in range(2)]
        s_yg = [sem(f"pair_rows_in{i}") for i in range(2)]
        s_fin = sem("out_made")
        s_out = [sem(f"out_stored{i}") for i in range(2)]

        block = ctx.enter_context(nc.Block())
        NPAR = 23

        @block.sync
        def _(sp):
            sp.dma_start(x[:, 0:12, :], x_d[0:12 * P, :].rearrange("(t p) d -> p t d", p=P)).then_inc(s_x[0], 16)
            sp.dma_start(x[:, 12:24, :], x_d[12 * P:24 * P, :].rearrange("(t p) d -> p t d", p=P)).then_inc(s_x[1], 16)
            sp.wait_ge(s_xpad, 1)
            sp.dma_start(x[0:LAST, NT - 1, :], x_d[(NT - 1) * P:N, :]).then_inc(s_x[2], 16)
            sp.dma_start(dsti, dst_d).then_inc(s_edge, 16)
            sp.dma_start(srcs[:, :], src_d).then_inc(s_edge, 16)
            sp.dma_start(basei[:, :], first_d.to_broadcast([P, NG])).then_inc(s_edge, 16)

            def store_xn(t, j, p):
                sp.wait_ge(s_xn, t + 1)
                sp.dma_start(xn_d[ds(t * P, P), :], xn[p][:, :]).then_inc(s_xnst[p], 16)
            in_pairs(sp, NT, store_xn)

            def edges(n0, h0):
                def load(i, j, p):
                    sp.wait_ge(s_rlo, n0 + i + 1)
                    for half in range(2):
                        sp.dma_start(rbf[p][half * RB:(half + 1) * RB, :],
                                     rbf_d[ds(i, 1), :, :].rearrange("a r e -> (a r) e")).then_inc(s_rbf[p], 16)
                in_pairs(sp, NG, load)
            edges(0, 0)
            sp.wait_ge(s_flag, 1)
            left = sp.value_load(flag[0:1, 0:1], min_val=0, max_val=E)
            with sp.If(left > 0):
                with sp.Fori(0, NW) as w:
                    edges((w + 1) * NG, (w + 1) * (NG // 2))

            def store_xn2(t, j, p):
                sp.wait_ge(s_xn2, t + 1)
                sp.dma_start(xn2_d[ds(t * P, P), :], xn[p][:, :]).then_inc(s_xn2st[p], 16)
            in_pairs(sp, NT, store_xn2)

            sp.wait_ge(s_texp, 1)
            def load_w(i, p, first=False):
                e = sp.value_load(texp[0:1, ds(i, 1)], min_val=0, max_val=NX - 1)
                for r in range(3):
                    if not first:
                        sp.wait_ge(s_wlo[r], i - 1)
                    if r < 2:
                        for m, w_d in enumerate((w1_d, w2_d)):
                            sp.dma_start(wst[r][p][:, 2 * m:2 * m + 2, :],
                                         w_d[ds(e, 1), :, r * SB:(r + 1) * SB].rearrange("e (c p) h -> p (e c) h", p=P))\
                                .then_inc(s_win[r][p], 16)
                    else:
                        sp.dma_start(wst[r][p], w3_d[ds(e, 1), :, :].rearrange("e (c p) h -> p (e c) h", p=P))\
                            .then_inc(s_win[r][p], 16)
            load_w(0, 0, True)
            load_w(1, 1, True)
            end = last_pair(sp, lastp)
            with sp.Fori(1, CAPB // 2) as j:
                with sp.If(end > j - 1):
                    load_w(j * 2, 0)
                    load_w(j * 2 + 1, 1)

            for p in range(2):
                sp.wait_ge(s_yst[p], 32 * end + 32)
            y_rows = y_d[0:2 * NP, :].rearrange("(k n) d -> n k d", k=2)
            def load_y(t, p, rows=P):
                sp.dma_start(yg[p][0:rows, :, :], y_rows[ds(t * P, rows), :, :]).then_inc(s_yg[p], 16)
            load_y(0, 0)
            load_y(1, 1)
            def store_out(t, j, p, rows=P):
                sp.wait_ge(s_fin, t + 3)
                sp.dma_start(out_d[ds(t * P, rows), :], oo[p][0:rows, 1, :]).then_inc(s_out[p], 16)
            with sp.Fori(0, NT // 2 - 1) as j:
                store_out(j * 2, j, 0)
                load_y(j * 2 + 2, 0)
                store_out(j * 2 + 1, j, 1)
                load_y(j * 2 + 3, 1)
            store_out(NT - 3, NT // 2 - 1, 0)
            load_y(NT - 1, 0, LAST)
            store_out(NT - 2, NT // 2 - 1, 1)
            store_out(NT - 1, NT // 2, 0, LAST)
            for p in range(2):
                sp.wait_ge(s_out[p], 16 * ((NT + 1 - p) // 2))

        @block.gpsimd
        def _(pool):
            steps = [0]

            def link(ins):
                steps[0] += 1
                ins.then_inc(s_pc, 1)
                pool.wait_ge(s_pc, steps[0])

            pool.memset(x[:, NT - 1, :], 0.0).then_inc(s_xpad, 1)
            link(pool.memset(ident[:, :], 0.0))
            link(pool.affine_select(out=ident[:, :], in_=ident[:, :], compare_op=ALU.not_equal, fill=1.0,
                                    base=0, pattern=[[-1, P]], channel_multiplier=1))
            link(pool.memset(ones[:, :], 1.0))
            link(pool.affine_select(out=before[:, :], in_=ones[:, :], compare_op=ALU.is_gt, fill=0.0,
                                    base=0, pattern=[[1, P]], channel_multiplier=-1))
            link(pool.iota(iota[:, :], [[1, FW]], base=0, channel_multiplier=0,
                           allow_small_or_imprecise_dtypes=True))
            link(pool.iota(tok[:, :, :], [[PK, 2], [P, NT]], base=1, channel_multiplier=1,
                           allow_small_or_imprecise_dtypes=True))
            link(pool.affine_select(out=tok[:, :, :], in_=tok[:, :, :], compare_op=ALU.is_gt, fill=0.0,
                                    base=N, pattern=[[0, 2], [-P, NT]], channel_multiplier=-1))
            link(pool.affine_select(out=valid[:, :], in_=ones[:, 0:1], compare_op=ALU.is_gt, fill=0.0,
                                    base=LAST, pattern=[[0, 1]], channel_multiplier=-1))
            for p in range(2):
                link(pool.memset(khs[p][:, :, P:P + 2], 1.0))
            link(pool.iota(slot[:, :], [[P, NS]], base=2 * NP, channel_multiplier=1,
                           allow_small_or_imprecise_dtypes=True))
            pool.sem_inc(s_const, 1)

            pool.sem_inc(s_xnT, 2)
            def keep(t, j, p):
                pool.wait_ge(s_xt, t + 1)
                pool.tensor_copy(xnT[:, :, ds(t * P, P)], xt[p][:, :, :]).then_inc(s_xnT, 1)
            in_pairs(pool, NT, keep)

            pool.wait_ge(s_par, 16 * NPAR)
            pool.wait_ge(s_xn, NT)
            link(pool.tensor_tensor(cb[:, 0, :], cb[:, 0, :], cb[:, 1, :], ALU.add))
            def biased(t, j, p):
                pool.tensor_tensor(x[:, ds(t, 1), :], x[:, ds(t, 1), :], cb[:, 0:1, :], ALU.add).then_inc(s_xcb, 1)
            in_pairs(pool, NT, biased)

            for p in range(2):
                pool.wait_ge(s_xnst[p], 16 * ((NT + 1 - p) // 2))
            pool.wait_ge(s_edge, 48)

            def edges(n0, h0):
                def gather(i, j, p):
                    pool.wait_ge(s_msg, n0 + i + 1)
                    pool.tensor_copy(idx[p][:, :], srcs[:, ds(i * ET, ET)]).then_inc(s_idx, 1)
                    pool.wait_ge(s_edge, 64)
                    pool.wait_ge(s_idx, n0 + i + 1)
                    for s in range(ET):
                        pool.indirect_dma_start(hg[p][:, s, :], None, xn_d[:, :],
                                                bass.IndirectOffsetOnAxis(idx[p][:, s:s + 1], 0))\
                            .then_inc(s_hg[p], 16)
                in_pairs(pool, NG, gather)
            pool.wait_ge(s_mv, 2)
            edges(0, 0)
            pool.wait_ge(s_flag, 1)
            left = pool.value_load(flag[0:1, 0:1], min_val=0, max_val=E)
            with pool.If(left > 0):
                with pool.Fori(0, NW) as w:
                    edges((w + 1) * NG, (w + 1) * (NG // 2))

            def stage(t, j, p):
                pool.wait_ge(s_uo, t + 1)
                pool.tensor_copy(xt[p][:, :, :], xnT[:, :, ds(t * P, P)]).then_inc(s_xnc, 1)
            in_pairs(pool, NT, stage)

            for p in range(2):
                pool.wait_ge(s_xn2st[p], 16 * ((NT + 1 - p) // 2))
            pool.wait_ge(s_tabi, 1)
            def gather_slots(i, p):
                pool.wait_ge(s_xsp, i + 1)
                pool.tensor_copy(idx[p][:, 0:2], tab[:, ds(i * 2, 2)]).then_inc(s_sidx, 1)
                pool.wait_ge(s_tabi, 1)
                pool.wait_ge(s_sidx, i + 1)
                for s in range(2):
                    pool.indirect_dma_start(xs[p][:, s, :], None, xn2_d[:, :],
                                            bass.IndirectOffsetOnAxis(idx[p][:, s:s + 1], 0))\
                        .then_inc(s_xs[p], 16)

            def scatter_slots(i, p):
                pool.wait_ge(s_y, i + 3)
                pool.tensor_copy(idx[p][:, 2:4], dest[:, ds(i * 2, 2)]).then_inc(s_didx, 1)
                pool.wait_ge(s_tabi, 1)
                pool.wait_ge(s_didx, i + 3)
                for s in range(2):
                    pool.indirect_dma_start(y_d[:, :], bass.IndirectOffsetOnAxis(idx[p][:, 2 + s:3 + s], 0),
                                            ys[p][:, s, :], None).then_inc(s_yst[p], 16)
            pool.sem_inc(s_didx, 2)
            for i in range(4):
                gather_slots(i, i % 2)
            pool.wait_ge(s_texp, 1)
            end = last_pair(pool, lastp)
            with pool.Fori(2, CAPB // 2) as j:
                with pool.If(end > j - 1):
                    gather_slots(j * 2, 0)
                    scatter_slots(j * 2 - 4, 0)
                    gather_slots(j * 2 + 1, 1)
                    scatter_slots(j * 2 - 3, 1)
            for i in range(4):
                scatter_slots(end * 2 - 2 + i, i % 2)

        @block.scalar
        def _(act):
            def row(ap, n, parts=P):
                return ap.rearrange("(a n) -> a n", a=1).to_broadcast([parts, n])

            for dst, src in (
                (wkv[:, :, :], wkvT_d.rearrange("(c p) n -> p c n", p=P)),
                (W1[0:RB, :], W1_d), (W1[RB:P, :], W1_d), (W2[:, :, :], W2_d.rearrange("(c p) n -> p c n", p=P)),
                (b1[:, :], b1_d),
                (c1[:, :], c1_d),
                (b2bc[:, 0, :], row(b2_d, D)), (b2bc[:, 1, :], row(b2_d, D)),
                (U1[:, :, :], U1_d.rearrange("(c p) n -> p c n", p=P)),
                (U2[:, :, :], U2_d.rearrange("(c p) n -> p c n", p=P)),
                (wq[:, :, :], wq_d.rearrange("(c p) n -> p c n", p=P)),
                (woT[:, :, :], woT_d.rearrange("(c p) n -> p c n", p=P)),
                (cb[:, 0, :], row(c2_d, D)), (cb[:, 1, :], row(bo_d, D)),
                (kgb[:, 0, 0:HD], row(kg_d, HD)), (kgb[:, 0, HD:P], row(kg_d, HD)),
                (kgb[:, 1, 0:HD], row(kb_d, HD)), (kgb[:, 1, HD:P], row(kb_d, HD)),
                (vgb[0:HD, 0:1], vg_d.rearrange("(n a) -> n a", a=1)),
                (vgb[HD:P, 0:1], vg_d.rearrange("(n a) -> n a", a=1)),
                (vgb[0:HD, 1:2], vb_d.rearrange("(n a) -> n a", a=1)),
                (vgb[HD:P, 1:2], vb_d.rearrange("(n a) -> n a", a=1)),
                (gw[:, :, :], gw_d.rearrange("(c p) n -> p c n", p=P)),
            ):
                act.dma_start(dst, src).then_inc(s_par, 16)
            act.dma_start(gb[:, :], row(gb_d, NX)).then_inc(s_edge, 16)
            act.wait_ge(s_par, 16 * NPAR)

            act.sem_inc(s_kvd, 2)
            def copy_xt(t, p):
                act.wait_ge(s_tp, t + 3)
                act.wait_ge(s_xnT, t + 1)
                act.wait_ge(s_kv, t + 1)
                act.copy(xt[p][:, :, :], ps[:, p, 0:D].rearrange("p (c q) -> p c q", c=DC)).then_inc(s_xt, 1)

            def drain_kv(t, j, p):
                act.wait_ge(s_kv, t + 3)
                act.copy(kvc[:, ds(t, 1), :].rearrange("p a c -> p (a c)"), ps[:, 2 + p, :])
                act.wait_ge(s_sq, t + 1)
                act.activation(sq[p], ps[:, 2 + p, :], ACT.Square).then_inc(s_kvd, 1)
            copy_xt(0, 0)
            with act.Fori(0, NT // 2) as j:
                copy_xt(j * 2 + 1, 1)
                drain_kv(j * 2, j, 0)
                copy_xt(j * 2 + 2, 0)
                drain_kv(j * 2 + 1, j, 1)
            drain_kv(NT - 1, NT // 2, 0)

            for k, (dst, src) in enumerate(((W1s[0], W1[:, :]), (W2s[0], W2[:, :, :]))):
                act.copy(dst, src).then_inc(s_whi, 1)
            act.sem_inc(s_silu, 4)
            act.wait_ge(s_mv, 5)
            def edges(n0, h0):
                def rbf_high(i, j, p):
                    act.wait_ge(s_rbf[p], (h0 + j + 1) * 32)
                    act.wait_ge(s_w1, (n0 + i) * 2 + 2)
                    act.copy(rbs[p], rbf[p][:, :]).then_inc(s_rhi, 1)

                def silu(i, p):
                    act.wait_ge(s_hlo, n0 + i + 1)
                    for m in range(DC):
                        act.wait_ge(s_w1, (n0 + i) * 2 + 5 + m)
                        act.activation(h1f[:, m, :], ps[:, 6 * p + m, :], ACT.Silu, bias=b1[:, m:m + 1]).then_inc(s_silu, 1)
                    act.wait_ge(s_w2, (n0 + i) * 2 + 2)
                    act.wait_ge(s_silu, (n0 + i) * 2 + 6)
                    act.copy(h1s[p][0], h1f[:, :, :]).then_inc(s_hhi, 1)

                def tanh(i, p):
                    act.wait_ge(s_zb, (n0 + i) * 2 + 4)
                    act.activation(th[p], th[p], ACT.Tanh, scale=0.5).then_inc(s_th, 1)
                rbf_high(0, 0, 0)
                rbf_high(1, 0, 1)
                silu(0, 0)
                rbf_high(2, 1, 0)
                silu(1, 1)
                with act.Fori(0, NG // 2 - 2) as j:
                    tanh(j * 2, 0)
                    rbf_high(j * 2 + 3, j + 1, 1)
                    silu(j * 2 + 2, 0)
                    tanh(j * 2 + 1, 1)
                    rbf_high(j * 2 + 4, j + 2, 0)
                    silu(j * 2 + 3, 1)
                tanh(NG - 4, 0)
                rbf_high(NG - 1, NG // 2 - 1, 1)
                silu(NG - 2, 0)
                tanh(NG - 3, 1)
                silu(NG - 1, 1)
                tanh(NG - 2, 0)
                tanh(NG - 1, 1)
            edges(0, 0)
            act.wait_ge(s_flag, 1)
            left = act.value_load(flag[0:1, 0:1], min_val=0, max_val=E)
            with act.If(left > 0):
                with act.Fori(0, NW) as w:
                    edges((w + 1) * NG, (w + 1) * (NG // 2))

            act.sem_inc(s_us, 2)
            def u1_silu(t, j, p):
                act.wait_ge(s_u1, t + 1)
                act.wait_ge(s_uo, t + 1)
                for m in range(DC):
                    last = act.activation(sst[p][:, m, :], ps[:, p, m * P:(m + 1) * P], ACT.Silu, bias=c1[:, m:m + 1])
                last.then_inc(s_us, 1)
            in_pairs(act, NT, u1_silu)

            def copy_xt2(t, j, p):
                act.wait_ge(s_tp2, t + 3)
                act.wait_ge(s_lg, t + 1)
                act.copy(xt[p][:, :, :], ps[:, 4 + p, 0:D].rearrange("p (c q) -> p c q", c=DC)).then_inc(s_xt2, 1)
            in_pairs(act, NT, copy_xt2)

            act.wait_ge(s_dif, 1)
            act.activation(exw[:, :], exw[:, :], ACT.Exp).then_inc(s_ex, 1)

            act.sem_inc(s_y, 2)
            def w_high(r, i, j, p, first=False):
                act.wait_ge(s_win[r][p], (j + 1) * (32 if r < 2 else 16))
                if not first:
                    act.wait_ge(*((s_h, i * 4 + 4 + 2 * r + 2) if r < 2 else (s_o, i + 2)))
                act.copy(ws[r][0], wst[r][p]).then_inc(s_wh[r], 1)

            def slots_high(i, p):
                act.wait_ge(s_xsp, i + 3)
                act.wait_ge(s_h, i * 4 + 4)
                act.copy(xTs[p][0], ps[:, 7, :].rearrange("p (c q) -> p c q", c=DC)).then_inc(s_xhi, 1)

            def silu_g(i, q):
                act.wait_ge(s_h, i * 4 + 8 + 2 * q + 1)
                act.wait_ge(s_hid, i * 2 + q + 1)
                act.activation(gate[q], ps[:, q, :], ACT.Silu).then_inc(s_g, 1)

            def hid_high(i, p, q):
                act.wait_ge(s_hid, i * 2 + q + 3)
                act.wait_ge(s_o, i + 1)
                act.copy(hids[p][0][:, 2 * q:2 * q + 2, :], hidf[q]).then_inc(s_hdh, 1)

            def copy_y(i, j, p):
                act.wait_ge(s_o, i + 3)
                if not (type(i) is int and i == p):
                    act.wait_ge(s_yst[p], j * 32)
                act.copy(ys[p], ps[:, 4 + p, :].rearrange("p (s d) -> p s d", s=2)).then_inc(s_y, 1)

            def block_steps(i, j, p, jn, last=False):
                silu_g(i, 0)
                if not last:
                    w_high(0, i + 1, jn, 1 - p)
                    slots_high(i + 1, 1 - p)
                hid_high(i, p, 0)
                w_high(2, i, j, p, first=(type(i) is int and i == 0))
                if not (type(i) is int and i == 0):
                    copy_y(i - 1, jn - 1, 1 - p)
                silu_g(i, 1)
                hid_high(i, p, 1)
                if not last:
                    w_high(1, i + 1, jn, 1 - p)
            w_high(0, 0, 0, 0, True)
            slots_high(0, 0)
            w_high(1, 0, 0, 0, True)
            block_steps(0, 0, 0, 0)
            block_steps(1, 0, 1, 1)
            block_steps(2, 1, 0, 1)
            block_steps(3, 1, 1, 2)
            act.wait_ge(s_texp, 1)
            end = last_pair(act, lastp)
            with act.Fori(2, CAPB // 2 - 1) as j:
                with act.If(end > j):
                    block_steps(j * 2, j, 0, j)
                    block_steps(j * 2 + 1, j, 1, j + 1)
            block_steps(end * 2, end, 0, end)
            block_steps(end * 2 + 1, end, 1, end + 1, last=True)
            copy_y(end * 2 + 1, end, 1)

        @block.vector
        def _(dve):
            steps = [0]

            def link(ins):
                steps[0] = steps[0] + 1
                ins.then_inc(s_dve, 1)
                dve.wait_ge(s_dve, steps[0])

            def rsqrt(y, v, a, b):
                link(dve.tensor_scalar(a.bitcast(i32), v.bitcast(i32), 1, None, ALU.arith_shift_right))
                link(dve.tensor_scalar(y.bitcast(i32), a.bitcast(i32), -1.0, MAGIC, ALU.mult, ALU.add))
                for _ in range(4):
                    link(dve.tensor_tensor(a, y, y, ALU.mult))
                    link(dve.tensor_tensor(b, a, v, ALU.mult))
                    link(dve.tensor_scalar(a, b, -0.5, 1.5, ALU.mult, ALU.add))
                    link(dve.tensor_tensor(y, y, a, ALU.mult))

            def layer_stats():
                a, b, v = v_a[:, 0:NT], v_b[:, 0:NT], v_c[:, 0:NT]
                link(dve.tensor_tensor(a, st6[:, :, 1], st6[:, :, 4], ALU.add))
                link(dve.tensor_scalar(mean[:, :], a, 0.5, None, ALU.mult))
                link(dve.tensor_tensor(a, st6[:, :, 1], st6[:, :, 4], ALU.subtract))
                link(dve.tensor_tensor(b, a, a, ALU.mult))
                link(dve.tensor_tensor(a, st6[:, :, 2], st6[:, :, 5], ALU.add))
                link(dve.tensor_scalar(b, b, 0.25, EPS, ALU.mult, ALU.add))
                link(dve.scalar_tensor_tensor(v, a, 1.0 / D, b, ALU.mult, ALU.add))
                rsqrt(rstd[:, :], v, a, b)

            def stats(t, j=None, p=None):
                return dve.bn_stats(st6[:, ds(t, 1), :].rearrange("p a s -> p (a s)"),
                                    x[:, ds(t, 1), :].rearrange("p a d -> p (a d)"))
            dve.wait_ge(s_x[0], 16)
            with dve.Fori(0, 12) as t:
                stats(t)
            dve.wait_ge(s_x[1], 16)
            with dve.Fori(12, 24) as t:
                stats(t)
            dve.wait_ge(s_x[2], 16)
            link(stats(NT - 1))
            layer_stats()

            dve.wait_ge(s_par, 16 * NPAR)
            for c in range(DC):
                heads = wkv[:, c, :].rearrange("p (h d) -> p h d", d=HD)
                link(dve.tensor_reduce(v_a[:, 0:8], heads, X, ALU.add))
                link(dve.tensor_scalar(v_a[:, 0:8], v_a[:, 0:8], 1.0 / HD, None, ALU.mult))
                link(dve.tensor_tensor(heads, heads, v_a[:, 0:8].unsqueeze(2).to_broadcast([P, 8, HD]), ALU.subtract))
            dve.sem_inc(s_mv, 1)

            dve.sem_inc(s_sq, 2)
            def make_xn(t, j, p, ready, stored, used):
                if not (type(t) is int and t == p):
                    dve.wait_ge(stored[p], j * 16)
                dve.wait_ge(used, t + 1)
                dve.tensor_scalar(xn[p][:, :], x[:, ds(t, 1), :].rearrange("p a d -> p (a d)"),
                                  mean[:, ds(t, 1)], rstd[:, ds(t, 1)], ALU.subtract, ALU.mult).then_inc(ready, 1)

            def xn1(t, j, p):
                make_xn(t, j, p, s_xn, s_xnst, s_tp)

            def sum_sq(t, j, p):
                dve.wait_ge(s_kvd, t + 3)
                dve.tensor_reduce(ssq[:, ds(t * 8, 8)], sq[p].rearrange("p (h d) -> p h d", d=HD), X, ALU.add)\
                    .then_inc(s_sq, 1)
            xn1(0, 0, 0)
            xn1(1, 0, 1)
            with dve.Fori(0, NT // 2 - 1) as j:
                xn1(j * 2 + 2, j + 1, 0)
                sum_sq(j * 2, j, 0)
                xn1(j * 2 + 3, j + 1, 1)
                sum_sq(j * 2 + 1, j, 1)
            xn1(NT - 1, NT // 2, 0)
            for t in range(NT - 3, NT):
                sum_sq(t, t // 2, t % 2)
            dve.wait_ge(s_sq, NT + 2)
            link(dve.tensor_scalar(v_c[:, :], ssq[:, :], 1.0 / HD, EPS, ALU.mult, ALU.add))
            rsqrt(kvr[:, :], v_c[:, :], v_a[:, :], v_b[:, :])

            def scale_kv(t, j, p):
                dve.wait_ge(s_khp, t + 1)
                r = kvr[:, ds(t * 8, 8)].unsqueeze(2).to_broadcast([P, 8, HD])
                kv = kvc[:, ds(t, 1), :].rearrange("p a (h d) -> p (a h) d", d=HD)
                for jj in range(2):
                    dve.tensor_tensor(khs[p][:, jj, 0:P].rearrange("p (h d) -> p h d", d=HD),
                                      kv[:, 2 * jj:2 * jj + 2, :], r[:, 2 * jj:2 * jj + 2, :], ALU.mult)
                dve.tensor_tensor(vhs[p].rearrange("p (h d) -> p h d", d=HD), kv[:, 4:8, :], r[:, 4:8, :], ALU.mult)\
                    .then_inc(s_kh, 1)
            dve.wait_ge(s_const, 1)
            in_pairs(dve, NT, scale_kv)

            dve.wait_ge(s_mx, 1)
            link(dve.memset(kvt, 0.0))
            for c in range(DC):
                link(dve.tensor_copy(kv_s, ps[:, 4 + c, P:P + 1]))
                link(dve.tensor_tensor(kv_t, ps[:, 4 + c, 0:P], kgb[:, 0, :], ALU.mult))
                link(dve.scalar_tensor_tensor(kv_t, kgb[:, 1, :], kv_s, kv_t, ALU.mult, ALU.add))
                link(dve.tensor_tensor(kv_r, ps[:, 6, c * P:(c + 1) * P], kgb[:, 0, :], ALU.mult))
                link(dve.scalar_tensor_tensor(kv_r, kgb[:, 1, :], float(N), kv_r, ALU.mult, ALU.add))
                link(dve.tensor_scalar(kv_t, kv_t, vgb[:, 0:1], None, ALU.mult))
                for h in range(2):
                    q = slice(h * HD, (h + 1) * HD)
                    link(dve.scalar_tensor_tensor(kvt[q, c, q], kv_r[q, :][:, q], vgb[q, 1:2], kv_t[q, :][:, q],
                                                  ALU.mult, ALU.add))
            dve.memset(agg, 0.0)
            dve.sem_inc(s_mv, 1)
            dve.wait_ge(s_mx, 2)
            link(dve.tensor_copy(A1, ps[:, 0, :].rearrange("p (c n) -> p c n", c=DC)))
            dve.sem_inc(s_mv, 1)
            dve.wait_ge(s_mx, 3)
            link(dve.tensor_scalar(M, ps[:, 1, :].rearrange("p (c n) -> p c n", c=DC), 1.0 / N, None, ALU.mult))
            for c in range(DC):
                q = slice(c * P, (c + 1) * P)
                link(dve.tensor_tensor(M[:, c, q], M[:, c, q], ident[:, :], ALU.add))
            dve.sem_inc(s_mv, 2)

            dve.wait_ge(s_whi, 2)
            dve.tensor_tensor(W1s[1], W1[:, :], W1s[0].bitcast(f32), ALU.subtract)
            dve.tensor_tensor(W2s[1], W2[:, :, :], W2s[0].bitcast(f32), ALU.subtract).then_inc(s_wlow, 1)

            dve.wait_ge(s_edge, 64)
            link(dve.tensor_copy(dstf[:, :], dsti))
            link(dve.tensor_copy(basef[:, :], basei[:, :]))
            link(dve.tensor_scalar(basef[:, :], basef[:, :], 0.0, float(AW - W), ALU.max, ALU.min))
            link(dve.tensor_copy(basei[:, :], basef[:, :]))
            link(dve.tensor_tensor(rel[:, :].rearrange("p (g s) -> p g s", s=ET),
                                   dstf[:, :].rearrange("p (g s) -> p g s", s=ET),
                                   basef[:, :].unsqueeze(2).to_broadcast([P, NG, ET]), ALU.subtract))
            link(dve.tensor_scalar(cover, rel[:, :], 0.0, None, ALU.is_ge))
            link(dve.scalar_tensor_tensor(cover, rel[:, :], float(W), cover, ALU.is_lt, ALU.mult))
            link(dve.scalar_tensor_tensor(cover, dstf[:, :], 1.0, cover, ALU.add, ALU.mult))
            link(dve.tensor_tensor(dstf[:, :], dstf[:, :], cover, ALU.subtract))
            link(dve.tensor_scalar(cover, dstf[:, :], 0.0, None, ALU.is_ge))
            link(dve.scalar_tensor_tensor(cover, dstf[:, :], float(N), cover, ALU.is_lt, ALU.mult))
            link(dve.tensor_reduce(v_a[:, 0:1], cover, X, ALU.add))
            dve.sem_inc(s_cov, 1)
            dve.wait_ge(s_cov, 2)
            dve.tensor_copy(flag[:, :], ps[:, 7, 0:1]).then_inc(s_flag, 1)

            dve.sem_inc(s_rlo, 2)
            dve.sem_inc(s_hlo, 1)
            dve.sem_inc(s_zb, 2)
            dve.sem_inc(s_msg, 2)
            dve.sem_inc(s_agg, 2)

            def edges(n0, h0, w_n, base, rel_t):
                def rbf_low(i, p):
                    dve.wait_ge(s_rhi, n0 + i + 1)
                    q = slice(RB, P)
                    dve.tensor_tensor(rbs[p][q, :], rbf[p][q, :], rbs[p][q, :].bitcast(f32), ALU.subtract)\
                        .then_inc(s_rlo, 1)

                def h1_low(i, p):
                    dve.wait_ge(s_hhi, n0 + i + 1)
                    dve.tensor_tensor(h1s[p][1], h1f[:, :, :], h1s[p][0].bitcast(f32), ALU.subtract).then_inc(s_hlo, 1)

                def bias(i, p):
                    for b in range(2):
                        dve.wait_ge(s_w2, (n0 + i) * 2 + 5 + b)
                        dve.tensor_tensor(th[p][:, 2 * b:2 * b + 2, :],
                                          ps[:, 2 + b, :].rearrange("p (s d) -> p s d", s=2),
                                          b2bc[:, :, :], ALU.add).then_inc(s_zb, 1)

                def onehot(i, p):
                    dve.wait_ge(s_sc, n0 + i + 1)
                    dve.tensor_tensor(oh[p][:, :, 0:w_n], iota[:, 0:w_n].unsqueeze(1).to_broadcast([P, ET, w_n]),
                                      rel_t[:, ds(i * ET, ET)].unsqueeze(2).to_broadcast([P, ET, w_n]), ALU.is_equal)

                def message(i, j, p):
                    dve.wait_ge(s_th, n0 + i + 1)
                    dve.wait_ge(s_hg[p], (h0 + j + 1) * (16 * ET))
                    dve.scalar_tensor_tensor(msg[p], th[p], 1.0, hg[p], ALU.add, ALU.mult)\
                        .then_inc(s_msg, 1)

                def add_window(i, p):
                    at = base(i)
                    dve.wait_ge(s_sc, n0 + i + 3)
                    dve.wait_ge(s_agg, n0 + i + 2)
                    a = agg[:, :, ds(at, w_n)]
                    dve.scalar_tensor_tensor(a, ps[:, 4 + p, 0:DC * w_n].rearrange("p (c w) -> p c w", c=DC), 0.5,
                                             a, ALU.mult, ALU.add).then_inc(s_agg, 1)

                def step(i, j, p, after=3, first=False):
                    bias(i, p)
                    if after > 0:
                        h1_low(i + 1, 1 - p)
                    message(i, j, p)
                    if after > 2:
                        rbf_low(i + 3, 1 - p)
                    if not first:
                        add_window(i - 1, 1 - p)
                    if after > 0:
                        onehot(i + 1, 1 - p)
                rbf_low(0, 0)
                rbf_low(1, 1)
                h1_low(0, 0)
                rbf_low(2, 0)
                onehot(0, 0)
                step(0, 0, 0, first=True)
                step(1, 0, 1)
                with dve.Fori(1, NG // 2 - 2) as j:
                    step(j * 2, j, 0)
                    step(j * 2 + 1, j, 1)
                for i in range(NG - 4, NG):
                    step(i, i // 2, i % 2, after=NG - 1 - i)
                add_window(NG - 1, 1)
            edges(0, 0, W, lambda i: dve.value_load(basei[0:1, ds(i, 1)], min_val=0, max_val=AW - W), rel)
            left = dve.value_load(flag[0:1, 0:1], min_val=0, max_val=E)
            with dve.If(left > 0):
                with dve.Fori(0, NW) as w:
                    edges((w + 1) * NG, (w + 1) * (NG // 2), FW, lambda i: w * FW, dstf)
                    dve.tensor_scalar(dstf[:, :], dstf[:, :], float(FW), None, ALU.subtract).then_inc(s_cov, 1)
                    dve.wait_ge(s_cov, w + 3)
            link(dve.tensor_copy(v_a[:, 0:1], agg[:, 0, 0:1]))
            dve.sem_inc(s_gnn, 1)

            dve.wait_ge(s_xcb, NT)
            dve.sem_inc(s_x1, 2)
            def x1(t, j, p):
                dve.wait_ge(s_uo, t + 3)
                xr = x[:, ds(t, 1), :].rearrange("p a d -> p (a d)")
                dve.tensor_tensor(xr, ps[:, 2 + p, 0:D], xr, ALU.add).then_inc(s_x1, 1)
            x1(0, 0, 0)
            with dve.Fori(0, NT // 2) as j:
                for p in range(2):
                    x1(j * 2 + p + 1, j, 1 - p)
                    dve.wait_ge(s_x1, j * 2 + p + 3)
                    stats(j * 2 + p)
            dve.wait_ge(s_x1, NT + 2)
            link(stats(NT - 1))
            layer_stats()

            def xn2(t, j, p):
                make_xn(t, j, p, s_xn2, s_xn2st, s_tp2)

            def logits(t, j, p):
                dve.wait_ge(s_lg, t + 3)
                dve.tensor_tensor(lg[:, ds(t, 1), :].rearrange("p a n -> p (a n)"), ps[:, 6 + p, 0:NX], gb[:, :], ALU.add)\
                    .then_inc(s_lgc, 1)
            dve.sem_inc(s_lgc, 2)
            xn2(0, 0, 0)
            xn2(1, 0, 1)
            with dve.Fori(0, NT // 2 - 1) as j:
                xn2(j * 2 + 2, j + 1, 0)
                logits(j * 2, j, 0)
                xn2(j * 2 + 3, j + 1, 1)
                logits(j * 2 + 1, j, 1)
            xn2(NT - 1, NT // 2, 0)
            for t in range(NT - 3, NT):
                logits(t, t // 2, t % 2)
            dve.wait_ge(s_lgc, NT + 2)

            io = iota[:, 0:NX].unsqueeze(1).to_broadcast([P, NT, NX])
            for k in range(2):
                m = top[:, k, :]
                link(dve.tensor_reduce(m, lg, X, ALU.max))
                link(dve.tensor_tensor(t_a, lg, m.unsqueeze(2).to_broadcast([P, NT, NX]), ALU.is_equal))
                link(dve.tensor_scalar(t_a, t_a, -float(NX), float(NX), ALU.mult, ALU.add))
                link(dve.tensor_tensor(t_a, t_a, io, ALU.add))
                link(dve.tensor_reduce(v_a[:, 0:NT], t_a, X, ALU.min))
                link(dve.tensor_tensor(ohx[k], io, v_a[:, 0:NT].unsqueeze(2).to_broadcast([P, NT, NX]), ALU.is_equal))
                if k == 0:
                    link(dve.scalar_tensor_tensor(lg, ohx[0], -3e38, lg, ALU.mult, ALU.add))
            link(dve.tensor_tensor(exw[:, :], top[:, 1, :], top[:, 0, :], ALU.subtract))
            dve.sem_inc(s_dif, 1)
            for k in range(2):
                link(dve.tensor_scalar(ohx[k][:, NT - 1, :], ohx[k][:, NT - 1, :], valid[:, 0:1], None, ALU.mult))
            link(dve.tensor_tensor(m12, ohx[0], ohx[1], ALU.add))
            dve.sem_inc(s_m12, 1)
            dve.wait_ge(s_ex, 1)
            link(dve.tensor_scalar(v_a[:, 0:NT], exw[:, :], 1.0, None, ALU.add))
            link(dve.reciprocal(wts[:, 0, :], v_a[:, 0:NT]))
            link(dve.tensor_tensor(wts[:, 1, :], wts[:, 0, :], exw[:, :], ALU.mult))

            dve.wait_ge(s_cnt, 1)
            link(dve.memset(onerow, 1.0))
            link(dve.tensor_copy(t_et, ps[:, 1, 0:TX].rearrange("p (t e) -> p e t", e=NX)))
            ff = lambda ap: ap.rearrange("p a b -> p (a b)")
            link(dve.tensor_tensor_scan(ff(t_in), onerow, ff(t_et), 0.0, ALU.mult, ALU.add))
            link(dve.tensor_tensor(t_ex, t_in, t_et, ALU.subtract))
            link(dve.tensor_tensor(n_e, t_in[:, :, NT - 1], t_ex[:, :, 0], ALU.subtract))
            link(dve.tensor_scalar(c_i[:, :], n_e, float(SB - 1), None, ALU.add))
            link(dve.tensor_scalar(c_i[:, :], c_i[:, :], SB.bit_length() - 1, None, ALU.arith_shift_right))
            link(dve.tensor_copy(c_e, c_i[:, :]))
            link(dve.tensor_tensor_scan(cend, onerow[:, 0:NX], c_e, 0.0, ALU.mult, ALU.add))
            link(dve.tensor_tensor(off, cend, c_e, ALU.subtract))
            link(dve.scalar_tensor_tensor(off, off, float(SB), t_ex[:, :, 0], ALU.mult, ALU.subtract))
            link(dve.tensor_tensor(t_a, t_ex.rearrange("p e t -> p t e"),
                                   off.unsqueeze(1).to_broadcast([P, NT, NX]), ALU.add))
            link(dve.tensor_tensor(t_a, ps[:, 0, 0:TX].rearrange("p (t e) -> p t e", e=NX), t_a, ALU.add))
            for k in range(2):
                link(dve.tensor_tensor(t_b, ohx[k], t_a, ALU.mult))
                link(dve.tensor_reduce(posf[:, k, :], t_b, X, ALU.add))
            link(dve.tensor_copy(posi[:, :, :], posf))
            link(dve.tensor_scalar(bits, posi[:, :, :], P - 1, None, ALU.bitwise_and))
            link(dve.tensor_copy(lof, bits))
            link(dve.tensor_scalar(bits, posi[:, :, :], 7, None, ALU.arith_shift_right))
            link(dve.tensor_copy(hif, bits))
            link(dve.tensor_tensor(tcmp, cend.unsqueeze(1).to_broadcast([P, CAPB, NX]),
                                   iota[:, 0:CAPB].unsqueeze(2).to_broadcast([P, CAPB, NX]), ALU.is_le))
            link(dve.tensor_reduce(texp_f, tcmp, X, ALU.add))
            link(dve.tensor_scalar(texp[:, :], texp_f, float(NX - 1), None, ALU.min))
            link(dve.tensor_scalar(lastp[:, :], cend[:, NX - 1:NX], -3.0, None, ALU.add))
            dve.tensor_scalar(lastp[:, :], lastp[:, :], 1, None, ALU.arith_shift_right).then_inc(s_texp, 1)

            def onehots(c, p, waits=True):
                k_t = lambda ap: ap.rearrange("p k t -> p (k t)")[:, ds(c, 1)]
                if waits:
                    dve.wait_ge(s_tab, c - 1)
                dve.tensor_scalar(tA[p], iota[:, 0:P], k_t(lof), None, ALU.is_equal)
                dve.tensor_scalar(tB[p], iota[:, 0:NS], k_t(hif), k_t(tok[:, :, :]), ALU.is_equal, ALU.mult)\
                    .then_inc(s_hot, 1)
            onehots(0, 0, False)
            onehots(1, 1, False)
            with dve.Fori(1, NT) as j:
                onehots(j * 2, 0)
                onehots(j * 2 + 1, 1)
            dve.wait_ge(s_tab, 2 * NT)
            held, second, row = tf
            link(dve.tensor_scalar(held, ps[:, 2, 0:NS], 1.0, None, ALU.is_ge))
            link(dve.tensor_scalar(second, ps[:, 2, 0:NS], float(PK + 1), None, ALU.is_ge))
            link(dve.tensor_tensor(row, ps[:, 2, 0:NS], held, ALU.subtract))
            link(dve.scalar_tensor_tensor(row, second, -float(PK), row, ALU.mult, ALU.add))
            link(dve.tensor_copy(tab[:, :], row))
            link(dve.scalar_tensor_tensor(row, second, float(NP), row, ALU.mult, ALU.add))
            link(dve.tensor_tensor(row, row, slot[:, :], ALU.subtract))
            link(dve.tensor_tensor(row, row, held, ALU.mult))
            link(dve.tensor_tensor(dest[:, :], row, slot[:, :], ALU.add))
            dve.sem_inc(s_tabi, 1)

            dve.sem_inc(s_hid, 2)
            dve.sem_inc(s_xlo, 1)
            def w_low(r, i, p):
                dve.wait_ge(s_wh[r], i + 1)
                dve.tensor_tensor(ws[r][1], wst[r][p], ws[r][0].bitcast(f32), ALU.subtract).then_inc(s_wlo[r], 1)

            def slots_low(i, p):
                dve.wait_ge(s_xhi, i + 1)
                dve.tensor_tensor(xTs[p][1], ps[:, 7, :].rearrange("p (c q) -> p c q", c=DC),
                                  xTs[p][0].bitcast(f32), ALU.subtract).then_inc(s_xlo, 1)

            def hidden(i, p, q):
                dve.wait_ge(s_h, i * 4 + 8 + 2 * q + 2)
                dve.wait_ge(s_g, i * 2 + q + 1)
                dve.tensor_tensor(hidf[q], gate[q].rearrange("p (k s) -> p k s", k=2),
                                  ps[:, 2 + q, :].rearrange("p (k s) -> p k s", k=2), ALU.mult).then_inc(s_hid, 1)

            def hidden_low(i, p, q):
                dve.wait_ge(s_hdh, i * 2 + q + 1)
                h = slice(2 * q, 2 * q + 2)
                dve.tensor_tensor(hids[p][1][:, h, :], hidf[q], hids[p][0][:, h, :].bitcast(f32), ALU.subtract)\
                    .then_inc(s_hdl, 1)

            def block_steps(i, p, last=False):
                hidden(i, p, 0)
                if not last:
                    w_low(0, i + 1, 1 - p)
                    slots_low(i + 1, 1 - p)
                hidden_low(i, p, 0)
                w_low(2, i, p)
                hidden(i, p, 1)
                hidden_low(i, p, 1)
                if not last:
                    w_low(1, i + 1, 1 - p)
            w_low(0, 0, 0)
            slots_low(0, 0)
            w_low(1, 0, 0)
            dve.wait_ge(s_texp, 1)
            end = last_pair(dve, lastp)
            with dve.Fori(0, CAPB // 2 - 1) as j:
                with dve.If(end > j):
                    block_steps(j * 2, 0)
                    block_steps(j * 2 + 1, 1)
            block_steps(end * 2, 0)
            block_steps(end * 2 + 1, 1, last=True)

            dve.sem_inc(s_fin, 2)
            def combine(t, j, p, n=P):
                dve.wait_ge(s_yg[p], (j + 1) * 16)
                if not (type(t) is int and t == p):
                    dve.wait_ge(s_out[p], j * 16)
                dve.scalar_tensor_tensor(oo[p][0:n, 0, :], yg[p][0:n, 0, :], wts[0:n, 0, ds(t, 1)],
                                         x[0:n, ds(t, 1), :].rearrange("p a d -> p (a d)"), ALU.mult, ALU.add)\
                    .then_inc(s_x1, 1)
                dve.wait_ge(s_x1, t + NT + 3)
                dve.scalar_tensor_tensor(oo[p][0:n, 1, :], yg[p][0:n, 1, :], wts[0:n, 1, ds(t, 1)],
                                         oo[p][0:n, 0, :], ALU.mult, ALU.add).then_inc(s_fin, 1)
            combine(0, 0, 0)
            combine(1, 0, 1)
            with dve.Fori(1, NT // 2) as j:
                combine(j * 2, j, 0)
                combine(j * 2 + 1, j, 1)
            combine(NT - 1, NT // 2, 0, LAST)

        @block.tensor
        def _(pe):
            mm = pe.matmul
            pe.wait_ge(s_const, 1)
            pe.sem_inc(s_tp, 2)
            pe.sem_inc(s_kv, 2)
            pe.wait_ge(s_mv, 1)

            def transpose_xn(t, p, bank, ready, made, copied=None):
                pe.wait_ge(made, t + 1)
                if copied is not None:
                    pe.wait_ge(*copied)
                for c in range(DC):
                    last = pe.transpose(ps[:, bank + p, c * P:(c + 1) * P], xn[p][:, c * P:(c + 1) * P], ident[:, :])
                last.then_inc(ready, 1)

            def project(t, p):
                pe.wait_ge(s_xt, t + 1)
                pe.wait_ge(s_kvd, t + 1)
                for c in range(DC):
                    last = mm(ps[:, 2 + p, :], xt[p][:, c, :], wkv[:, c, :], start=c == 0, stop=c == DC - 1)
                last.then_inc(s_kv, 1)
            transpose_xn(0, 0, 0, s_tp, s_xn)
            transpose_xn(1, 1, 0, s_tp, s_xn)
            project(0, 0)
            with pe.Fori(1, NT // 2) as j:
                transpose_xn(j * 2, 0, 0, s_tp, s_xn, (s_xt, j * 2 - 1))
                project(j * 2 - 1, 1)
                transpose_xn(j * 2 + 1, 1, 0, s_tp, s_xn, (s_xt, j * 2))
                project(j * 2, 0)
            transpose_xn(NT - 1, 0, 0, s_tp, s_xn, (s_xt, NT - 2))
            project(NT - 2, 1)
            project(NT - 1, 0)

            pe.sem_inc(s_khp, 2)
            def sum_kv(t, p, start=False, stop=False):
                pe.wait_ge(s_kh, t + 1)
                for c in range(DC):
                    mm(ps[:, 4 + c, 0:P + 1], vhs[p][:, c * P:(c + 1) * P], khs[p][:, c, 0:P + 1], start=start, stop=stop)
                mm(ps[:, 6, 0:D].rearrange("p (c d) -> p c d", c=DC), ones[:, :], khs[p][:, :, 0:P],
                   start=start, stop=stop).then_inc(s_khp, 1)
            sum_kv(0, 0, start=True)
            sum_kv(1, 1)
            with pe.Fori(1, NT // 2) as j:
                sum_kv(j * 2, 0)
                sum_kv(j * 2 + 1, 1)
            sum_kv(NT - 1, 0, stop=True)
            pe.wait_ge(s_khp, NT + 2)
            pe.sem_inc(s_mx, 1)
            pe.wait_ge(s_mv, 2)
            for c in range(DC):
                last = mm(ps[:, 0, c * D:(c + 1) * D], kvt[:, c, :], woT[:, c, :], start=True, stop=True)
            last.then_inc(s_mx, 1)
            pe.wait_ge(s_mv, 3)
            for m in range(DC):
                for c in range(DC):
                    last = mm(ps[:, 1, m * D:(m + 1) * D], wq[:, c, m * P:(m + 1) * P], A1[:, c, :],
                              start=c == 0, stop=c == DC - 1)
            last.then_inc(s_mx, 1)
            pe.wait_ge(s_cov, 1)
            mm(ps[:, 7, 0:1], ones[:, :], v_a[:, 0:1], start=True, stop=True).then_inc(s_cov, 1)

            pe.sem_inc(s_w1, 4)
            pe.sem_inc(s_w2, 4)
            pe.sem_inc(s_sc, 2)
            pe.wait_ge(s_mv, 5)
            pe.wait_ge(s_flag, 1)
            pe.wait_ge(s_wlow, 1)

            def edges(n0, h0, w_n):
                def up(i, p):
                    pe.wait_ge(s_rlo, n0 + i + 3)
                    for m in range(DC):
                        pe.wait_ge(s_silu, (n0 + i) * 2 + m + 1)
                        for k in range(2):
                            last = mm(ps[:, 6 * p + m, :], W1s[k][:, m * P:(m + 1) * P], rbs[p],
                                      start=k == 0, stop=k == 1)
                        last.then_inc(s_w1, 1)

                def gates(i, p):
                    pe.wait_ge(s_hlo, n0 + i + 2)
                    for s in range(ET):
                        if s % 2 == 0:
                            pe.wait_ge(s_zb, (n0 + i) * 2 + s // 2 + 1)
                        for c in range(DC):
                            for a, b in PARTS:
                                last = mm(ps[:, 2 + s // 2, (s % 2) * D:(s % 2 + 1) * D],
                                          h1s[p][a][:, c, s * P:(s + 1) * P], W2s[b][:, c, :],
                                          start=c == 0 and (a, b) == PARTS[0], stop=c == DC - 1 and (a, b) == PARTS[-1])
                        if s % 2:
                            last.then_inc(s_w2, 1)

                def scatter(i, p):
                    pe.wait_ge(s_msg, n0 + i + 3)
                    pe.wait_ge(s_agg, n0 + i + 1)
                    for c in range(DC):
                        for s in range(ET):
                            last = mm(ps[:, 4 + p, c * w_n:(c + 1) * w_n], msg[p][:, s, c * P:(c + 1) * P],
                                      oh[p][:, s, 0:w_n], start=s == 0, stop=s == ET - 1)
                    last.then_inc(s_sc, 1)
                up(0, 0)
                up(1, 1)
                gates(0, 0)
                up(2, 0)
                with pe.Fori(1, NG // 2 - 1) as j:
                    gates(j * 2 - 1, 1)
                    up(j * 2 + 1, 1)
                    scatter(j * 2 - 2, 0)
                    gates(j * 2, 0)
                    up(j * 2 + 2, 0)
                    scatter(j * 2 - 1, 1)
                gates(NG - 3, 1)
                up(NG - 1, 1)
                scatter(NG - 4, 0)
                gates(NG - 2, 0)
                scatter(NG - 3, 1)
                gates(NG - 1, 1)
                scatter(NG - 2, 0)
                scatter(NG - 1, 1)
            edges(0, 0, W)
            pe.wait_ge(s_flag, 1)
            left = pe.value_load(flag[0:1, 0:1], min_val=0, max_val=E)
            with pe.If(left > 0):
                with pe.Fori(0, NW) as w:
                    edges((w + 1) * NG, (w + 1) * (NG // 2), FW)

            pe.sem_inc(s_uo, 2)
            pe.wait_ge(s_gnn, 1)
            pe.wait_ge(s_xnT, NT + 2)
            def node_up(t, p):
                pe.wait_ge(s_us, t + 1)
                for m in range(DC):
                    for k in range(2 * DC):
                        src = (xnT if k < DC else agg)[:, k % DC, ds(t * P, P)]
                        last = mm(ps[:, p, m * P:(m + 1) * P], U1[:, k, m * P:(m + 1) * P], src,
                                  start=k == 0, stop=k == 2 * DC - 1)
                last.then_inc(s_u1, 1)

            def node_down(t, p):
                pe.wait_ge(s_us, t + 3)
                pe.wait_ge(s_xnc, t + 1)
                for k in range(2 * DC):
                    lhs, rhs = (sst[p][:, k, :], U2[:, k, :]) if k < DC else (xt[p][:, k - DC, :], M[:, k - DC, :])
                    last = mm(ps[:, 2 + p, 0:D], lhs, rhs, start=k == 0, stop=k == 2 * DC - 1)
                last.then_inc(s_uo, 1)
            node_up(0, 0)
            node_up(1, 1)
            node_down(0, 0)
            with pe.Fori(1, NT // 2) as j:
                node_up(j * 2, 0)
                pe.wait_ge(s_x1, j * 2)
                node_down(j * 2 - 1, 1)
                node_up(j * 2 + 1, 1)
                pe.wait_ge(s_x1, j * 2 + 1)
                node_down(j * 2, 0)
            node_up(NT - 1, 0)
            pe.wait_ge(s_x1, NT - 1)
            node_down(NT - 2, 1)
            pe.wait_ge(s_x1, NT)
            node_down(NT - 1, 0)

            pe.sem_inc(s_tp2, 2)
            pe.sem_inc(s_lg, 2)
            def gate_logits(t, p):
                pe.wait_ge(s_xt2, t + 1)
                pe.wait_ge(s_lgc, t + 1)
                for c in range(DC):
                    last = mm(ps[:, 6 + p, 0:NX], xt[p][:, c, :], gw[:, c, :], start=c == 0, stop=c == DC - 1)
                last.then_inc(s_lg, 1)
            transpose_xn(0, 0, 4, s_tp2, s_xn2)
            transpose_xn(1, 1, 4, s_tp2, s_xn2)
            gate_logits(0, 0)
            with pe.Fori(1, NT // 2) as j:
                transpose_xn(j * 2, 0, 4, s_tp2, s_xn2, (s_xt2, j * 2 - 1))
                gate_logits(j * 2 - 1, 1)
                transpose_xn(j * 2 + 1, 1, 4, s_tp2, s_xn2, (s_xt2, j * 2))
                gate_logits(j * 2, 0)
            transpose_xn(NT - 1, 0, 4, s_tp2, s_xn2, (s_xt2, NT - 2))
            gate_logits(NT - 2, 1)
            gate_logits(NT - 1, 0)

            pe.wait_ge(s_m12, 1)
            mf = m12.rearrange("p t e -> p (t e)")
            mm(ps[:, 0, 0:TX], before[:, :], mf, start=True, stop=True)
            mm(ps[:, 1, 0:TX], ones[:, :], mf, start=True, stop=True).then_inc(s_cnt, 1)

            def place(c, p, start=False, stop=False):
                pe.wait_ge(s_hot, c + 1)
                mm(ps[:, 2, 0:NS], tA[p], tB[p], start=start, stop=stop).then_inc(s_tab, 1)
            place(0, 0, start=True)
            place(1, 1)
            with pe.Fori(1, NT - 1) as j:
                place(j * 2, 0)
                place(j * 2 + 1, 1)
            place(2 * NT - 2, 0)
            place(2 * NT - 1, 1, stop=True)

            pe.sem_inc(s_xsp, 2)
            pe.sem_inc(s_h, 8)
            pe.sem_inc(s_o, 2)
            pe.wait_ge(s_tabi, 1)
            def turn(i, j, p):
                pe.wait_ge(s_xs[p], (j + 1) * 32)
                pe.wait_ge(s_xlo, i + 1)
                for s in range(2):
                    for c in range(DC):
                        last = pe.transpose(ps[:, 7, c * SB + s * P:c * SB + (s + 1) * P],
                                            xs[p][:, s, c * P:(c + 1) * P], ident[:, :])
                last.then_inc(s_xsp, 1)

            def expert_up(i, p, q):
                pe.wait_ge(s_wlo[q], i + 1)
                pe.wait_ge(s_xlo, i + 2)
                pe.wait_ge(s_hid, i * 2 + q + 1)
                for m in range(2):
                    for k in range(2):
                        for c in range(DC):
                            for a, b in PARTS:
                                last = mm(ps[:, 2 * m + q, k * SB:(k + 1) * SB],
                                          ws[q][a][:, 2 * m + c, k * P:(k + 1) * P], xTs[p][b][:, c, :],
                                          start=c == 0 and (a, b) == PARTS[0], stop=c == DC - 1 and (a, b) == PARTS[-1])
                    last.then_inc(s_h, 1)

            def expert_down(i, p):
                pe.wait_ge(s_wlo[2], i + 1)
                pe.wait_ge(s_hdl, i * 2 + 2)
                pe.wait_ge(s_y, i + 1)
                for s in range(2):
                    for k in range(HC):
                        for a, b in PARTS:
                            last = mm(ps[:, 4 + p, s * D:(s + 1) * D], hids[p][a][:, k, s * P:(s + 1) * P],
                                      ws[2][b][:, k, :],
                                      start=k == 0 and (a, b) == PARTS[0], stop=k == HC - 1 and (a, b) == PARTS[-1])
                last.then_inc(s_o, 1)
            turn(0, 0, 0)
            expert_up(0, 0, 0)
            turn(1, 0, 1)
            expert_up(0, 0, 1)
            pe.wait_ge(s_texp, 1)
            end = last_pair(pe, lastp)
            with pe.Fori(0, CAPB // 2 - 1) as j:
                with pe.If(end > j):
                    expert_up(j * 2 + 1, 1, 0)
                    turn(j * 2 + 2, j + 1, 0)
                    expert_down(j * 2, 0)
                    expert_up(j * 2 + 1, 1, 1)
                    expert_up(j * 2 + 2, 0, 0)
                    turn(j * 2 + 3, j + 1, 1)
                    expert_down(j * 2 + 1, 1)
                    expert_up(j * 2 + 2, 0, 1)
            expert_up(end * 2 + 1, 1, 0)
            expert_down(end * 2, 0)
            expert_up(end * 2 + 1, 1, 1)
            expert_down(end * 2 + 1, 1)


def kernel(x, src, dst, edge_attr_64, L0_gnn_W1, L0_gnn_b1, L0_gnn_W2, L0_gnn_b2, L0_gnn_U1, L0_gnn_c1,
           L0_gnn_U2, L0_gnn_c2, L0_mix_wq, L0_mix_wk, L0_mix_wv, L0_mix_wo, L0_mix_bo, L0_mix_ln_k_g,
           L0_mix_ln_k_b, L0_mix_ln_v_g, L0_mix_ln_v_b, L0_ffn_gate_w, L0_ffn_gate_b, L0_ffn_w1,
           L0_ffn_w2, L0_ffn_w3):
    import numpy as np
    import concourse.bacc as bacc
    from concourse.bass_utils import run_bass_kernel_spmd

    def edge_columns(a, fill):
        a = np.pad(np.asarray(a), (0, EP - E), constant_values=fill)
        return np.ascontiguousarray(a.reshape(NG * ET, P).T)

    rbf = np.pad(np.asarray(edge_attr_64), ((0, EP - E), (0, 0)))
    arrays = {
        "x": x,
        "src": edge_columns(src, 0),
        "dst": edge_columns(dst, FAR),
        "first": np.asarray(dst)[::EG].reshape(1, NG),
        "rbf": rbf.reshape(NG, EG, RB).transpose(0, 2, 1),
        "W1": L0_gnn_W1, "b1": np.asarray(L0_gnn_b1).reshape(DC, P).T, "W2": L0_gnn_W2, "b2": L0_gnn_b2,
        "U1": L0_gnn_U1, "c1": np.asarray(L0_gnn_c1).reshape(DC, P).T, "U2": L0_gnn_U2, "c2": L0_gnn_c2,
        "wq": L0_mix_wq,
        "wkvT": np.concatenate([np.asarray(L0_mix_wk).T, np.asarray(L0_mix_wv).T], axis=1),
        "woT": np.asarray(L0_mix_wo).T, "bo": L0_mix_bo,
        "kg": L0_mix_ln_k_g, "kb": L0_mix_ln_k_b, "vg": L0_mix_ln_v_g, "vb": L0_mix_ln_v_b,
        "gw": L0_ffn_gate_w, "gb": L0_ffn_gate_b, "w1": L0_ffn_w1, "w2": L0_ffn_w2, "w3": L0_ffn_w3,
    }
    arrays = {"in_" + k: np.ascontiguousarray(v) for k, v in arrays.items()}
    nc = bacc.Bacc("TRN2", target_bir_lowering=False, num_devices=1)
    args = [nc.dram_tensor(k, v.shape, mybir.dt.from_np(v.dtype), kind="ExternalInput").ap()
            for k, v in arrays.items()]
    out = nc.dram_tensor("out", (N, D), f32, kind="ExternalOutput").ap()
    gps_layer(nc, *args, out)
    r = run_bass_kernel_spmd(nc, [arrays], core_ids=[0])
    return r.results[0]["out"]
```

```python
import concourse.bass as bass
import concourse.mybir as mybir
from contextlib import ExitStack

f32 = mybir.dt.float32
f32r = mybir.dt.float32r
i32 = mybir.dt.int32
ALU = mybir.AluOpType
ACT = mybir.ActivationFunctionType
X = mybir.AxisListType.X

P = 128
N, D, E, RB = 3125, 256, 50000, 64
DC = D // P
NT = -(-N // P)
NP = NT * P
LAST = N - (NT - 1) * P
EG = 512
ET = EG // P
NG = -(-E // EG)
EP = NG * EG
W = 96
FW = 2 * W
NW = -(-NP // FW)
AW = NW * FW
FAR = 1 << 20
HEADS, HD = 4, 64
NX, HF = 16, 512
HC = HF // P
SB = 256
CH = 6
CHUNKS = [(t, t + CH if t + 2 * CH <= NT else NT) for t in range(0, NT - CH, CH)]
NB = -(-NT // 2)
LAG = 8
TC = 5
HALF = 12
KLAG = 8
CAPB = (2 * N - NX) // SB + NX
CAPB += CAPB % 2
LOWP = (2 * N - 1) // (2 * SB)
NS = CAPB * SB // P
PARTS = ((0, 0), (0, 1), (1, 0))
EPS = 1e-5
MAGIC = 1597463007.0


def peeled(i, n):
    return isinstance(i, int) and i == n


def nothing():
    pass


def ds(start, size):
    return bass.ds(start, size)


def in_pairs(eng, n, body):
    with eng.Fori(0, n // 2) as j:
        body(j * 2, j, 0)
        body(j * 2 + 1, j, 1)
    if n % 2:
        body(n - 1, n // 2, 0)


def last_pair(eng, lastp):
    return eng.value_load(lastp[0:1, 0:1], min_val=LOWP - 1, max_val=CAPB // 2 - 2) + 1


def gps_layer(nc, x_d, src_d, dst_d, first_d, rbf_d, W1_d, b1_d, W2_d, b2_d, U1_d, c1_d, U2_d, c2_d,
              wq_d, wkvT_d, woT_d, bo_d, kg_d, kb_d, vg_d, vb_d, gw_d, gb_d, w1_d, w2_d, w3_d, out_d):
    xn_d = nc.dram_tensor("xn_rows", (NP, D), f32).ap()
    xn2_d = nc.dram_tensor("xn2_rows", (NP, D), f32).ap()
    acc_d = nc.dram_tensor("out_rows", (NP + SB, D), f32).ap()

    ctx = ExitStack()
    with ctx:
        def sb(name, shape, dt=f32):
            return ctx.enter_context(nc.sbuf_tensor(name, shape, dt))

        def sem(name):
            return ctx.enter_context(nc.semaphore(name))

        ident = sb("ident", [P, P])
        ones = sb("ones", [P, P])
        before = sb("before", [P, P])
        iota = sb("iota", [P, FW])
        spare = sb("spare", [P, NS])
        valid = sb("valid", [P, 1])
        tok = sb("tok", [P, 2, NT])
        W1 = sb("W1", [P, D])
        b1 = sb("b1", [P, DC])
        W2 = sb("W2", [P, DC, D])
        b2bc = sb("b2bc", [P, 2, D])
        U1 = sb("U1", [P, 2 * DC, D])
        c1 = sb("c1", [P, DC])
        U2 = sb("U2", [P, DC, D])
        cb = sb("cb", [P, 2, D])
        wq = sb("wq", [P, DC, D])
        wkv = sb("wkv", [P, DC, 2 * D])
        woT = sb("woT", [P, DC, D])
        kgb = sb("kgb", [P, 2, P])
        vgb = sb("vgb", [P, 2])
        gw = sb("gw", [P, DC, NX])
        gb = sb("gb", [P, NX])
        x = sb("x_nodes", [P, NT, D])
        xnT = sb("xnT", [P, DC, NP])
        xn = [sb(f"xn{i}", [P, D]) for i in range(2)]
        xt = [sb(f"xt{i}", [P, DC, P]) for i in range(2)]
        st6 = sb("st6", [P, NT, 6])
        mean = sb("mean", [P, NT])
        rstd = sb("rstd", [P, NT])
        v_a = sb("v_a", [P, NT * 8])
        v_b = sb("v_b", [P, NT * 8])
        v_c = sb("v_c", [P, NT * 8])
        ssq = sb("ssq", [P, NT * 8])
        kvr = sb("kvr", [P, NT * 8])
        v_p = sb("v_p", [P, DC * 8])
        M = wkv[:, :, 0:D]
        big = sb("big", [P, NT * 2 * D])

        def part(mem, at, *shape):
            size = 1
            for n in shape:
                size *= n
            ap = mem[:, at:at + size]
            if len(shape) == 3:
                return ap.rearrange("p (a b c) -> p a b c", a=shape[0], b=shape[1])
            return ap if len(shape) == 1 else ap.rearrange("p (a b) -> p a b", a=shape[0])
        kvc = part(big, 0, NT, 2 * D)
        agg = part(big, 0, DC, AW)
        EV = DC * AW
        th = [part(big, EV + ET * D * i, ET, D) for i in range(2)]
        hg = [part(big, EV + ET * D * (2 + i), ET, D) for i in range(2)]
        msg = [part(big, EV + ET * D * (4 + i), ET, D) for i in range(2)]
        fr = sb("fr", [P, 12 * 1024], f32r)
        h1s = [[part(fr, EG * DC * (2 * i + k), DC, EG) for k in range(2)] for i in range(2)]
        rbs = [part(fr, 4096 + EG * i, EG) for i in range(2)]
        W1s = [part(fr, 5120 + D * k, D) for k in range(2)]
        W2s = [part(fr, 5632 + DC * D * k, DC, D) for k in range(2)]
        U1s = [part(fr, 6656 + 1024 * k, 2 * DC, D) for k in range(2)]
        UMs = [part(fr, 8704 + 1024 * k, 2 * DC, D) for k in range(2)]
        xns = [[part(fr, 512 * (2 * i + k), DC, 2 * P) for k in range(2)] for i in range(2)]
        ags = [[part(fr, 2048 + 512 * (2 * i + k), DC, 2 * P) for k in range(2)] for i in range(2)]
        sts = [[part(fr, (4096, 10752)[i] + 512 * k, DC, 2 * P) for k in range(2)] for i in range(2)]
        ws = [[part(fr, 1024 * (2 * r + k), 4, D) for k in range(2)] for r in range(3)]
        xTs = [[part(fr, 6144 + 512 * (2 * i + k), DC, SB) for k in range(2)] for i in range(2)]
        hids = [[part(fr, 8192 + HC * SB * (2 * i + k), HC, SB) for k in range(2)] for i in range(2)]
        srcs = sb("srcs", [P, NG * ET], i32)
        dstf = sb("dstf", [P, NG * ET])
        rel = sb("rel", [P, NG * ET])
        dsti = rel[:, :].bitcast(i32)
        basef = sb("basef", [P, NG])
        basei = sb("basei", [P, NG], i32)
        left_p = sb("left_p", [P, 1])
        flag = sb("flag", [P, 1], i32)
        rbf = [sb(f"rbf{i}", [P, EG]) for i in range(2)]
        cover = rbf[1][:, 0:NG * ET]
        h1f = sb("h1f", [P, DC, EG])
        oh = [sb(f"oh{i}", [P, ET, FW]) for i in range(2)]
        idx = [sb(f"idx{i}", [P, ET], i32) for i in range(2)]

        sq = [h1f[:, i, :] for i in range(2)]
        oflat = [oh[i][:, :, :].rearrange("p s w -> p (s w)") for i in range(2)]
        xt2 = [oflat[i][:, 0:D].rearrange("p (c q) -> p c q", c=DC) for i in range(2)]
        khs = [oflat[i][:, 0:2 * (P + 2)].rearrange("p (j c) -> p j c", j=2) for i in range(2)]
        vhs = [oflat[i][:, 2 * (P + 2):2 * (P + 2) + D] for i in range(2)]
        hflat = h1f[:, :, :].rearrange("p c e -> p (c e)")
        MX = EV + ET * D * 5
        kvt = part(big, MX, DC, P)
        kv_t = part(big, MX + 256, P)
        kv_r = part(big, MX + 384, P)
        A1 = part(big, MX + 512, DC, D)
        kv_s = v_b[:, 0:1]
        sst = [part(hflat, 512 * i, DC, 2 * P) for i in range(2)]
        TX = NT * NX
        lg = part(big, EV, NT, NX)
        ohx = [part(big, EV + TX * (1 + k), NT, NX) for k in range(2)]
        m12 = part(big, EV + TX * 3, NT, NX)
        t_a = part(big, EV + TX * 4, NT, NX)
        t_b = part(big, EV + TX * 5, NT, NX)
        t_et = part(big, EV + TX * 6, NX, NT)
        t_in = part(big, EV + TX * 7, NX, NT)
        t_ex = part(big, EV + TX * 8, NX, NT)
        top = part(big, EV + TX * 9, 2, NT)
        n_e = part(big, EV + TX * 9 + 64, NX)
        c_e = part(big, EV + TX * 9 + 80, NX)
        cend = part(big, EV + TX * 9 + 96, NX)
        off = part(big, EV + TX * 9 + 112, NX)
        c_i = sb("c_i", [P, NX], i32)
        texp_f = part(big, EV + TX * 9 + 128, CAPB)
        tcmp = part(big, EV + TX * 10, CAPB, NX)
        onerow = part(big, EV + TX * 10 + CAPB * NX, TX)
        texp = sb("texp", [P, CAPB], i32)
        lastp = sb("lastp", [P, 1], i32)
        posf = part(big, EV + TX * 6 + 0, 2, NT)
        posi = sb("posi", [P, 2, NT], i32)
        bits = part(big, EV + TX * 6 + 64, 2, NT).bitcast(i32)
        lof = part(big, EV + TX * 6 + 128, 2, NT)
        hif = part(big, EV + TX * 6 + 192, 2, NT)
        wts = sb("wts", [P, 2, NT])
        exw = sb("exw", [P, NT])
        tab = sb("tab", [P, NS], i32)
        dest = sb("dest", [P, NS], i32)
        wslot = sb("wslot", [P, NS])
        tf = [part(big, EV + TX * 3 + 128 * i, NS) for i in range(2)]
        wst = [[part(big, 1024 * (2 * r + i), 4, D) for i in range(2)] for r in range(3)]
        xfl = xnT[:, :, :].rearrange("p c n -> p (c n)")
        tA = [part(xfl, 1024 * i, TC, P) for i in range(2)]
        tB = [part(xfl, 2048 + 1024 * i, TC, 2 * NS) for i in range(2)]
        tE = [part(xfl, 4096 + 512 * i, TC, NS) for i in range(2)]
        xs = [part(xfl, 512 * i, 2, D) for i in range(2)]
        gate = [part(xfl, 1024 + 512 * i, 512) for i in range(2)]
        hidf = [part(xfl, 2048 + 512 * i, 2, SB) for i in range(2)]
        ys = [part(xfl, 3072 + 512 * i, 2, D) for i in range(2)]

        ps = ctx.enter_context(nc.psum_tensor("ps", [P, 8, 512], f32))

        s_par = sem("params_in")
        s_wkv = sem("wkv_in")
        s_cen = sem("wkv_centred")
        s_x = [sem(f"x_in{i}") for i in range(4)]
        s_edge = sem("edge_tables_in")
        s_src = sem("src_in")
        s_const = sem("constants_made")
        s_pc = sem("pool_steps")
        s_xpad = sem("x_padding_zeroed")
        s_dve = sem("vector_steps")
        s_xn = sem("xn_made")
        s_xnst = [sem(f"xn_stored{i}") for i in range(2)]
        s_tp = sem("xn_transposed")
        s_xt = sem("xt_copied")
        s_xnT = sem("xnT_kept")
        s_kv = sem("kv_projected")
        s_kvd = sem("kv_drained")
        s_sq = sem("squares_summed")
        s_kvr = sem("kv_rstd_made")
        s_kh = sem("k_scaled")
        s_vh = sem("v_scaled")
        s_khp = sem("kv_summed")
        s_mx = sem("mix_products")
        s_mv = sem("mix_vector")
        s_rbf = [sem(f"rbf_in{i}") for i in range(2)]
        s_whi = sem("edge_weights_high")
        s_wlow = sem("edge_weights_low")
        s_rhi = sem("rbf_high")
        s_rlo = sem("rbf_low")
        s_hhi = sem("edge_hidden_high")
        s_hlo = sem("edge_hidden_low")
        s_w1 = sem("edge_w1_done")
        s_silu = sem("edge_silu_done")
        s_w2 = sem("edge_w2_done")
        s_zb = sem("edge_bias_added")
        s_th = sem("edge_tanh_done")
        s_idx = sem("src_indices_staged")
        s_hg = [sem(f"src_rows_in{i}") for i in range(2)]
        s_msg = sem("messages_made")
        s_sc = sem("messages_scattered")
        s_aggz = sem("aggregate_zeroed")
        s_agg = sem("window_added")
        s_cov = sem("uncovered_counted")
        s_flag = sem("flag_ready")
        s_gnn = sem("aggregate_done")
        s_xcb = sem("x_plus_biases")
        s_uhi = sem("update_weights_high")
        s_ulo = sem("update_weights_low")
        s_nhi = sem("node_operands_high")
        s_nlo = sem("node_operands_low")
        s_ux = sem("xn_parts_done")
        s_shi = sem("u1_silu_high")
        s_slo = sem("u1_silu_low")
        s_u1 = sem("u1_done")
        s_us = sem("u1_silu_done")
        s_uo = sem("u2_done")
        s_x1 = sem("x1_made")
        s_xn2 = sem("xn2_made")
        s_xn2st = [sem(f"xn2_stored{i}") for i in range(2)]
        s_tp2 = sem("xn2_transposed")
        s_xt2 = sem("xt2_copied")
        s_lg = sem("logits_done")
        s_lgc = sem("logits_copied")
        s_m12 = sem("choices_made")
        s_cnt = sem("choices_counted")
        s_dif = sem("logit_gap_made")
        s_ex = sem("gap_exp_done")
        s_eq = sem("slot_onehots_made")
        s_hot = sem("slot_tokens_made")
        s_hotw = sem("slot_weights_made")
        s_tab = sem("slot_table_done")
        s_tabi = sem("slot_table_kept")
        s_texp = sem("block_experts_ready")
        s_win = [[sem(f"w_in{r}{i}") for i in range(2)] for r in range(3)]
        s_wh = [sem(f"w_high{r}") for r in range(3)]
        s_wlo = [sem(f"w_low{r}") for r in range(3)]
        s_sidx = sem("slot_indices_staged")
        s_xs = [sem(f"slot_rows_in{i}") for i in range(2)]
        s_xsp = sem("slots_transposed")
        s_xhi = sem("slots_high")
        s_xlo = sem("slots_low")
        s_hdh = sem("expert_hidden_high")
        s_hdl = sem("expert_hidden_low")
        s_didx = sem("slot_rows_staged")
        s_h = sem("expert_up_done")
        s_g = sem("expert_silu_done")
        s_hid = sem("expert_hidden_made")
        s_o = sem("expert_down_done")
        s_y = sem("expert_out_copied")
        s_acc = sem("x1_stored")
        s_yst = [sem(f"expert_rows_added{i}") for i in range(2)]
        s_out = sem("out_stored")

        block = ctx.enter_context(nc.Block())
        NPAR = 23

        @block.sync
        def _(sp):
            for k, (a, b) in enumerate(((0, HALF // 2), (HALF // 2, HALF), (HALF, NT - 1))):
                sp.dma_start(x[:, a:b, :], x_d[a * P:b * P, :].rearrange("(t p) d -> p t d", p=P)).then_inc(s_x[k], 16)
            sp.wait_ge(s_xpad, 1)
            sp.dma_start(x[0:LAST, NT - 1, :], x_d[(NT - 1) * P:N, :]).then_inc(s_x[3], 16)
            sp.dma_start(dsti, dst_d).then_inc(s_edge, 16)
            sp.dma_start(basei[:, :], first_d.to_broadcast([P, NG])).then_inc(s_edge, 16)
            sp.dma_start(srcs[:, :], src_d).then_inc(s_src, 16)

            def store_xn(t, j, p):
                sp.wait_ge(s_xn, t + 1)
                sp.dma_start(xn_d[ds(t * P, P), :], xn[p][:, :]).then_inc(s_xnst[p], 16)
            in_pairs(sp, NT, store_xn)

            def edges(n0, h0):
                def load(i, j, p):
                    sp.wait_ge(s_rlo, n0 + i + 1)
                    for half in range(2):
                        sp.dma_start(rbf[p][half * RB:(half + 1) * RB, :],
                                     rbf_d[ds(i, 1), :, :].rearrange("a r e -> (a r) e")).then_inc(s_rbf[p], 16)
                in_pairs(sp, NG, load)
            sp.wait_ge(s_flag, 1)
            edges(0, 0)
            left = sp.value_load(flag[0:1, 0:1], min_val=0, max_val=E)
            with sp.If(left > 0):
                with sp.Fori(0, NW) as w:
                    edges((w + 1) * NG, (w + 1) * (NG // 2))

            for t0, end in CHUNKS:
                if t0:
                    with sp.Fori((t0 - CH) // 2, t0 // 2) as j:
                        for p in range(2):
                            sp.wait_ge(s_xn2, j * 2 + p + 1)
                            sp.dma_start(xn2_d[ds((j * 2 + p) * P, P), :], xn[p][:, :]).then_inc(s_xn2st[p], 16)
                sp.wait_ge(s_x1, (end + 1) // 2 + 2)
                sp.dma_start(acc_d[t0 * P:end * P, :].rearrange("(t p) d -> p t d", p=P), x[:, t0:end, :])\
                    .then_inc(s_acc, 16)
                if t0 == 0:
                    sp.dma_start(acc_d[NP:, :].rearrange("(t p) d -> p t d", p=P), x[:, 0:SB // P, :])\
                        .then_inc(s_acc, 16)
            for t in range(*CHUNKS[-1]):
                sp.wait_ge(s_xn2, t + 1)
                sp.dma_start(xn2_d[t * P:(t + 1) * P, :], xn[t % 2][:, :]).then_inc(s_xn2st[t % 2], 16)

            sp.wait_ge(s_texp, 1)
            def load_w(i, p, first=False):
                e = sp.value_load(texp[0:1, ds(i, 1)], min_val=0, max_val=NX - 1)
                for r in range(3):
                    if not first:
                        sp.wait_ge(s_wlo[r], i - 1)
                    if r < 2:
                        for m, w_d in enumerate((w1_d, w2_d)):
                            sp.dma_start(wst[r][p][:, 2 * m:2 * m + 2, :],
                                         w_d[ds(e, 1), :, r * SB:(r + 1) * SB].rearrange("e (c p) h -> p (e c) h", p=P))\
                                .then_inc(s_win[r][p], 16)
                    else:
                        sp.dma_start(wst[r][p], w3_d[ds(e, 1), :, :].rearrange("e (c p) h -> p (e c) h", p=P))\
                            .then_inc(s_win[r][p], 16)
            load_w(0, 0, True)
            load_w(1, 1, True)
            end = last_pair(sp, lastp)
            with sp.Fori(1, CAPB // 2) as j:
                with sp.If(end > j - 1):
                    load_w(j * 2, 0)
                    load_w(j * 2 + 1, 1)

            for p in range(2):
                sp.wait_ge(s_yst[p], 32 * end + 32)
            sp.dma_start(out_d[:, :], acc_d[0:N, :]).then_inc(s_out, 16)
            sp.wait_ge(s_out, 16)

        @block.gpsimd
        def _(pool):
            steps = [0]

            def link(ins):
                steps[0] += 1
                ins.then_inc(s_pc, 1)
                pool.wait_ge(s_pc, steps[0])

            pool.memset(x[:, NT - 1, :], 0.0).then_inc(s_xpad, 1)
            link(pool.memset(ident[:, :], 0.0))
            link(pool.affine_select(out=ident[:, :], in_=ident[:, :], compare_op=ALU.not_equal, fill=1.0,
                                    base=0, pattern=[[-1, P]], channel_multiplier=1))
            link(pool.memset(ones[:, :], 1.0))
            link(pool.affine_select(out=before[:, :], in_=ones[:, :], compare_op=ALU.is_gt, fill=0.0,
                                    base=0, pattern=[[1, P]], channel_multiplier=-1))
            link(pool.iota(iota[:, :], [[1, FW]], base=0, channel_multiplier=0,
                           allow_small_or_imprecise_dtypes=True))
            link(pool.iota(tok[:, :, :], [[0, 2], [P, NT]], base=1, channel_multiplier=1,
                           allow_small_or_imprecise_dtypes=True))
            link(pool.affine_select(out=tok[:, :, :], in_=tok[:, :, :], compare_op=ALU.is_gt, fill=0.0,
                                    base=N, pattern=[[0, 2], [-P, NT]], channel_multiplier=-1))
            link(pool.affine_select(out=valid[:, :], in_=ones[:, 0:1], compare_op=ALU.is_gt, fill=0.0,
                                    base=LAST, pattern=[[0, 1]], channel_multiplier=-1))
            for p in range(2):
                link(pool.memset(khs[p][:, :, P:P + 2], 1.0))
            link(pool.iota(spare[:, :], [[0, CAPB], [P, SB // P]], base=NP, channel_multiplier=1,
                           allow_small_or_imprecise_dtypes=True))
            pool.sem_inc(s_const, 1)
            pool.sem_inc(s_xnT, 2)

            pool.wait_ge(s_par, 16 * NPAR)
            link(pool.tensor_tensor(cb[:, 0, :], cb[:, 0, :], cb[:, 1, :], ALU.add))

            def low(halves, of):
                return pool.tensor_tensor(halves[1], of, halves[0].bitcast(f32), ALU.subtract)

            def keep(t, p):
                pool.wait_ge(s_xt, t + 1)
                pool.tensor_copy(xnT[:, :, ds(t * P, P)], xt[p][:, :, :]).then_inc(s_xnT, 1)
                pool.wait_ge(s_xn, t + 1)
                pool.tensor_tensor(x[:, ds(t, 1), :], x[:, ds(t, 1), :], cb[:, 0:1, :], ALU.add).then_inc(s_xcb, 1)

            def scale_v(t, p):
                pool.wait_ge(s_kvr, t + 1)
                pool.wait_ge(s_khp, t + 1)
                pool.tensor_tensor(vhs[p].rearrange("p (h d) -> p h d", d=HD),
                                   kvc[:, ds(t, 1), D:2 * D].rearrange("p a (h d) -> p (a h) d", d=HD),
                                   kvr[:, ds(t * 8 + 4, 4)].unsqueeze(2).to_broadcast([P, 4, HD]), ALU.mult)\
                    .then_inc(s_vh, 1)
            with pool.Fori(0, KLAG // 2) as j:
                keep(j * 2, 0)
                keep(j * 2 + 1, 1)
            with pool.Fori(KLAG // 2, NT // 2) as j:
                scale_v(j * 2 - KLAG, 0)
                keep(j * 2, 0)
                scale_v(j * 2 - KLAG + 1, 1)
                keep(j * 2 + 1, 1)
            keep(NT - 1, 0)
            with pool.Fori((NT - 1 - KLAG) // 2, NT // 2) as j:
                scale_v(j * 2, 0)
                scale_v(j * 2 + 1, 1)
            scale_v(NT - 1, 0)

            for p in range(2):
                pool.wait_ge(s_xnst[p], 16 * ((NT + 1 - p) // 2))
            pool.wait_ge(s_src, 16)

            def edges(n0, h0):
                def gather(i, j, p):
                    pool.wait_ge(s_msg, n0 + i + 1)
                    pool.tensor_copy(idx[p][:, :], srcs[:, ds(i * ET, ET)]).then_inc(s_idx, 1)
                    pool.wait_ge(s_src, 16)
                    pool.wait_ge(s_idx, n0 + i + 1)
                    for s in range(ET):
                        pool.indirect_dma_start(hg[p][:, s, :], None, xn_d[:, :],
                                                bass.IndirectOffsetOnAxis(idx[p][:, s:s + 1], 0))\
                            .then_inc(s_hg[p], 16)
                in_pairs(pool, NG, gather)
            pool.wait_ge(s_mx, 1)
            pool.memset(agg, 0.0).then_inc(s_aggz, 1)
            edges(0, 0)
            pool.wait_ge(s_flag, 1)
            left = pool.value_load(flag[0:1, 0:1], min_val=0, max_val=E)
            with pool.If(left > 0):
                with pool.Fori(0, NW) as w:
                    edges((w + 1) * NG, (w + 1) * (NG // 2))

            pool.wait_ge(s_uhi, 2)
            low(U1s, U1[:, :, :])
            low([u[:, 0:DC, :] for u in UMs], U2[:, :, :])
            pool.wait_ge(s_uhi, 3)
            low([u[:, DC:2 * DC, :] for u in UMs], M).then_inc(s_ulo, 1)
            def node_low(v, q, n=2):
                for k, (halves, src) in enumerate(((xns[q], xnT), (ags[q], agg))):
                    pool.wait_ge(s_nhi, v * 2 + k + 1)
                    last = low([h[:, :, 0:n * P] for h in halves], src[:, :, ds(v * 2 * P, n * P)])
                last.then_inc(s_nlo, 1)

            def silu_low(v, q, n=2):
                pool.wait_ge(s_shi, v + 1)
                low([h[:, :, 0:n * P] for h in sts[q]], sst[q][:, :, 0:n * P]).then_inc(s_slo, 1)
            pool.sem_inc(s_slo, 2)
            node_low(0, 0)
            node_low(1, 1)
            silu_low(0, 0)
            node_low(2, 0)
            with pool.Fori(0, NB // 2 - 2) as j:
                silu_low(j * 2 + 1, 1)
                node_low(j * 2 + 3, 1)
                silu_low(j * 2 + 2, 0)
                node_low(j * 2 + 4, 0)
            silu_low(NB - 4, 1)
            node_low(NB - 2, 1)
            silu_low(NB - 3, 0)
            node_low(NB - 1, 0, 1)
            silu_low(NB - 2, 1)
            silu_low(NB - 1, 0, 1)

            def weigh(c, j, p):
                pool.wait_ge(s_eq, c + 1)
                pool.wait_ge(s_tab, c + 1)
                pool.tensor_tensor(tB[p][:, :, NS:2 * NS], tE[p],
                                   wts[:, :, :].rearrange("p k t -> p (k t)")[:, ds(c * TC, TC)].unsqueeze(2)
                                   .to_broadcast([P, TC, NS]), ALU.mult).then_inc(s_hotw, 1)
            in_pairs(pool, 2 * NT // TC, weigh)

            for p in range(2):
                pool.wait_ge(s_xn2st[p], 16 * ((NT + 1 - p) // 2))
            pool.wait_ge(s_tabi, 1)
            def gather_slots(i, p):
                pool.wait_ge(s_xsp, i + 1)
                pool.tensor_copy(idx[p][:, 0:2], tab[:, ds(i * 2, 2)]).then_inc(s_sidx, 1)
                pool.wait_ge(s_tabi, 1)
                pool.wait_ge(s_sidx, i + 1)
                for s in range(2):
                    pool.indirect_dma_start(xs[p][:, s, :], None, xn2_d[:, :],
                                            bass.IndirectOffsetOnAxis(idx[p][:, s:s + 1], 0))\
                        .then_inc(s_xs[p], 16)

            def scatter_slots(i, jp, p):
                pool.wait_ge(s_y, i + 3)
                if not peeled(i, 0):
                    pool.wait_ge(s_yst[1 - p], (jp + p) * 32)
                pool.tensor_copy(idx[p][:, 2:4], dest[:, ds(i * 2, 2)]).then_inc(s_didx, 1)
                pool.wait_ge(s_tabi, 1)
                pool.wait_ge(s_didx, i + 3)
                for s in range(2):
                    pool.indirect_dma_start(acc_d[:, :], bass.IndirectOffsetOnAxis(idx[p][:, 2 + s:3 + s], 0),
                                            ys[p][:, s, :], None, compute_op=ALU.add).then_inc(s_yst[p], 16)
            pool.sem_inc(s_didx, 2)
            for i in range(4):
                gather_slots(i, i % 2)
            pool.wait_ge(s_texp, 1)
            end = last_pair(pool, lastp)
            pool.wait_ge(s_acc, 16 * (len(CHUNKS) + 1))
            gather_slots(4, 0)
            scatter_slots(0, 0, 0)
            gather_slots(5, 1)
            scatter_slots(1, 0, 1)
            with pool.Fori(3, CAPB // 2) as j:
                with pool.If(end > j - 1):
                    gather_slots(j * 2, 0)
                    scatter_slots(j * 2 - 4, j - 2, 0)
                    gather_slots(j * 2 + 1, 1)
                    scatter_slots(j * 2 - 3, j - 2, 1)
            for k in range(2):
                scatter_slots(end * 2 - 2 + 2 * k, end - 1 + k, 0)
                scatter_slots(end * 2 - 1 + 2 * k, end - 1 + k, 1)

        @block.scalar
        def _(act):
            def row(ap, n, parts=P):
                return ap.rearrange("(a n) -> a n", a=1).to_broadcast([parts, n])

            act.dma_start(wkv[:, :, :], wkvT_d.rearrange("(c p) n -> p c n", p=P)).then_inc(s_wkv, 16)
            for dst, src in (
                (W1[0:RB, :], W1_d), (W1[RB:P, :], W1_d), (W2[:, :, :], W2_d.rearrange("(c p) n -> p c n", p=P)),
                (b1[:, :], b1_d),
                (c1[:, :], c1_d),
                (b2bc[:, 0, :], row(b2_d, D)), (b2bc[:, 1, :], row(b2_d, D)),
                (U1[:, :, :], U1_d.rearrange("(c p) n -> p c n", p=P)),
                (U2[:, :, :], U2_d.rearrange("(c p) n -> p c n", p=P)),
                (wq[:, :, :], wq_d.rearrange("(c p) n -> p c n", p=P)),
                (woT[:, :, :], woT_d.rearrange("(c p) n -> p c n", p=P)),
                (cb[:, 0, :], row(c2_d, D)), (cb[:, 1, :], row(bo_d, D)),
                (kgb[:, 0, 0:HD], row(kg_d, HD)), (kgb[:, 0, HD:P], row(kg_d, HD)),
                (kgb[:, 1, 0:HD], row(kb_d, HD)), (kgb[:, 1, HD:P], row(kb_d, HD)),
                (vgb[0:HD, 0:1], vg_d.rearrange("(n a) -> n a", a=1)),
                (vgb[HD:P, 0:1], vg_d.rearrange("(n a) -> n a", a=1)),
                (vgb[0:HD, 1:2], vb_d.rearrange("(n a) -> n a", a=1)),
                (vgb[HD:P, 1:2], vb_d.rearrange("(n a) -> n a", a=1)),
                (gw[:, :, :], gw_d.rearrange("(c p) n -> p c n", p=P)), (gb[:, :], row(gb_d, NX)),
            ):
                act.dma_start(dst, src).then_inc(s_par, 16)

            act.sem_inc(s_kvd, 2)
            def copy_xt(t, p):
                act.wait_ge(s_tp, t + 3)
                act.wait_ge(s_xnT, t + 1)
                act.wait_ge(s_kv, t + 1)
                act.copy(xt[p][:, :, :], ps[:, p, 0:D].rearrange("p (c q) -> p c q", c=DC)).then_inc(s_xt, 1)

            def drain_kv(t, j, p):
                act.wait_ge(s_kv, t + 3)
                act.copy(kvc[:, ds(t, 1), :].rearrange("p a c -> p (a c)"), ps[:, 2 + p, :])
                act.wait_ge(s_sq, t + 1)
                act.activation(sq[p], ps[:, 2 + p, :], ACT.Square).then_inc(s_kvd, 1)
            copy_xt(0, 0)
            with act.Fori(0, NT // 2) as j:
                copy_xt(j * 2 + 1, 1)
                drain_kv(j * 2, j, 0)
                copy_xt(j * 2 + 2, 0)
                drain_kv(j * 2 + 1, j, 1)
            drain_kv(NT - 1, NT // 2, 0)

            act.wait_ge(s_par, 16 * NPAR)
            for dst, src in ((W1s[0], W1[:, :]), (W2s[0], W2[:, :, :])):
                act.copy(dst, src).then_inc(s_whi, 1)
            for dst, src in ((U1s[0], U1[:, :, :]), (UMs[0][:, 0:DC, :], U2[:, :, :])):
                act.copy(dst, src).then_inc(s_uhi, 1)
            act.sem_inc(s_silu, 4)
            act.wait_ge(s_sq, NT + 2)
            def edges(n0, h0):
                def rbf_high(i, j, p):
                    act.wait_ge(s_rbf[p], (h0 + j + 1) * 32)
                    act.wait_ge(s_w1, (n0 + i) * 2 + 2)
                    act.copy(rbs[p], rbf[p][:, :]).then_inc(s_rhi, 1)

                def silu(i, p):
                    act.wait_ge(s_hlo, n0 + i + 1)
                    for m in range(DC):
                        act.wait_ge(s_w1, (n0 + i) * 2 + 5 + m)
                        act.activation(h1f[:, m, :], ps[:, 6 * p + m, :], ACT.Silu, bias=b1[:, m:m + 1]).then_inc(s_silu, 1)
                    act.wait_ge(s_w2, (n0 + i) * 2 + 2)
                    act.wait_ge(s_silu, (n0 + i) * 2 + 6)
                    act.copy(h1s[p][0], h1f[:, :, :]).then_inc(s_hhi, 1)

                def tanh(i, p):
                    act.wait_ge(s_zb, (n0 + i) * 2 + 4)
                    act.activation(th[p], th[p], ACT.Tanh, scale=0.5).then_inc(s_th, 1)
                rbf_high(0, 0, 0)
                rbf_high(1, 0, 1)
                silu(0, 0)
                rbf_high(2, 1, 0)
                silu(1, 1)
                with act.Fori(0, NG // 2 - 2) as j:
                    tanh(j * 2, 0)
                    rbf_high(j * 2 + 3, j + 1, 1)
                    silu(j * 2 + 2, 0)
                    tanh(j * 2 + 1, 1)
                    rbf_high(j * 2 + 4, j + 2, 0)
                    silu(j * 2 + 3, 1)
                tanh(NG - 4, 0)
                rbf_high(NG - 1, NG // 2 - 1, 1)
                silu(NG - 2, 0)
                tanh(NG - 3, 1)
                silu(NG - 1, 1)
                tanh(NG - 2, 0)
                tanh(NG - 1, 1)
            edges(0, 0)
            act.wait_ge(s_flag, 1)
            left = act.value_load(flag[0:1, 0:1], min_val=0, max_val=E)
            with act.If(left > 0):
                with act.Fori(0, NW) as w:
                    edges((w + 1) * NG, (w + 1) * (NG // 2))

            act.copy(UMs[0][:, DC:2 * DC, :], M).then_inc(s_uhi, 1)
            act.sem_inc(s_us, 2)
            def node_high(v, q, n=2, parts=(0, 1)):
                act.wait_ge(s_ux, v + 1)
                for k in parts:
                    act.copy((xns, ags)[k][q][0][:, :, 0:n * P], (xnT, agg)[k][:, :, ds(v * 2 * P, n * P)])\
                        .then_inc(s_nhi, 1)

            def u1_silu(v, q, n=2):
                act.wait_ge(s_u1, v + 1)
                act.wait_ge(s_slo, v + 1)
                for m in range(DC):
                    last = act.activation(sst[q][:, m, 0:n * P], ps[:, q, m * 2 * P:m * 2 * P + n * P], ACT.Silu,
                                          bias=c1[:, m:m + 1])
                last.then_inc(s_us, 1)
                act.wait_ge(s_us, v + 3)
                act.wait_ge(s_uo, v + 1)
                act.copy(sts[q][0][:, :, 0:n * P], sst[q][:, :, 0:n * P]).then_inc(s_shi, 1)

            def copy_xt2(t, p):
                act.wait_ge(s_tp2, t + 3)
                act.wait_ge(s_lg, t + 1)
                act.copy(xt2[p], ps[:, 6 + p, 0:D].rearrange("p (c q) -> p c q", c=DC)).then_inc(s_xt2, 1)

            def copy_lg(t, p):
                act.wait_ge(s_lg, t + 3)
                act.copy(lg[:, ds(t, 1), :].rearrange("p a n -> p (a n)"), ps[:, 6 + p, D:D + NX]).then_inc(s_lgc, 1)

            def keep_xn2(t, more=lambda: None, first=False):
                if not first:
                    copy_lg(t - 2, 0)
                    copy_lg(t - 1, 1)
                more()
                copy_xt2(t, 0)
                copy_xt2(t + 1, 1)
            act.sem_inc(s_lgc, 2)
            act.wait_ge(s_w1, 2 * NG + 4)
            act.wait_ge(s_w2, 2 * NG + 4)
            node_high(0, 0, parts=(0,))
            act.wait_ge(s_gnn, 1)
            node_high(0, 0, parts=(1,))
            node_high(1, 1)
            u1_silu(0, 0)
            node_high(2, 0)
            with act.Fori(0, LAG // 4) as j:
                u1_silu(j * 2 + 1, 1)
                node_high(j * 2 + 3, 1)
                u1_silu(j * 2 + 2, 0)
                node_high(j * 2 + 4, 0)
            for v in range(LAG // 2, NB - 1):
                u1_silu(v + 1, 1 - v % 2, 1 if v + 1 == NB - 1 else 2)
                keep_xn2(v * 2 - LAG, lambda: node_high(v + 3, 1 - v % 2, 1 if v + 3 == NB - 1 else 2)
                         if v + 3 < NB else None, first=v * 2 == LAG)
            with act.Fori((NT - LAG) // 2, NT // 2) as j:
                keep_xn2(j * 2)
            copy_lg(NT - 3, 0)
            copy_lg(NT - 2, 1)
            copy_xt2(NT - 1, 0)
            copy_lg(NT - 1, 0)

            act.wait_ge(s_dif, 1)
            act.activation(exw[:, :], exw[:, :], ACT.Exp).then_inc(s_ex, 1)

            act.sem_inc(s_y, 2)
            def w_high(r, i, j, p, first=False):
                act.wait_ge(s_win[r][p], (j + 1) * (32 if r < 2 else 16))
                if not first:
                    act.wait_ge(*((s_h, i * 4 + 4 + 2 * r + 2) if r < 2 else (s_o, i + 2)))
                act.copy(ws[r][0], wst[r][p]).then_inc(s_wh[r], 1)

            def slots_high(i, p):
                act.wait_ge(s_xsp, i + 3)
                act.wait_ge(s_h, i * 4 + 4)
                act.copy(xTs[p][0], ps[:, 7, :].rearrange("p (c q) -> p c q", c=DC)).then_inc(s_xhi, 1)

            def silu_g(i, q):
                act.wait_ge(s_h, i * 4 + 8 + 2 * q + 1)
                act.wait_ge(s_hid, i * 2 + q + 1)
                act.activation(gate[q], ps[:, q, :], ACT.Silu).then_inc(s_g, 1)

            def hid_high(i, p, q):
                act.wait_ge(s_hid, i * 2 + q + 3)
                act.wait_ge(s_o, i + 1)
                act.copy(hids[p][0][:, 2 * q:2 * q + 2, :], hidf[q]).then_inc(s_hdh, 1)

            def copy_y(i, j, p):
                act.wait_ge(s_o, i + 3)
                if not peeled(i, p):
                    act.wait_ge(s_yst[p], j * 32)
                for s in range(2):
                    last = act.activation(ys[p][:, s, :], ps[:, 4 + p, s * D:(s + 1) * D], ACT.Copy,
                                          scale=wslot[:, ds(i * 2 + s, 1)])
                last.then_inc(s_y, 1)

            def block_steps(i, j, p, jn, last=False):
                silu_g(i, 0)
                if not last:
                    w_high(0, i + 1, jn, 1 - p)
                    slots_high(i + 1, 1 - p)
                hid_high(i, p, 0)
                w_high(2, i, j, p, first=peeled(i, 0))
                if not peeled(i, 0):
                    copy_y(i - 1, jn - 1, 1 - p)
                silu_g(i, 1)
                hid_high(i, p, 1)
                if not last:
                    w_high(1, i + 1, jn, 1 - p)
            w_high(0, 0, 0, 0, True)
            slots_high(0, 0)
            w_high(1, 0, 0, 0, True)
            block_steps(0, 0, 0, 0)
            block_steps(1, 0, 1, 1)
            block_steps(2, 1, 0, 1)
            block_steps(3, 1, 1, 2)
            act.wait_ge(s_texp, 1)
            end = last_pair(act, lastp)
            with act.Fori(2, CAPB // 2 - 1) as j:
                with act.If(end > j):
                    block_steps(j * 2, j, 0, j)
                    block_steps(j * 2 + 1, j, 1, j + 1)
            block_steps(end * 2, end, 0, end)
            block_steps(end * 2 + 1, end, 1, end + 1, last=True)
            copy_y(end * 2 + 1, end, 1)

        @block.vector
        def _(dve):
            steps = [0]

            def link(ins):
                steps[0] = steps[0] + 1
                ins.then_inc(s_dve, 1)
                dve.wait_ge(s_dve, steps[0])

            def rsqrt(y, v, a, b):
                link(dve.tensor_scalar(a.bitcast(i32), v.bitcast(i32), 1, None, ALU.arith_shift_right))
                link(dve.tensor_scalar(y.bitcast(i32), a.bitcast(i32), -1.0, MAGIC, ALU.mult, ALU.add))
                for _ in range(3):
                    link(dve.tensor_tensor(a, y, y, ALU.mult))
                    link(dve.scalar_tensor_tensor(b, a, -0.5, v, ALU.mult, ALU.mult))
                    link(dve.scalar_tensor_tensor(y, b, 1.5, y, ALU.add, ALU.mult))

            def layer_stats(t, n):
                a, b, v = v_a[:, 0:n], v_b[:, 0:n], v_c[:, 0:n]
                q = slice(t, t + n)
                link(dve.tensor_tensor(a, st6[:, q, 1], st6[:, q, 4], ALU.add))
                link(dve.tensor_scalar(mean[:, q], a, 0.5, None, ALU.mult))
                link(dve.tensor_tensor(a, st6[:, q, 1], st6[:, q, 4], ALU.subtract))
                link(dve.tensor_tensor(b, a, a, ALU.mult))
                link(dve.tensor_tensor(a, st6[:, q, 2], st6[:, q, 5], ALU.add))
                link(dve.tensor_scalar(b, b, 0.25, EPS, ALU.mult, ALU.add))
                link(dve.scalar_tensor_tensor(v, a, 1.0 / D, b, ALU.mult, ALU.add))
                rsqrt(rstd[:, q], v, a, b)

            def stats(t):
                return dve.bn_stats(st6[:, t, :], x[:, t, :])

            for k in range(2):
                dve.wait_ge(s_x[k], 16)
                for t in range(k * HALF // 2, (k + 1) * HALF // 2):
                    last = stats(t)
            link(last)
            layer_stats(0, HALF)

            def make_xn(t, j, p, ready, stored, used):
                if j > 0:
                    dve.wait_ge(stored[p], j * 16)
                dve.wait_ge(used, t + 1)
                dve.tensor_scalar(xn[p][:, :], x[:, t, :], mean[:, t:t + 1], rstd[:, t:t + 1],
                                  ALU.subtract, ALU.mult).then_inc(ready, 1)

            def centre_wkv():
                dve.wait_ge(s_wkv, 16)
                heads = wkv[:, :, :].rearrange("p c (h d) -> p (c h) d", d=HD)
                link(dve.tensor_reduce(v_p[:, :], heads, X, ALU.add))
                link(dve.tensor_scalar(v_p[:, :], v_p[:, :], 1.0 / HD, None, ALU.mult))
                link(dve.tensor_tensor(heads, heads, v_p[:, :].unsqueeze(2).to_broadcast([P, DC * 8, HD]), ALU.subtract))
                dve.sem_inc(s_cen, 1)

            def sum_sq(t, p):
                dve.wait_ge(s_kvd, t + 3)
                dve.tensor_reduce(ssq[:, t * 8:t * 8 + 8], sq[p].rearrange("p (h d) -> p h d", d=HD), X, ALU.add)\
                    .then_inc(s_sq, 1)

            def kv_rstd(a, b):
                dve.wait_ge(s_sq, b + 2)
                q, n = slice(a * 8, b * 8), (b - a) * 8
                link(dve.tensor_scalar(v_c[:, 0:n], ssq[:, q], 1.0 / HD, EPS, ALU.mult, ALU.add))
                rsqrt(kvr[:, q], v_c[:, 0:n], v_a[:, 0:n], v_b[:, 0:n])
                dve.sem_inc(s_kvr, b - a)

            def scale_k(t, p):
                dve.wait_ge(s_khp, t + 1)
                dve.tensor_tensor(khs[p][:, :, 0:P].rearrange("p j (h d) -> p j h d", d=HD),
                                  kvc[:, t, 0:D].rearrange("p (j h d) -> p j h d", j=2, d=HD),
                                  kvr[:, t * 8:t * 8 + 4].rearrange("p (j h) -> p j h", j=2).unsqueeze(3)
                                  .to_broadcast([P, 2, 2, HD]), ALU.mult).then_inc(s_kh, 1)

            def edge_tables():
                dve.wait_ge(s_edge, 32)
                link(dve.tensor_copy(dstf[:, :], dsti))
                link(dve.tensor_copy(basef[:, :], basei[:, :]))
                link(dve.tensor_scalar(basef[:, :], basef[:, :], 0.0, float(AW - W), ALU.max, ALU.min))
                link(dve.tensor_copy(basei[:, :], basef[:, :]))
                link(dve.tensor_tensor(rel[:, :].rearrange("p (g s) -> p g s", s=ET),
                                       dstf[:, :].rearrange("p (g s) -> p g s", s=ET),
                                       basef[:, :].unsqueeze(2).to_broadcast([P, NG, ET]), ALU.subtract))
                link(dve.tensor_scalar(cover, rel[:, :], 0.0, None, ALU.is_ge))
                link(dve.scalar_tensor_tensor(cover, rel[:, :], float(W), cover, ALU.is_lt, ALU.mult))

            def edges_left():
                link(dve.scalar_tensor_tensor(cover, dstf[:, :], 1.0, cover, ALU.add, ALU.mult))
                link(dve.tensor_tensor(dstf[:, :], dstf[:, :], cover, ALU.subtract))
                link(dve.tensor_scalar(cover, dstf[:, :], 0.0, None, ALU.is_ge))
                link(dve.scalar_tensor_tensor(cover, dstf[:, :], float(N), cover, ALU.is_lt, ALU.mult))
                link(dve.tensor_reduce(left_p[:, :], cover, X, ALU.add))
                dve.sem_inc(s_cov, 1)

            dve.sem_inc(s_sq, 2)
            dve.sem_inc(s_rlo, 2)
            dve.sem_inc(s_hlo, 1)
            dve.sem_inc(s_zb, 2)
            dve.sem_inc(s_msg, 2)
            dve.sem_inc(s_agg, 2)
            dve.wait_ge(s_const, 1)
            for t in range(NT + KLAG):
                p = t % 2
                if t < NT:
                    make_xn(t, t // 2, p, s_xn, s_xnst, s_tp)
                if t == 1:
                    centre_wkv()
                if t == 10:
                    edge_tables()
                if t == 16:
                    edges_left()
                if t < (NT - 1 - HALF) // 2:
                    if t == 0:
                        dve.wait_ge(s_x[2], 16)
                    stats(HALF + 2 * t)
                    stats(HALF + 2 * t + 1)
                if t == (NT - 1 - HALF) // 2:
                    dve.wait_ge(s_x[3], 16)
                    link(stats(NT - 1))
                    layer_stats(HALF, NT - HALF)
                if 2 <= t < NT + 2:
                    sum_sq(t - 2, p)
                if t in (CH + 1, 2 * CH + 1, 3 * CH + 1):
                    kv_rstd(t - 1 - CH, t - 1)
                if t == NT + 1:
                    dve.wait_ge(s_cov, 2)
                    dve.tensor_copy(flag[:, :], ps[:, 7, 0:1]).then_inc(s_flag, 1)
                    kv_rstd(3 * CH, NT)
                if t >= KLAG:
                    scale_k(t - KLAG, p)
                if t == NT + 3:
                    dve.wait_ge(s_whi, 2)
                    dve.tensor_tensor(W1s[1], W1[:, :], W1s[0].bitcast(f32), ALU.subtract)
                    dve.tensor_tensor(W2s[1], W2[:, :, :], W2s[0].bitcast(f32), ALU.subtract).then_inc(s_wlow, 1)




            def mix_kv():
                dve.wait_ge(s_mx, 1)
                link(dve.memset(kvt, 0.0))
                for c in range(DC):
                    link(dve.tensor_copy(kv_s, ps[:, 4 + c, P:P + 1]))
                    link(dve.tensor_tensor(kv_t, ps[:, 4 + c, 0:P], kgb[:, 0, :], ALU.mult))
                    link(dve.scalar_tensor_tensor(kv_t, kgb[:, 1, :], kv_s, kv_t, ALU.mult, ALU.add))
                    link(dve.tensor_tensor(kv_r, ps[:, 6, c * P:(c + 1) * P], kgb[:, 0, :], ALU.mult))
                    link(dve.scalar_tensor_tensor(kv_r, kgb[:, 1, :], float(N), kv_r, ALU.mult, ALU.add))
                    link(dve.tensor_scalar(kv_t, kv_t, vgb[:, 0:1], None, ALU.mult))
                    for h in range(2):
                        q = slice(h * HD, (h + 1) * HD)
                        link(dve.scalar_tensor_tensor(kvt[q, c, q], kv_r[q, :][:, q], vgb[q, 1:2], kv_t[q, :][:, q],
                                                      ALU.mult, ALU.add))
                dve.sem_inc(s_mv, 1)

            def mix_a1():
                dve.wait_ge(s_mx, 2)
                link(dve.tensor_copy(A1, ps[:, 4, :].rearrange("p (c n) -> p c n", c=DC)))
                dve.sem_inc(s_mv, 1)

            def mix_m():
                dve.wait_ge(s_mx, 3)
                link(dve.tensor_scalar(M, ps[:, 5, :].rearrange("p (c n) -> p c n", c=DC), 1.0 / N, None, ALU.mult))
                for c in range(DC):
                    q = slice(c * P, (c + 1) * P)
                    link(dve.tensor_tensor(M[:, c, q], M[:, c, q], ident[:, :], ALU.add))
                dve.sem_inc(s_mv, 1)
                dve.wait_ge(s_aggz, 1)

            def edges(n0, h0, w_n, base, rel_t, mix=(nothing, nothing, nothing)):
                def rbf_low(i, p):
                    dve.wait_ge(s_rhi, n0 + i + 1)
                    q = slice(RB, P)
                    dve.tensor_tensor(rbs[p][q, :], rbf[p][q, :], rbs[p][q, :].bitcast(f32), ALU.subtract)\
                        .then_inc(s_rlo, 1)

                def h1_low(i, p):
                    dve.wait_ge(s_hhi, n0 + i + 1)
                    dve.tensor_tensor(h1s[p][1], h1f[:, :, :], h1s[p][0].bitcast(f32), ALU.subtract).then_inc(s_hlo, 1)

                def bias(i, p):
                    for b in range(2):
                        dve.wait_ge(s_w2, (n0 + i) * 2 + 5 + b)
                        dve.tensor_tensor(th[p][:, 2 * b:2 * b + 2, :],
                                          ps[:, 2 + b, :].rearrange("p (s d) -> p s d", s=2),
                                          b2bc[:, :, :], ALU.add).then_inc(s_zb, 1)

                def onehot(i, p):
                    dve.wait_ge(s_sc, n0 + i + 1)
                    dve.tensor_tensor(oh[p][:, :, 0:w_n], iota[:, 0:w_n].unsqueeze(1).to_broadcast([P, ET, w_n]),
                                      rel_t[:, ds(i * ET, ET)].unsqueeze(2).to_broadcast([P, ET, w_n]), ALU.is_equal)

                def message(i, j, p):
                    dve.wait_ge(s_th, n0 + i + 1)
                    dve.wait_ge(s_hg[p], (h0 + j + 1) * (16 * ET))
                    dve.scalar_tensor_tensor(msg[p], th[p], 1.0, hg[p], ALU.add, ALU.mult)\
                        .then_inc(s_msg, 1)

                def add_window(i, p):
                    at = base(i)
                    dve.wait_ge(s_sc, n0 + i + 3)
                    dve.wait_ge(s_agg, n0 + i + 2)
                    a = agg[:, :, ds(at, w_n)]
                    dve.scalar_tensor_tensor(a, ps[:, 4 + p, 0:DC * w_n].rearrange("p (c w) -> p c w", c=DC), 0.5,
                                             a, ALU.mult, ALU.add).then_inc(s_agg, 1)

                def step(i, j, p, after=3, first=False):
                    bias(i, p)
                    if after > 0:
                        h1_low(i + 1, 1 - p)
                    message(i, j, p)
                    if after > 2:
                        rbf_low(i + 3, 1 - p)
                    if not first:
                        add_window(i - 1, 1 - p)
                    if after > 0:
                        onehot(i + 1, 1 - p)
                rbf_low(0, 0)
                rbf_low(1, 1)
                mix[0]()
                h1_low(0, 0)
                mix[1]()
                rbf_low(2, 0)
                onehot(0, 0)
                step(0, 0, 0, first=True)
                mix[2]()
                step(1, 0, 1)
                with dve.Fori(1, NG // 2 - 2) as j:
                    step(j * 2, j, 0)
                    step(j * 2 + 1, j, 1)
                for i in range(NG - 4, NG):
                    step(i, i // 2, i % 2, after=NG - 1 - i)
                add_window(NG - 1, 1)
            edges(0, 0, W, lambda i: dve.value_load(basei[0:1, ds(i, 1)], min_val=0, max_val=AW - W), rel,
                  (mix_kv, mix_a1, mix_m))
            left = dve.value_load(flag[0:1, 0:1], min_val=0, max_val=E)
            with dve.If(left > 0):
                with dve.Fori(0, NW) as w:
                    edges((w + 1) * NG, (w + 1) * (NG // 2), FW, lambda i: w * FW, dstf)
                    dve.tensor_scalar(dstf[:, :], dstf[:, :], float(FW), None, ALU.subtract).then_inc(s_cov, 1)
                    dve.wait_ge(s_cov, w + 3)
            link(dve.tensor_copy(v_a[:, 0:1], agg[:, 0, 0:1]))
            dve.sem_inc(s_gnn, 1)

            dve.wait_ge(s_xcb, NT)
            dve.sem_inc(s_x1, 2)
            def x1(v, q, n):
                dve.wait_ge(s_uo, v + 3)
                xr = x[:, 2 * v:2 * v + n, :]
                dve.tensor_tensor(xr, ps[:, 2 + 2 * q:2 + 2 * q + n, 0:D], xr, ALU.add).then_inc(s_x1, 1)

            def xn2(t, j, p):
                make_xn(t, j, p, s_xn2, s_xn2st, s_tp2)

            def top2(a, b):
                q, n = slice(a, b), b - a
                shape = [P, n, NX]
                io = iota[:, 0:NX].unsqueeze(1).to_broadcast(shape)
                dve.wait_ge(s_lgc, b + 2)
                link(dve.tensor_tensor(lg[:, q, :], lg[:, q, :], gb[:, :].unsqueeze(1).to_broadcast(shape), ALU.add))
                for k in range(2):
                    m = top[:, k, q]
                    link(dve.tensor_reduce(m, lg[:, q, :], X, ALU.max))
                    link(dve.tensor_tensor(t_a[:, q, :], lg[:, q, :], m.unsqueeze(2).to_broadcast(shape), ALU.is_equal))
                    link(dve.scalar_tensor_tensor(t_a[:, q, :], t_a[:, q, :], -float(NX), io, ALU.mult, ALU.add))
                    link(dve.tensor_reduce(v_a[:, 0:n], t_a[:, q, :], X, ALU.min))
                    link(dve.tensor_tensor(ohx[k][:, q, :], t_a[:, q, :],
                                           v_a[:, 0:n].unsqueeze(2).to_broadcast(shape), ALU.is_equal))
                    if k == 0:
                        link(dve.scalar_tensor_tensor(lg[:, q, :], ohx[0][:, q, :], -3e38, lg[:, q, :],
                                                      ALU.mult, ALU.add))

            for c, (t0, end) in enumerate(CHUNKS):
                for t in range(t0, end, 2):
                    n = min(2, end - t)
                    x1(t // 2, t // 2 % 2, n)
                    if t0 and t < t0 + CH:
                        for k in range(2):
                            xn2(t + k - CH, (t - CH) // 2, k)
                    if t == t0 + 2 and c >= 2:
                        top2(*CHUNKS[c - 2])
                    dve.wait_ge(s_x1, t // 2 + 3)
                    for k in range(n):
                        last = stats(t + k)
                link(last)
                layer_stats(t0, end - t0)
            for t in range(*CHUNKS[-1]):
                xn2(t, t // 2, t % 2)
            link(dve.memset(onerow, 1.0))
            top2(CHUNKS[-2][0], NT)

            link(dve.tensor_tensor(exw[:, :], top[:, 1, :], top[:, 0, :], ALU.subtract))
            dve.sem_inc(s_dif, 1)
            for k in range(2):
                link(dve.tensor_scalar(ohx[k][:, NT - 1, :], ohx[k][:, NT - 1, :], valid[:, 0:1], None, ALU.mult))
            link(dve.tensor_tensor(m12, ohx[0], ohx[1], ALU.add))
            dve.sem_inc(s_m12, 1)
            dve.wait_ge(s_ex, 1)
            link(dve.tensor_scalar(v_a[:, 0:NT], exw[:, :], 1.0, None, ALU.add))
            link(dve.reciprocal(wts[:, 0, :], v_a[:, 0:NT]))
            link(dve.tensor_tensor(wts[:, 1, :], wts[:, 0, :], exw[:, :], ALU.mult))
            link(dve.tensor_scalar(wts[:, :, NT - 1], wts[:, :, NT - 1], valid[:, 0:1], None, ALU.mult))

            dve.wait_ge(s_cnt, 1)
            link(dve.tensor_copy(t_et, ps[:, 1, 0:TX].rearrange("p (t e) -> p e t", e=NX)))
            ff = lambda ap: ap.rearrange("p a b -> p (a b)")
            link(dve.tensor_tensor_scan(ff(t_in), onerow, ff(t_et), 0.0, ALU.mult, ALU.add))
            link(dve.tensor_tensor(t_ex, t_in, t_et, ALU.subtract))
            link(dve.tensor_tensor(n_e, t_in[:, :, NT - 1], t_ex[:, :, 0], ALU.subtract))
            link(dve.tensor_scalar(c_i[:, :], n_e, float(SB - 1), None, ALU.add))
            link(dve.tensor_scalar(c_i[:, :], c_i[:, :], SB.bit_length() - 1, None, ALU.arith_shift_right))
            link(dve.tensor_copy(c_e, c_i[:, :]))
            link(dve.tensor_tensor_scan(cend, onerow[:, 0:NX], c_e, 0.0, ALU.mult, ALU.add))
            link(dve.tensor_tensor(off, cend, c_e, ALU.subtract))
            link(dve.scalar_tensor_tensor(off, off, float(SB), t_ex[:, :, 0], ALU.mult, ALU.subtract))
            link(dve.tensor_tensor(t_a, t_ex.rearrange("p e t -> p t e"),
                                   off.unsqueeze(1).to_broadcast([P, NT, NX]), ALU.add))
            link(dve.tensor_tensor(t_a, ps[:, 0, 0:TX].rearrange("p (t e) -> p t e", e=NX), t_a, ALU.add))
            for k in range(2):
                link(dve.tensor_tensor(t_b, ohx[k], t_a, ALU.mult))
                link(dve.tensor_reduce(posf[:, k, :], t_b, X, ALU.add))
            link(dve.tensor_copy(posi[:, :, :], posf))
            link(dve.tensor_scalar(bits, posi[:, :, :], P - 1, None, ALU.bitwise_and))
            link(dve.tensor_copy(lof, bits))
            link(dve.tensor_scalar(bits, posi[:, :, :], 7, None, ALU.arith_shift_right))
            link(dve.tensor_copy(hif, bits))
            link(dve.tensor_tensor(tcmp, cend.unsqueeze(1).to_broadcast([P, CAPB, NX]),
                                   iota[:, 0:CAPB].unsqueeze(2).to_broadcast([P, CAPB, NX]), ALU.is_le))
            link(dve.tensor_reduce(texp_f, tcmp, X, ALU.add))
            link(dve.tensor_scalar(texp[:, :], texp_f, float(NX - 1), None, ALU.min))
            link(dve.tensor_scalar(lastp[:, :], cend[:, NX - 1:NX], -3.0, None, ALU.add))
            dve.tensor_scalar(lastp[:, :], lastp[:, :], 1, None, ALU.arith_shift_right).then_inc(s_texp, 1)

            def onehots(c, j, p):
                def each(ap, n):
                    return ap.rearrange("p k t -> p (k t)")[:, ds(c * TC, TC)].unsqueeze(2).to_broadcast([P, TC, n])
                dve.wait_ge(s_tab, c + 1)
                dve.tensor_tensor(tE[p], iota[:, 0:NS].unsqueeze(1).to_broadcast([P, TC, NS]), each(hif, NS),
                                  ALU.is_equal).then_inc(s_eq, 1)
                dve.tensor_tensor(tA[p], iota[:, 0:P].unsqueeze(1).to_broadcast([P, TC, P]), each(lof, P), ALU.is_equal)
                dve.wait_ge(s_eq, c + 1)
                dve.tensor_tensor(tB[p][:, :, 0:NS], tE[p], each(tok[:, :, :], NS), ALU.mult).then_inc(s_hot, 1)
            in_pairs(dve, 2 * NT // TC, onehots)
            dve.wait_ge(s_tab, 2 * NT // TC + 2)
            held, row = tf
            link(dve.tensor_copy(wslot[:, :], ps[:, 2, NS:2 * NS]))
            link(dve.tensor_scalar(held, ps[:, 2, 0:NS], 1.0, None, ALU.is_ge))
            link(dve.tensor_tensor(row, ps[:, 2, 0:NS], held, ALU.subtract))
            link(dve.tensor_copy(tab[:, :], row))
            link(dve.tensor_tensor(row, row, spare[:, :], ALU.subtract))
            link(dve.tensor_tensor(row, row, held, ALU.mult))
            link(dve.tensor_tensor(dest[:, :], row, spare[:, :], ALU.add))
            dve.sem_inc(s_tabi, 1)

            dve.sem_inc(s_hid, 2)
            dve.sem_inc(s_xlo, 1)
            def w_low(r, i, p):
                dve.wait_ge(s_wh[r], i + 1)
                dve.tensor_tensor(ws[r][1], wst[r][p], ws[r][0].bitcast(f32), ALU.subtract).then_inc(s_wlo[r], 1)

            def slots_low(i, p):
                dve.wait_ge(s_xhi, i + 1)
                dve.tensor_tensor(xTs[p][1], ps[:, 7, :].rearrange("p (c q) -> p c q", c=DC),
                                  xTs[p][0].bitcast(f32), ALU.subtract).then_inc(s_xlo, 1)

            def hidden(i, p, q):
                dve.wait_ge(s_h, i * 4 + 8 + 2 * q + 2)
                dve.wait_ge(s_g, i * 2 + q + 1)
                dve.tensor_tensor(hidf[q], gate[q].rearrange("p (k s) -> p k s", k=2),
                                  ps[:, 2 + q, :].rearrange("p (k s) -> p k s", k=2), ALU.mult).then_inc(s_hid, 1)

            def hidden_low(i, p, q):
                dve.wait_ge(s_hdh, i * 2 + q + 1)
                h = slice(2 * q, 2 * q + 2)
                dve.tensor_tensor(hids[p][1][:, h, :], hidf[q], hids[p][0][:, h, :].bitcast(f32), ALU.subtract)\
                    .then_inc(s_hdl, 1)

            def block_steps(i, p, last=False):
                hidden(i, p, 0)
                if not last:
                    w_low(0, i + 1, 1 - p)
                    slots_low(i + 1, 1 - p)
                hidden_low(i, p, 0)
                w_low(2, i, p)
                hidden(i, p, 1)
                hidden_low(i, p, 1)
                if not last:
                    w_low(1, i + 1, 1 - p)
            w_low(0, 0, 0)
            slots_low(0, 0)
            w_low(1, 0, 0)
            dve.wait_ge(s_texp, 1)
            end = last_pair(dve, lastp)
            with dve.Fori(0, CAPB // 2 - 1) as j:
                with dve.If(end > j):
                    block_steps(j * 2, 0)
                    block_steps(j * 2 + 1, 1)
            block_steps(end * 2, 0)
            block_steps(end * 2 + 1, 1, last=True)

        @block.tensor
        def _(pe):
            mm = pe.matmul
            pe.wait_ge(s_const, 1)
            pe.sem_inc(s_tp, 2)
            pe.sem_inc(s_kv, 2)
            def transpose_xn(t, p, bank, ready, made, copied=None):
                pe.wait_ge(made, t + 1)
                if copied is not None:
                    pe.wait_ge(*copied)
                for c in range(DC):
                    last = pe.transpose(ps[:, bank + p, c * P:(c + 1) * P], xn[p][:, c * P:(c + 1) * P], ident[:, :])
                last.then_inc(ready, 1)

            def project(t, p):
                pe.wait_ge(s_xt, t + 1)
                pe.wait_ge(s_kvd, t + 1)
                for c in range(DC):
                    last = mm(ps[:, 2 + p, :], xt[p][:, c, :], wkv[:, c, :], start=c == 0, stop=c == DC - 1)
                last.then_inc(s_kv, 1)
            pe.sem_inc(s_khp, 2)
            def sum_kv(t, p, start=False, stop=False):
                pe.wait_ge(s_kh, t + 1)
                pe.wait_ge(s_vh, t + 1)
                for c in range(DC):
                    mm(ps[:, 4 + c, 0:P + 1], vhs[p][:, c * P:(c + 1) * P], khs[p][:, c, 0:P + 1], start=start, stop=stop)
                mm(ps[:, 6, 0:D].rearrange("p (c d) -> p c d", c=DC), ones[:, :], khs[p][:, :, 0:P],
                   start=start, stop=stop).then_inc(s_khp, 1)
            transpose_xn(0, 0, 0, s_tp, s_xn)
            transpose_xn(1, 1, 0, s_tp, s_xn)
            pe.wait_ge(s_cen, 1)
            project(0, 0)
            def norm_pair(j, sums=True, start=False):
                transpose_xn(j * 2, 0, 0, s_tp, s_xn, (s_xt, j * 2 - 1))
                project(j * 2 - 1, 1)
                if sums:
                    sum_kv(j * 2 - KLAG, 0, start=start)
                transpose_xn(j * 2 + 1, 1, 0, s_tp, s_xn, (s_xt, j * 2))
                project(j * 2, 0)
                if sums:
                    sum_kv(j * 2 - KLAG + 1, 1)
            with pe.Fori(1, KLAG // 2) as j:
                norm_pair(j, sums=False)
            norm_pair(KLAG // 2, start=True)
            with pe.Fori(KLAG // 2 + 1, NT // 2) as j:
                norm_pair(j)
            transpose_xn(NT - 1, 0, 0, s_tp, s_xn, (s_xt, NT - 2))
            project(NT - 2, 1)
            project(NT - 1, 0)
            pe.wait_ge(s_cov, 1)
            mm(ps[:, 7, 0:1], ones[:, :], left_p[:, :], start=True, stop=True).then_inc(s_cov, 1)
            with pe.Fori((NT - 1 - KLAG) // 2, NT // 2) as j:
                sum_kv(j * 2, 0)
                sum_kv(j * 2 + 1, 1)
            sum_kv(NT - 1, 0, stop=True)
            pe.wait_ge(s_khp, NT + 2)
            pe.sem_inc(s_mx, 1)

            pe.sem_inc(s_w1, 4)
            pe.sem_inc(s_w2, 4)
            pe.sem_inc(s_sc, 2)
            pe.wait_ge(s_wlow, 1)

            def mix_a1():
                pe.wait_ge(s_mv, 1)
                for c in range(DC):
                    last = mm(ps[:, 4, c * D:(c + 1) * D], kvt[:, c, :], woT[:, c, :], start=True, stop=True)
                last.then_inc(s_mx, 1)
                pe.wait_ge(s_flag, 1)

            def mix_m():
                pe.wait_ge(s_mv, 2)
                for m in range(DC):
                    for c in range(DC):
                        last = mm(ps[:, 5, m * D:(m + 1) * D], wq[:, c, m * P:(m + 1) * P], A1[:, c, :],
                                  start=c == 0, stop=c == DC - 1)
                last.then_inc(s_mx, 1)

            def edges(n0, h0, w_n, mix=(nothing, nothing)):
                def up(i, p):
                    pe.wait_ge(s_rlo, n0 + i + 3)
                    for m in range(DC):
                        pe.wait_ge(s_silu, (n0 + i) * 2 + m + 1)
                        for k in range(2):
                            last = mm(ps[:, 6 * p + m, :], W1s[k][:, m * P:(m + 1) * P], rbs[p],
                                      start=k == 0, stop=k == 1)
                        last.then_inc(s_w1, 1)

                def gates(i, p):
                    pe.wait_ge(s_hlo, n0 + i + 2)
                    for s in range(ET):
                        if s % 2 == 0:
                            pe.wait_ge(s_zb, (n0 + i) * 2 + s // 2 + 1)
                        for c in range(DC):
                            for a, b in PARTS:
                                last = mm(ps[:, 2 + s // 2, (s % 2) * D:(s % 2 + 1) * D],
                                          h1s[p][a][:, c, s * P:(s + 1) * P], W2s[b][:, c, :],
                                          start=c == 0 and (a, b) == PARTS[0], stop=c == DC - 1 and (a, b) == PARTS[-1])
                        if s % 2:
                            last.then_inc(s_w2, 1)

                def scatter(i, p):
                    pe.wait_ge(s_msg, n0 + i + 3)
                    pe.wait_ge(s_agg, n0 + i + 1)
                    for c in range(DC):
                        for s in range(ET):
                            last = mm(ps[:, 4 + p, c * w_n:(c + 1) * w_n], msg[p][:, s, c * P:(c + 1) * P],
                                      oh[p][:, s, 0:w_n], start=s == 0, stop=s == ET - 1)
                    last.then_inc(s_sc, 1)
                up(0, 0)
                mix[0]()
                up(1, 1)
                gates(0, 0)
                mix[1]()
                up(2, 0)
                with pe.Fori(1, NG // 2 - 1) as j:
                    gates(j * 2 - 1, 1)
                    up(j * 2 + 1, 1)
                    scatter(j * 2 - 2, 0)
                    gates(j * 2, 0)
                    up(j * 2 + 2, 0)
                    scatter(j * 2 - 1, 1)
                gates(NG - 3, 1)
                up(NG - 1, 1)
                scatter(NG - 4, 0)
                gates(NG - 2, 0)
                scatter(NG - 3, 1)
                gates(NG - 1, 1)
                scatter(NG - 2, 0)
                scatter(NG - 1, 1)
            edges(0, 0, W, (mix_a1, mix_m))
            pe.wait_ge(s_flag, 1)
            left = pe.value_load(flag[0:1, 0:1], min_val=0, max_val=E)
            with pe.If(left > 0):
                with pe.Fori(0, NW) as w:
                    edges((w + 1) * NG, (w + 1) * (NG // 2), FW)

            pe.sem_inc(s_uo, 2)
            pe.sem_inc(s_ux, 2)
            pe.wait_ge(s_gnn, 1)
            pe.wait_ge(s_ulo, 1)
            def node_xn(v, q, n=2):
                pe.wait_ge(s_nlo, v + 1)
                pe.wait_ge(s_us, v + 1)
                for m in range(DC):
                    for k in range(2 * DC):
                        for a, b in PARTS:
                            last = mm(ps[:, q, m * 2 * P:(m + 1) * 2 * P], U1s[a][:, k, m * P:(m + 1) * P],
                                      (xns if k < DC else ags)[q][b][:, k % DC, :],
                                      start=k == 0 and (a, b) == PARTS[0], stop=k == 2 * DC - 1 and (a, b) == PARTS[-1])
                last.then_inc(s_u1, 1)
                pe.wait_ge(s_x1, v + 1)
                for h in range(n):
                    for k in range(DC):
                        for a, b in PARTS:
                            last = mm(ps[:, 2 + 2 * q + h, 0:D], xns[q][a][:, k, h * P:(h + 1) * P],
                                      UMs[b][:, DC + k, :], start=k == 0 and (a, b) == PARTS[0], stop=False)
                last.then_inc(s_ux, 1)

            def node_silu(v, q, n=2):
                pe.wait_ge(s_slo, v + 3)
                for h in range(n):
                    for k in range(DC):
                        for a, b in PARTS:
                            last = mm(ps[:, 2 + 2 * q + h, 0:D], sts[q][a][:, k, h * P:(h + 1) * P],
                                      UMs[b][:, k, :], start=False, stop=k == DC - 1 and (a, b) == PARTS[-1])
                last.then_inc(s_uo, 1)

            pe.sem_inc(s_tp2, 2)
            pe.sem_inc(s_lg, 2)
            def transpose_xn2(t, p):
                transpose_xn(t, p, 6, s_tp2, s_xn2, (s_lgc, t + 1))

            def gate_logits(t, p):
                pe.wait_ge(s_xt2, t + 1)
                for c in range(DC):
                    last = mm(ps[:, 6 + p, D:D + NX], xt2[p][:, c, :], gw[:, c, :], start=c == 0, stop=c == DC - 1)
                last.then_inc(s_lg, 1)

            def pair_step(v, q, t, n=2):
                if n:
                    node_xn(v + 1, 1 - q, n)
                if t is not None and not peeled(t, 0):
                    gate_logits(t - 2, 0)
                    gate_logits(t - 1, 1)
                node_silu(v, q, 2 if n else 1)
                if t is not None:
                    transpose_xn2(t, 0)
                    transpose_xn2(t + 1, 1)
            node_xn(0, 0)
            with pe.Fori(0, LAG // 4) as j:
                pair_step(j * 2, 0, None)
                pair_step(j * 2 + 1, 1, None)
            pair_step(LAG // 2, 0, 0)
            pair_step(LAG // 2 + 1, 1, 2)
            with pe.Fori(LAG // 4 + 1, NB // 2 - 1) as j:
                pair_step(j * 2, 0, j * 4 - LAG)
                pair_step(j * 2 + 1, 1, j * 4 - LAG + 2)
            pair_step(NB - 3, 0, 2 * NB - 6 - LAG)
            pair_step(NB - 2, 1, 2 * NB - 4 - LAG, 1)
            pair_step(NB - 1, 0, 2 * NB - 2 - LAG, 0)
            with pe.Fori((NT - LAG) // 2 + 1, NT // 2) as j:
                gate_logits(j * 2 - 2, 0)
                gate_logits(j * 2 - 1, 1)
                transpose_xn2(j * 2, 0)
                transpose_xn2(j * 2 + 1, 1)
            gate_logits(NT - 3, 0)
            gate_logits(NT - 2, 1)
            transpose_xn2(NT - 1, 0)
            gate_logits(NT - 1, 0)

            pe.wait_ge(s_m12, 1)
            mf = m12.rearrange("p t e -> p (t e)")
            mm(ps[:, 0, 0:TX], before[:, :], mf, start=True, stop=True)
            mm(ps[:, 1, 0:TX], ones[:, :], mf, start=True, stop=True).then_inc(s_cnt, 1)

            pe.sem_inc(s_tab, 2)
            def place(c, p, start=False, stop=False):
                pe.wait_ge(s_hot, c + 1)
                pe.wait_ge(s_hotw, c + 1)
                for k in range(TC):
                    last = mm(ps[:, 2, 0:2 * NS], tA[p][:, k, :], tB[p][:, k, :],
                              start=start and k == 0, stop=stop and k == TC - 1)
                last.then_inc(s_tab, 1)
            place(0, 0, start=True)
            place(1, 1)
            with pe.Fori(1, NT // TC - 1) as j:
                place(j * 2, 0)
                place(j * 2 + 1, 1)
            place(2 * NT // TC - 2, 0)
            place(2 * NT // TC - 1, 1, stop=True)

            pe.sem_inc(s_xsp, 2)
            pe.sem_inc(s_h, 8)
            pe.sem_inc(s_o, 2)
            pe.wait_ge(s_tabi, 1)
            def turn(i, j, p):
                pe.wait_ge(s_xs[p], (j + 1) * 32)
                pe.wait_ge(s_xlo, i + 1)
                for s in range(2):
                    for c in range(DC):
                        last = pe.transpose(ps[:, 7, c * SB + s * P:c * SB + (s + 1) * P],
                                            xs[p][:, s, c * P:(c + 1) * P], ident[:, :])
                last.then_inc(s_xsp, 1)

            def expert_up(i, p, q):
                pe.wait_ge(s_wlo[q], i + 1)
                pe.wait_ge(s_xlo, i + 2)
                pe.wait_ge(s_hid, i * 2 + q + 1)
                for m in range(2):
                    for k in range(2):
                        for c in range(DC):
                            for a, b in PARTS:
                                last = mm(ps[:, 2 * m + q, k * SB:(k + 1) * SB],
                                          ws[q][a][:, 2 * m + c, k * P:(k + 1) * P], xTs[p][b][:, c, :],
                                          start=c == 0 and (a, b) == PARTS[0], stop=c == DC - 1 and (a, b) == PARTS[-1])
                    last.then_inc(s_h, 1)

            def expert_down(i, p):
                pe.wait_ge(s_wlo[2], i + 1)
                pe.wait_ge(s_hdl, i * 2 + 2)
                pe.wait_ge(s_y, i + 1)
                for s in range(2):
                    for k in range(HC):
                        for a, b in PARTS:
                            last = mm(ps[:, 4 + p, s * D:(s + 1) * D], hids[p][a][:, k, s * P:(s + 1) * P],
                                      ws[2][b][:, k, :],
                                      start=k == 0 and (a, b) == PARTS[0], stop=k == HC - 1 and (a, b) == PARTS[-1])
                last.then_inc(s_o, 1)
            turn(0, 0, 0)
            expert_up(0, 0, 0)
            turn(1, 0, 1)
            expert_up(0, 0, 1)
            pe.wait_ge(s_texp, 1)
            end = last_pair(pe, lastp)
            with pe.Fori(0, CAPB // 2 - 1) as j:
                with pe.If(end > j):
                    expert_up(j * 2 + 1, 1, 0)
                    turn(j * 2 + 2, j + 1, 0)
                    expert_down(j * 2, 0)
                    expert_up(j * 2 + 1, 1, 1)
                    expert_up(j * 2 + 2, 0, 0)
                    turn(j * 2 + 3, j + 1, 1)
                    expert_down(j * 2 + 1, 1)
                    expert_up(j * 2 + 2, 0, 1)
            expert_up(end * 2 + 1, 1, 0)
            expert_down(end * 2, 0)
            expert_up(end * 2 + 1, 1, 1)
            expert_down(end * 2 + 1, 1)


def kernel(x, src, dst, edge_attr_64, L0_gnn_W1, L0_gnn_b1, L0_gnn_W2, L0_gnn_b2, L0_gnn_U1, L0_gnn_c1,
           L0_gnn_U2, L0_gnn_c2, L0_mix_wq, L0_mix_wk, L0_mix_wv, L0_mix_wo, L0_mix_bo, L0_mix_ln_k_g,
           L0_mix_ln_k_b, L0_mix_ln_v_g, L0_mix_ln_v_b, L0_ffn_gate_w, L0_ffn_gate_b, L0_ffn_w1,
           L0_ffn_w2, L0_ffn_w3):
    import numpy as np
    import concourse.bacc as bacc
    from concourse.bass_utils import run_bass_kernel_spmd

    def edge_columns(a, fill):
        a = np.pad(np.asarray(a), (0, EP - E), constant_values=fill)
        return np.ascontiguousarray(a.reshape(NG * ET, P).T)

    rbf = np.pad(np.asarray(edge_attr_64), ((0, EP - E), (0, 0)))
    arrays = {
        "x": x,
        "src": edge_columns(src, 0),
        "dst": edge_columns(dst, FAR),
        "first": np.asarray(dst)[::EG].reshape(1, NG),
        "rbf": rbf.reshape(NG, EG, RB).transpose(0, 2, 1),
        "W1": L0_gnn_W1, "b1": np.asarray(L0_gnn_b1).reshape(DC, P).T, "W2": L0_gnn_W2, "b2": L0_gnn_b2,
        "U1": L0_gnn_U1, "c1": np.asarray(L0_gnn_c1).reshape(DC, P).T, "U2": L0_gnn_U2, "c2": L0_gnn_c2,
        "wq": L0_mix_wq,
        "wkvT": np.concatenate([np.asarray(L0_mix_wk).T, np.asarray(L0_mix_wv).T], axis=1),
        "woT": np.asarray(L0_mix_wo).T, "bo": L0_mix_bo,
        "kg": L0_mix_ln_k_g, "kb": L0_mix_ln_k_b, "vg": L0_mix_ln_v_g, "vb": L0_mix_ln_v_b,
        "gw": L0_ffn_gate_w, "gb": L0_ffn_gate_b, "w1": L0_ffn_w1, "w2": L0_ffn_w2, "w3": L0_ffn_w3,
    }
    arrays = {"in_" + k: np.ascontiguousarray(v) for k, v in arrays.items()}
    nc = bacc.Bacc("TRN2", target_bir_lowering=False, num_devices=1)
    args = [nc.dram_tensor(k, v.shape, mybir.dt.from_np(v.dtype), kind="ExternalInput").ap()
            for k, v in arrays.items()]
    out = nc.dram_tensor("out", (N, D), f32, kind="ExternalOutput").ap()
    gps_layer(nc, *args, out)
    r = run_bass_kernel_spmd(nc, [arrays], core_ids=[0])
    return r.results[0]["out"]
```
